# Optimizing a Trainium2 kernel written in Bass

```python
import numpy as np
import jax
import jax.numpy as jnp

def _softmax(x, axis=-1):
    return jax.nn.softmax(x, axis=axis)

def _gelu(x):
    return jax.nn.gelu(x, approximate=True)

def _silu(x):
    return jax.nn.silu(x)

def _sigmoid(x):
    return jax.nn.sigmoid(x)

def _layernorm(x, axis=-1, eps=1e-05):
    m = jnp.mean(x, axis=axis, keepdims=True)
    v = jnp.var(x, axis=axis, keepdims=True)
    return (x - m) / jnp.sqrt(v + eps)

def _scatter_add(tgt, idx, src, axis=0):
    return tgt.at[idx].add(src)

def _segment_sum(src, seg, n):
    return jax.ops.segment_sum(src, seg, n)
kernel_name = 'mk_gnn_preln_d2_gnn_r8_5acd78'

def setup_inputs(seed: int=0):
    np.random.seed(seed)
    _w = jnp.asarray

    def _rec_inputs():
        import jax
        import jax.numpy as jnp
        _gk = jax.random.key(seed)
        x = -2.525e-05 + 0.125 * jax.random.normal(jax.random.fold_in(_gk, 1), (12500, 64), jnp.float32)
        _s = jax.random.randint(jax.random.fold_in(_gk, 2), (100000,), 0, 12500, jnp.int32)
        _d = jax.random.randint(jax.random.fold_in(_gk, 3), (100000,), 0, 12500, jnp.int32)
        _loop = jnp.arange(12500, dtype=jnp.int32)
        src = jnp.concatenate([_s, _d, _loop])
        dst = jnp.concatenate([_d, _s, _loop])
        _o = jnp.argsort(dst, stable=True)
        src = src[_o]
        dst = dst[_o]
        edge_attr_16 = 0.000254156 + 0.999948 * jax.random.normal(jax.random.fold_in(_gk, 12), (212500, 16), jnp.float32)
        edge_type_8 = jax.random.randint(jax.random.fold_in(_gk, 14), (212500,), 0, 8, jnp.int32)
        return (x, src, dst, edge_attr_16, edge_type_8)
    x, src, dst, edge_attr_16, edge_type_8 = _rec_inputs()

    def _L0_gnn_setup():
        import jax, jax.numpy as jnp
        import numpy as np
        N_NODES = 12500
        N_EDGES = 160000
        HID = 64
        MSG = 64
        N_ETYPE = 8

        def _ggnn_forward(h, edge_matrix, w_ih, w_hh, b_ih, b_hh, edge_src, edge_dst, edge_type):
            N, H = h.shape
            T = edge_matrix.shape[0]
            M = edge_matrix.shape[1] // H
            A = edge_matrix.reshape(T, M, H)
            Ht = jnp.einsum('tmh,nh->tnm', A, h)
            msg = Ht[edge_type, edge_src]
            m_agg = jax.ops.segment_sum(msg, edge_dst, num_segments=N)
            gi = m_agg @ w_ih.T + b_ih
            gh = h @ w_hh.T + b_hh
            i_r, i_z, i_n = (gi[:, :H], gi[:, H:2 * H], gi[:, 2 * H:])
            h_r, h_z, h_n = (gh[:, :H], gh[:, H:2 * H], gh[:, 2 * H:])
            r = jax.nn.sigmoid(i_r + h_r)
            z = jax.nn.sigmoid(i_z + h_z)
            n = jnp.tanh(i_n + r * h_n)
            return (1.0 - z) * n + z * h
        key = jax.random.key(seed)
        ks = jax.random.split(key, 9)
        s = 1.0 / np.sqrt(HID)
        return {'h': jax.random.normal(ks[0], (N_NODES, HID), jnp.float32) * s, 'edge_matrix': jax.random.normal(ks[1], (N_ETYPE, MSG * HID), jnp.float32) * s, 'w_ih': jax.random.normal(ks[2], (3 * HID, MSG), jnp.float32) * s, 'w_hh': jax.random.normal(ks[3], (3 * HID, HID), jnp.float32) * s, 'b_ih': jax.random.normal(ks[4], (3 * HID,), jnp.float32) * s, 'b_hh': jax.random.normal(ks[5], (3 * HID,), jnp.float32) * s, 'edge_src': jax.random.randint(ks[6], (N_EDGES,), 0, N_NODES, jnp.int32), 'edge_dst': jax.random.randint(ks[7], (N_EDGES,), 0, N_NODES, jnp.int32), 'edge_type': jax.random.randint(ks[8], (N_ETYPE if False else N_EDGES,), 0, N_ETYPE, jnp.int32)}
    _L0_gnn_all = _L0_gnn_setup()
    _L0_gnn_in = {k: v for k, v in _L0_gnn_all.items() if k in ('edge_matrix', 'w_ih', 'w_hh', 'b_ih', 'b_hh')}
    del _L0_gnn_all

    def _L1_gnn_setup():
        import jax, jax.numpy as jnp
        import numpy as np
        N, E, D, ED = (6250, 100000, 64, 16)
        H1 = 2 * D + ED

        def _forward(x, edge_weights, W_att1, b_att1, W_att2, b_att2, W_lin, b_lin, W_ih, b_ih, W_hh, b_hh, edge_idx):
            num_nodes = x.shape[0]
            src = edge_idx[0]
            dst = edge_idx[1]
            lin_x = x @ W_lin.T + b_lin
            feat = jnp.concatenate([x[src], edge_weights, x[dst]], axis=1)
            h = jax.nn.relu(feat @ W_att1.T + b_att1)
            scores = (h @ W_att2.T + b_att2)[:, 0]
            m = jax.ops.segment_max(scores, src, num_segments=num_nodes)
            e = jnp.exp(scores - m[src])
            denom = jax.ops.segment_sum(e, src, num_segments=num_nodes)
            alpha = e / denom[src]
            msg = jax.ops.segment_sum(alpha[:, None] * lin_x[dst], src, num_segments=num_nodes)
            gi = x @ W_ih.T + b_ih
            gh = msg @ W_hh.T + b_hh
            i_r, i_z, i_n = jnp.split(gi, 3, axis=1)
            h_r, h_z, h_n = jnp.split(gh, 3, axis=1)
            r = jax.nn.sigmoid(i_r + h_r)
            z = jax.nn.sigmoid(i_z + h_z)
            n = jnp.tanh(i_n + r * h_n)
            new_h = (1.0 - z) * n + z * msg
            deg = jax.ops.segment_sum(jnp.ones_like(scores), src, num_segments=num_nodes)
            return jnp.where(deg[:, None] > 0, new_h, x)
        key = jax.random.key(seed)
        ks = jax.random.split(key, 16)
        s = 0.05
        inp = {'x': jax.random.normal(ks[0], (N, D), jnp.float32), 'edge_idx': jax.random.randint(ks[1], (2, E), 0, N, jnp.int64), 'edge_weights': jax.random.normal(ks[2], (E, ED), jnp.float32), 'W_att1': jax.random.normal(ks[3], (H1, H1), jnp.float32) * s, 'b_att1': jnp.zeros((H1,), jnp.float32), 'W_att2': jax.random.normal(ks[4], (1, H1), jnp.float32) * s, 'b_att2': jnp.zeros((1,), jnp.float32), 'W_lin': jax.random.normal(ks[5], (D, D), jnp.float32) * s, 'b_lin': jnp.zeros((D,), jnp.float32), 'W_ih': jax.random.normal(ks[6], (3 * D, D), jnp.float32) * s, 'b_ih': jnp.zeros((3 * D,), jnp.float32), 'W_hh': jax.random.normal(ks[7], (3 * D, D), jnp.float32) * s, 'b_hh': jnp.zeros((3 * D,), jnp.float32)}
        return inp
    _L1_gnn_all = _L1_gnn_setup()
    _L1_gnn_in = {k: v for k, v in _L1_gnn_all.items() if k in ('W_att1', 'b_att1', 'W_att2', 'b_att2', 'W_lin', 'b_lin', 'W_ih', 'b_ih', 'W_hh', 'b_hh')}
    del _L1_gnn_all
    return {'x': x, 'src': src, 'dst': dst, 'edge_attr_16': edge_attr_16, 'edge_type_8': edge_type_8, 'L0_gnn_edge_matrix': _L0_gnn_in['edge_matrix'], 'L0_gnn_w_ih': _L0_gnn_in['w_ih'], 'L0_gnn_w_hh': _L0_gnn_in['w_hh'], 'L0_gnn_b_ih': _L0_gnn_in['b_ih'], 'L0_gnn_b_hh': _L0_gnn_in['b_hh'], 'L1_gnn_W_att1': _L1_gnn_in['W_att1'], 'L1_gnn_b_att1': _L1_gnn_in['b_att1'], 'L1_gnn_W_att2': _L1_gnn_in['W_att2'], 'L1_gnn_b_att2': _L1_gnn_in['b_att2'], 'L1_gnn_W_lin': _L1_gnn_in['W_lin'], 'L1_gnn_b_lin': _L1_gnn_in['b_lin'], 'L1_gnn_W_ih': _L1_gnn_in['W_ih'], 'L1_gnn_b_ih': _L1_gnn_in['b_ih'], 'L1_gnn_W_hh': _L1_gnn_in['W_hh'], 'L1_gnn_b_hh': _L1_gnn_in['b_hh']}

def reference(x, src, dst, edge_attr_16, edge_type_8, L0_gnn_edge_matrix, L0_gnn_w_ih, L0_gnn_w_hh, L0_gnn_b_ih, L0_gnn_b_hh, L1_gnn_W_att1, L1_gnn_b_att1, L1_gnn_W_att2, L1_gnn_b_att2, L1_gnn_W_lin, L1_gnn_b_lin, L1_gnn_W_ih, L1_gnn_b_ih, L1_gnn_W_hh, L1_gnn_b_hh):
    import jax
    import jax.numpy as jnp

    def _L0_gnn_ref(h, edge_matrix, w_ih, w_hh, b_ih, b_hh, edge_src, edge_dst, edge_type):
        import jax, jax.numpy as jnp
        import numpy as np
        N_NODES = 12500
        N_EDGES = 160000
        HID = 64
        MSG = 64
        N_ETYPE = 8

        def _ggnn_forward(h, edge_matrix, w_ih, w_hh, b_ih, b_hh, edge_src, edge_dst, edge_type):
            N, H = h.shape
            T = edge_matrix.shape[0]
            M = edge_matrix.shape[1] // H
            A = edge_matrix.reshape(T, M, H)
            Ht = jnp.einsum('tmh,nh->tnm', A, h)
            msg = Ht[edge_type, edge_src]
            m_agg = jax.ops.segment_sum(msg, edge_dst, num_segments=N)
            gi = m_agg @ w_ih.T + b_ih
            gh = h @ w_hh.T + b_hh
            i_r, i_z, i_n = (gi[:, :H], gi[:, H:2 * H], gi[:, 2 * H:])
            h_r, h_z, h_n = (gh[:, :H], gh[:, H:2 * H], gh[:, 2 * H:])
            r = jax.nn.sigmoid(i_r + h_r)
            z = jax.nn.sigmoid(i_z + h_z)
            n = jnp.tanh(i_n + r * h_n)
            return (1.0 - z) * n + z * h
        return _ggnn_forward(h, edge_matrix, w_ih, w_hh, b_ih, b_hh, edge_src, edge_dst, edge_type)

    def _L1_gnn_ref(x, edge_idx, edge_weights, W_att1, b_att1, W_att2, b_att2, W_lin, b_lin, W_ih, b_ih, W_hh, b_hh):
        import jax, jax.numpy as jnp
        import numpy as np
        N, E, D, ED = (6250, 100000, 64, 16)
        H1 = 2 * D + ED

        def _forward(x, edge_weights, W_att1, b_att1, W_att2, b_att2, W_lin, b_lin, W_ih, b_ih, W_hh, b_hh, edge_idx):
            num_nodes = x.shape[0]
            src = edge_idx[0]
            dst = edge_idx[1]
            lin_x = x @ W_lin.T + b_lin
            feat = jnp.concatenate([x[src], edge_weights, x[dst]], axis=1)
            h = jax.nn.relu(feat @ W_att1.T + b_att1)
            scores = (h @ W_att2.T + b_att2)[:, 0]
            m = jax.ops.segment_max(scores, src, num_segments=num_nodes)
            e = jnp.exp(scores - m[src])
            denom = jax.ops.segment_sum(e, src, num_segments=num_nodes)
            alpha = e / denom[src]
            msg = jax.ops.segment_sum(alpha[:, None] * lin_x[dst], src, num_segments=num_nodes)
            gi = x @ W_ih.T + b_ih
            gh = msg @ W_hh.T + b_hh
            i_r, i_z, i_n = jnp.split(gi, 3, axis=1)
            h_r, h_z, h_n = jnp.split(gh, 3, axis=1)
            r = jax.nn.sigmoid(i_r + h_r)
            z = jax.nn.sigmoid(i_z + h_z)
            n = jnp.tanh(i_n + r * h_n)
            new_h = (1.0 - z) * n + z * msg
            deg = jax.ops.segment_sum(jnp.ones_like(scores), src, num_segments=num_nodes)
            return jnp.where(deg[:, None] > 0, new_h, x)
        return _forward(x, edge_weights, W_att1, b_att1, W_att2, b_att2, W_lin, b_lin, W_ih, b_ih, W_hh, b_hh, edge_idx)
    edge_index = jnp.stack([src, dst])
    h = jnp.maximum(_layernorm(x, axis=-1), 0.0)
    x = x + _L0_gnn_ref(h, L0_gnn_edge_matrix, L0_gnn_w_ih, L0_gnn_w_hh, L0_gnn_b_ih, L0_gnn_b_hh, src, dst, edge_type_8)
    h = jnp.maximum(_layernorm(x, axis=-1), 0.0)
    x = x + _L1_gnn_ref(h, edge_index, edge_attr_16, L1_gnn_W_att1, L1_gnn_b_att1, L1_gnn_W_att2, L1_gnn_b_att2, L1_gnn_W_lin, L1_gnn_b_lin, L1_gnn_W_ih, L1_gnn_b_ih, L1_gnn_W_hh, L1_gnn_b_hh)
    return x

_drawn_inputs = setup_inputs


def setup_inputs(seed=0):
    import zlib

    import numpy as np

    out = dict(_drawn_inputs(seed))
    spreads = {'L1_gnn_b_att1': (0.0, 0.8),
     'L1_gnn_b_lin': (0.0, 0.1),
     'L1_gnn_b_ih': (0.0, 0.1),
     'L1_gnn_b_hh': (0.0, 0.1)}
    factors = {'edge_attr_16': 8.0, 'L1_gnn_W_att1': 8.0, 'L1_gnn_W_att2': 8.0}
    for name, (base, spread) in spreads.items():
        noise = np.random.default_rng([zlib.crc32(name.encode()), seed]).standard_normal(out[name].shape)
        drawn = base * np.exp(spread * noise) if base else spread * noise
        out[name] = jnp.asarray(drawn.astype(out[name].dtype))
    for name, factor in factors.items():
        out[name] = (out[name] * factor).astype(out[name].dtype)
    return out
```

```python
import concourse.bass as bass
from concourse import mybir
from contextlib import ExitStack

P = 128
N_NODES = 12500
N_EDGES = 212500
HID = 64
ATTR = 16
TYPES = 8
GATES = 3 * HID
H1 = 2 * HID + ATTR
BANK = 512
N_WIN = -(-N_NODES // P)
NW = 4 * -(-N_WIN // 4)
N_KEYS = NW
LAST_NODES = N_NODES - (N_WIN - 1) * P
COLS = 1664
SLOTS = P * COLS
TILES = SLOTS // P
LAST_COLS = N_EDGES - (P - 1) * COLS
N_PAD = SLOTS - N_EDGES
PAD_KEY = N_WIN * P
GV = 4
NS = 4
BODY = GV * NS
VISITS = BODY * -(-(-(-N_EDGES // P) + N_WIN - 1) // BODY)
LOOPS = VISITS // BODY
VCHUNK = VISITS // 4
HW = N_WIN - 1
ROW = 84
ROW_ONE = ATTR + HID
ROW_SRC = ROW_ONE + 1
REC = 4
BIG = float(1 << 20)
MASKED = 1.0e30
EPS = 1.0e-5
SORT_COLS = 16
SORT_ROW = ATTR + 4
COUNT_LOOPS = N_KEYS // 2
PLACE_LOOPS = N_KEYS // 2
G_LOOPS = NW // 4


class Chain:

    def __init__(self, eng, sem):
        self.eng, self.sem = eng, sem
        self.base = self.k = self.i = self.per = 0

    def body(self, i, per):
        if not self.per:
            self.base += self.k
        self.i, self.per, self.k = i, per, 0

    def end_body(self):
        assert self.k == self.per, (self.k, self.per)
        self.k = 0

    def end_loop(self, n):
        self.base += n * self.per
        self.i = self.per = self.k = 0

    def do(self, ins):
        self.k += 1
        ins.then_inc(self.sem, 1)
        return self.base + self.i * self.per + self.k

    def need(self, mark):
        self.eng.wait_ge(self.sem, mark)

    def link(self, ins):
        self.need(self.do(ins))


def first(i):
    return isinstance(i, int) and i == 0


def build(nc, x, src, dst, attr, etype, edge_matrix, w_ih0, w_hh0, b_ih0, b_hh0,
          w_att1, b_att1, w_att2, b_att2, w_lin, b_lin, w_ih1, b_ih1, w_hh1, b_hh1, out):
    f32, i32, bf16, u16 = mybir.dt.float32, mybir.dt.int32, mybir.dt.bfloat16, mybir.dt.uint16
    ALU = mybir.AluOpType
    ACT = mybir.ActivationFunctionType
    AX = mybir.AxisListType
    ENG = mybir.EngineType
    ds = bass.ds
    ctx = ExitStack()

    def sb(name, shape, dt=f32):
        return ctx.enter_context(nc.sbuf_tensor(name, shape, dt))

    def sem(name):
        return ctx.enter_context(nc.semaphore(name))

    def sems(name, n):
        return [sem(f"{name}{j}") for j in range(n)]

    def dram(name, shape):
        return nc.dram_tensor(name, shape, f32, kind="Internal").ap()

    def regs(engine, tab, v, top):
        _, r = nc.values_load_multi_w_load_instructions(
            tab[0:1, ds(v, GV)], engines=(engine,), min_val=0, max_val=top,
            skip_runtime_bounds_check_because="the table's entries are bounded when it is made")
        return r

    def per_group(t, a):
        return t.unsqueeze(2).to_broadcast([P, GV, a])

    with ctx:
        table = dram("msg_table", [NW * P * TYPES, HID])
        recA = dram("rec0_by_dst", [SLOTS, 2])
        recB = dram("rec1_by_dst", [SLOTS, REC])
        attr_d = dram("attr_by_dst", [SLOTS, ATTR])
        rows_d = dram("rows_by_src", [SLOTS, ROW])

        sorted_d = dram("edges_by_dst", [SLOTS, SORT_ROW])

        xs = sb("xs", [P, NW, HID])
        h = sb("h", [P, NW, HID])
        acc = sb("acc", [P, NW, HID + 1])
        big = sb("big", [P, NW * H1])
        wbase = sb("wbase", [P, VISITS])
        wwin = sb("wwin", [1, VISITS], i32)
        wtile = sb("wtile", [1, VISITS], i32)
        RING = 9700
        ring = sb("ring", [P, RING])
        ident = sb("ident", [P, P])
        iota = sb("iota", [P, P])
        ones = sb("ones", [P, P])
        tri = sb("tri", [P, P])
        cnt = sb("cnt", [P, N_KEYS])
        place0 = sb("place0", [P, N_KEYS])
        small = sb("small", [P, 512])
        zeros = sb("zeros", [P, 3 * ATTR])
        AT = sb("AT", [HID, TYPES * HID])
        wih0T = sb("wih0T", [HID + 1, GATES])
        whh0T = sb("whh0T", [HID + 1, GATES])
        wih1T = sb("wih1T", [HID + 1, GATES])
        whh1T = sb("whh1T", [HID + 1, GATES])
        wlinT = sb("wlinT", [HID + 1, HID])
        waT = sb("waT", [HID + 1, H1])
        wv = sb("wv", [ATTR + HID, H1])
        w2bc = sb("w2bc", [P, H1])
        b2bc = sb("b2bc", [P, 1])
        eps_t = sb("eps_t", [P, 1])
        cc = [sb(f"cc{k}", [P, 1]) for k in range(2)]
        nt = sb("nt", [P, 1])
        off = sb("off", [P, 1])
        dbc = sb("dbc", [P, P])
        unsorted = sb("unsorted", [1, 1], i32)
        before = sb("before", [P, 1], i32)
        out_of_order = sb("out_of_order", [P, 1])
        mrun = sb("mrun", [P, NW])

        at = [0]

        def part(t, n, limit):
            at[0] += n
            assert at[0] <= limit, at[0]
            return t[:, at[0] - n:at[0]]

        dst_i = part(big, COLS, NW * H1).bitcast(i32)
        src_i = part(big, COLS, NW * H1).bitcast(i32)
        kB_flat = part(big, REC * COLS, NW * H1)
        kB = kB_flat.rearrange("p (c k) -> p c k", k=REC)
        kA_flat = kB_flat[:, 0:2 * COLS]
        kA = kA_flat.rearrange("p (c k) -> p c k", k=2)
        typ_i = kB_flat[:, 2 * COLS:3 * COLS].bitcast(i32)
        win = part(big, COLS // 2, NW * H1).bitcast(bf16)
        mask = part(big, COLS // 2, NW * H1).bitcast(bf16)
        scan = part(big, COLS, NW * H1)
        p_tab = big[:, :].rearrange("p (w j) -> p w j", j=H1)

        iota_v = ring[:, 0:VISITS]
        vmask = ring[:, VISITS:2 * VISITS]
        t0 = 2 * VISITS
        t_hT = ring[0:HID, t0:t0 + 2 * P].rearrange("p (s n) -> p s n", s=2)
        t_out = ring[:, t0 + 2 * P:t0 + 2 * P + 2 * BANK].rearrange("p (s n) -> p s n", s=2)

        d_place = kB_flat[:, 3 * COLS:4 * COLS]
        d_rows = ring[:, 6000:6000 + SORT_COLS * SORT_ROW].rearrange("p (c k) -> p c k", k=SORT_ROW)
        d_pos = ring[:, 6400:6400 + SORT_COLS].bitcast(i32)

        def groups(t, n, k):
            return part(t, n * GV * k, RING).rearrange("p (s u k) -> p s u k", s=n, u=GV)

        def marks(n=NS):
            return part(ring, n * GV, RING).rearrange("p (s u) -> p s u", s=n)

        t_h1 = ring[:, t0 + 2 * P + 2 * BANK:t0 + 3 * P + 2 * BANK].rearrange("p (s n) -> p s n", s=2)

        at[0] = 0
        A_D = groups(ring, NS, P)
        A_g = groups(ring, NS, HID)
        A_rec = groups(ring, NS, 2)
        A_kl = marks()

        at[0] = 0
        B_D = groups(ring, NS, P)
        B_DT = groups(ring, NS, P)
        B_row = groups(ring, NS, ROW)
        B_rec = groups(ring, NS, REC)
        B_kl, B_ge, B_in, B_sh = marks(), marks(), marks(), marks()
        B_pos = marks().bitcast(i32)
        B_h = part(ring, HID, RING)
        B_hT = part(ring, P, RING)[0:HID + 1, :]
        padrows = part(ring, 3 * ROW, RING).rearrange("p (a k) -> p a k", k=ROW)

        at[0] = 0
        C_S = groups(ring, NS, P)
        C_MK = groups(ring, NS, P)
        C_ST = groups(ring, NS, P)
        C_V = groups(ring, NS, ROW)
        C_VT = part(ring, GV * P, RING)[0:ATTR + HID, :].rearrange("p (u n) -> p u n", u=GV)
        C_W = groups(ring, 2, HID + 1)
        C_z = part(ring, H1, RING)
        C_kl, C_s, C_tm, C_mo, C_mn, C_df, C_cr, C_d, C_p = (marks() for _ in range(9))

        at[0] = 0
        G_T = part(ring, 8 * P, RING)[0:HID + 1, :].rearrange("p (s u n) -> p s u n", s=2, u=4)
        G_mT = part(ring, 4 * P, RING)[0:HID + 1, :].rearrange("p (s u n) -> p s u n", s=2, u=2)

        def pairs(n):
            return part(ring, 4 * n, RING).rearrange("p (s u n) -> p s u n", s=2, u=2)

        G_t = pairs(2 * HID)
        G_n, G_u, G_v, G_d, G_e, G_m = (pairs(HID) for _ in range(6))
        G_c = pairs(HID + 1)
        G_in = part(ring, 8 * HID, RING).rearrange("p (s u n) -> p s u n", s=2, u=4)
        has = part(ring, NW, RING)
        rden = part(ring, NW, RING)
        tmp_w = part(ring, NW, RING)

        bank = [ctx.enter_context(nc.psum_tensor(f"bank{j}", [P, BANK], f32)) for j in range(8)]

        def four(b, k):
            return b[:, 0:4 * k].rearrange("p (u k) -> p u k", u=4)

        def two(b, k):
            return b[:, 0:2 * k].rearrange("p (u k) -> p u k", u=2)

        block = ctx.enter_context(nc.Block())

        own = {e: sem(f"{e}_step") for e in ("dve", "pool")}
        turns = {e: sem(f"{e}_turns") for e in ("dve", "pool", "pe")}
        s_const, s_padded, s_ids, s_x, s_w, s_attr = (sem(f"s_{k}") for k in ("const", "padded", "ids", "x", "w", "attr"))
        s_wT, s_wcopied = sem("s_wT"), sem("s_wcopied")
        s_var, s_std, s_h = sem("s_var"), sem("s_std"), sem("s_h")
        s_kA, s_recA, s_kB, s_recB = sem("s_kA"), sem("s_recA"), sem("s_kB"), sem("s_recB")
        s_iotav = sem("s_iotav")
        s_cnt, s_tot, s_cc, s_start, s_nt, s_vstart, s_off, s_shift, s_vmask, s_vsum, s_vtab = (
            sem(f"s_{k}") for k in ("cnt", "tot", "cc", "start", "nt", "vstart", "off", "shift", "vmask", "vsum", "vtab"))
        s_before, s_flagp, s_flag = sem("s_before"), sem("s_flagp"), sem("s_flag")
        d_step, d_attr, d_ready, d_sc, d_free, d_sent, d_back, d_ids = (
            sem(f"d_{k}") for k in ("step", "attr", "ready", "sc", "free", "sent", "back", "ids"))
        t_st, a_rec, a_g = sems("t_st", 2), sems("a_rec", NS), sems("a_g", NS)
        b_in, b_sc, c_in = sems("b_in", NS), sems("b_sc", NS), sems("c_in", NS)
        t_h, t_T, t_Tc, t_mm, t_cp = (sem(f"t_{k}") for k in ("h", "T", "Tc", "mm", "cp"))
        g_in, n_in, b_hc = sem("g0_in"), sem("g1_in"), sem("b_hc")
        a_D, a_mm = sem("a_D"), sem("a_mm")
        a_acc, a_zero, a_done = sem("a_acc"), sem("a_zero"), sem("a_done")
        b_kl, b_D, b_pos, b_DT, b_DTc, b_hr, b_row = (sem(f"b_{k}") for k in ("kl", "D", "pos", "DT", "DTc", "hr", "row"))
        b_pad, b_padout, b_sent, b_pT, b_pTc, b_pmm, b_pcp = (
            sem(f"b_{k}") for k in ("pad", "padout", "sent", "pT", "pTc", "pmm", "pcp"))
        c_kl, c_S, c_nb, c_St, c_STc, c_Vt, c_VTc, c_pre, c_sc, c_MK, c_MKt, c_tm, c_mn, c_df, c_cr, c_mg, c_d, c_p, c_W, c_ag, c_acc = (
            sem(f"c_{k}") for k in ("kl", "S", "nb", "St", "STc", "Vt", "VTc", "pre", "sc", "MK", "MKt", "tm", "mn", "df", "cr", "mg", "d", "p", "W", "ag", "acc"))
        c_init, c_done = sem("c_init"), sem("c_done")
        g_T, g_Tc, g_mm, g_t, g_v, g_n, g_x = (sem(f"g0_{k}") for k in ("T", "Tc", "mm", "t", "v", "n", "x"))
        n_c, n_T, n_Tc, n_ms, n_msc, n_mm, n_t, n_v, n_n, n_x = (
            sem(f"g1_{k}") for k in ("c", "T", "Tc", "ms", "msc", "mm", "t", "v", "n", "x"))
        g_ones, n_ones, s_final = sem("g_ones"), sem("n_ones"), sem("s_final")
        N_CONST = 7

        def turn(eng, name):
            eng.sem_inc(turns[name], 1)

        jobs = []
        em = edge_matrix.rearrange("t (m k) -> (t m) k", k=HID)
        for w, wT in ((em, AT), (w_ih0, wih0T), (w_hh0, whh0T), (w_lin, wlinT), (w_ih1, wih1T),
                      (w_hh1, whh1T), (w_att1[:, 0:HID], waT), (w_att1[:, HID:H1], wv)):
            n, c = w.shape
            for r in range(0, n, P):
                m = min(P, n - r)
                jobs.append((w[r:r + m, :], m, c, wT[0:c, r:r + m]))
        biases = [(b_ih0, wih0T), (b_hh0, whh0T), (b_lin, wlinT), (b_ih1, wih1T), (b_hh1, whh1T), (b_att1, waT)]
        WR = ATTR + HID
        raw = [ring[0:m, WR * j:WR * j + c] for j, (_, m, c, _) in enumerate(jobs)]
        N_WDMA = len(jobs) + len(biases) + 2

        recA_t = recA.rearrange("(t p) k -> t p k", p=P)
        recB_t = recB.rearrange("(t p) k -> t p k", p=P)
        attr_t = attr_d.rearrange("(t p) k -> t p k", p=P)
        rows_t = rows_d.rearrange("(t p) k -> t p k", p=P)

        def tile_of(t, r):
            return t[ds(r, 1), :, :].rearrange("a p k -> (a p) k")

        def run_ticks(eng, tick, ch=None, steps=None):
            def body(i, slots, alive):
                for s in slots:
                    tick(i, s, {k: ((s - k) % NS, i if s >= k else i - 1) for k in range(4) if alive(s, k)})

            def straight(i, slots, alive):
                body(i, slots, alive)
                if ch:
                    ch.base, ch.k = ch.base + ch.k, 0
            straight(0, range(NS), lambda s, k: s >= k)
            straight(1, range(NS), lambda s, k: True)
            per = NS * sum(steps.values()) if ch else 0
            if ch:
                ch.base -= 2 * per
            with eng.Fori(2, LOOPS) as i:
                if ch:
                    ch.body(i, per)
                body(i, range(NS), lambda s, k: True)
                if ch:
                    ch.end_body()
            if ch:
                ch.end_loop(LOOPS)
            straight(LOOPS, range(3), lambda s, k: s < k)

        def loop(eng, n, body, start=0):
            if start == 0:
                body(0)
                start = 1
            with eng.Fori(start, n) as i:
                body(i)

        def after(eng, s, t, j, back=0, slots=NS, incs=1):
            v = j * slots + (t + 1 - back)
            if not (isinstance(v, int) and v < 1):
                eng.wait_ge(s, v * incs)

        def after2(eng, s, t, j, back=0, incs=1):
            after(eng, s, t, j, back, 2, incs)

        @block.sync
        def _(sp):
            sp.wait_ge(s_padded, 5)
            for v, t in ((dst, dst_i), (src, src_i), (etype, typ_i)):
                sp.dma_start(t[0:P - 1, :], v[0:(P - 1) * COLS].rearrange("(p c) -> p c", c=COLS)).then_inc(s_ids, 16)
                sp.dma_start(t[P - 1:P, 0:LAST_COLS],
                             v[(P - 1) * COLS:N_EDGES].rearrange("(a c) -> a c", a=1)).then_inc(s_ids, 16)
            ends = dst[0:(P - 1) * COLS].rearrange("(p c) -> p c", c=COLS)[:, COLS - 1:COLS]
            sp.dma_start(before[1:P, :], ends, allow_slow_non_contiguous=True).then_inc(s_before, 16)
            whole = (N_WIN - 1) * P
            sp.dma_start(xs[:, 0:N_WIN - 1, :], x[0:whole, :].rearrange("(w p) f -> p w f", p=P)).then_inc(s_x, 16)
            sp.dma_start(xs[0:LAST_NODES, N_WIN - 1, :], x[whole:N_NODES, :]).then_inc(s_x, 16)
            for (w, _, _, _), r in zip(jobs, raw):
                sp.dma_start(r, w).then_inc(s_w, 16)
            for b, t in biases:
                sp.dma_start(t[HID:HID + 1, :], b.rearrange("(a n) -> a n", a=1)).then_inc(s_w, 16)
            sp.dma_start(w2bc[:, :], w_att2[0:1, :].to_broadcast([P, H1])).then_inc(s_w, 16)
            sp.dma_start(b2bc[:, :], b_att2.rearrange("(a n) -> a n", a=1).to_broadcast([P, 1])).then_inc(s_w, 16)
            sp.dma_start(attr_d[0:N_EDGES, :].rearrange("(a b) k -> a (b k)", a=500),
                         attr.rearrange("(a b) k -> a (b k)", a=500)).then_inc(s_attr, 16)
            sp.wait_ge(s_const, N_CONST)
            sp.dma_start(attr_d[N_EDGES:N_EDGES + 3 * P, :].rearrange("(p a) k -> p (a k)", a=3), zeros[:, :]).then_inc(s_attr, 16)
            sp.dma_start(attr_d[N_EDGES + 3 * P:SLOTS, :], zeros[0:N_PAD - 3 * P, 0:ATTR]).then_inc(s_attr, 16)
            table_w = table.rearrange("(w p t) m -> w p (t m)", p=P, t=TYPES)

            def store_table(i):
                for s in range(2):
                    after2(sp, t_cp, s, i)
                    sp.dma_start(tile_of(table_w, i * 2 + s), t_out[:, s, :]).then_inc(t_st[s], 16)
            loop(sp, NW // 2, store_table)

            sp.wait_ge(s_flag, 1)
            flag = sp.value_load(unsorted[0:1, 0:1], min_val=0, max_val=N_EDGES)
            with sp.If(flag > 0):
                sp.wait_ge(s_attr, 48)
                attr_p = attr_d.rearrange("(p c) k -> p c k", p=P)

                def load_attr(i):
                    if not first(i):
                        sp.wait_ge(d_free, i)
                    sp.dma_start(d_rows[:, :, 0:ATTR], attr_p[:, ds(i * SORT_COLS, SORT_COLS), :]).then_inc(d_attr, 16)
                loop(sp, COLS // SORT_COLS, load_attr)
                sp.wait_ge(d_sent, 1)
                sp.dma_start(attr_d[:, :], sorted_d[:, 0:ATTR]).then_inc(d_back, 16)
                sp.dma_start(kB, sorted_d.rearrange("(p c) k -> p c k", p=P)[:, :, ATTR:SORT_ROW]).then_inc(d_ids, 16)
                sp.wait_ge(d_back, 16)

            sp.wait_ge(s_kA, 2)
            sp.dma_start(recA.rearrange("(p c) k -> p (c k)", p=P), kA_flat).then_inc(s_recA, 16)

            sp.wait_ge(s_recA, 16)
            sp.wait_ge(s_vtab, 1)

            def load_recA(i):
                for s in range(NS):
                    r = regs(ENG.SP, wtile, i * BODY + s * GV, TILES - 1)
                    after(sp, a_mm, s, i, NS)
                    for u in range(GV):
                        sp.dma_start(A_rec[:, s, u, :], tile_of(recA_t, r[u])).then_inc(a_rec[s], 16)
            loop(sp, LOOPS, load_recA)

            sp.wait_ge(s_kB, 1)
            sp.dma_start(recB.rearrange("(p c) k -> p (c k)", p=P), kB_flat).then_inc(s_recB, 16)
            sp.wait_ge(b_pad, 5)
            sp.dma_start(rows_d[N_EDGES:N_EDGES + 3 * P, :].rearrange("(p a) k -> p (a k)", a=3),
                         padrows.rearrange("p a k -> p (a k)")).then_inc(b_padout, 16)
            sp.dma_start(rows_d[N_EDGES + 3 * P:SLOTS, :], padrows[0:N_PAD - 3 * P, 0, :]).then_inc(b_padout, 16)
            sp.wait_ge(s_recB, 16)
            sp.wait_ge(s_attr, 48)

            def load_recB(i):
                for s in range(NS):
                    r = regs(ENG.SP, wtile, i * BODY + s * GV, TILES - 1)
                    if not first(i):
                        sp.wait_ge(b_sc[s], 16 * GV * i)
                    for u in range(GV):
                        sp.dma_start(B_rec[:, s, u, :], tile_of(recB_t, r[u])).then_inc(b_in[s], 16)
                        sp.dma_start(B_row[:, s, u, 0:ATTR], tile_of(attr_t, r[u])).then_inc(b_in[s], 16)
            loop(sp, LOOPS, load_recB)

            sp.wait_ge(b_sent, 1)
            sp.wait_ge(b_padout, 32)
            sp.wait_ge(s_vtab, 2)

            def load_rows(i):
                for s in range(NS):
                    r = regs(ENG.SP, wtile, i * BODY + s * GV, TILES - 1)
                    after(sp, c_W, s, i, NS)
                    for u in range(GV):
                        sp.dma_start(C_V[:, s, u, :], tile_of(rows_t, r[u])).then_inc(c_in[s], 16)
            loop(sp, LOOPS, load_rows)

            sp.wait_ge(n_x, 2 * G_LOOPS)
            sp.dma_start(out[0:whole, :].rearrange("(w p) f -> p w f", p=P), xs[:, 0:N_WIN - 1, :]).then_inc(s_final, 16)
            sp.dma_start(out[whole:N_NODES, :], xs[0:LAST_NODES, N_WIN - 1, :]).then_inc(s_final, 16)
            sp.wait_ge(s_final, 32)

        @block.gpsimd
        def _(pool):
            g = nc.gpsimd
            ch = Chain(pool, own["pool"])
            g.memset(zeros[:, :], 0.0).then_inc(s_const, 1)
            g.memset(ones[:, :], 1.0).then_inc(s_const, 1)
            ch.link(g.memset(ident[:, :], 0.0))
            g.memset(eps_t[:, :], EPS).then_inc(s_const, 1)
            g.iota(iota[:, :], pattern=[[1, P]], base=0, channel_multiplier=0,
                   allow_small_or_imprecise_dtypes=True).then_inc(s_const, 1)
            g.memset(mrun[:, :], -MASKED).then_inc(s_const, 1)
            g.affine_select(out=ident[:, :], in_=ident[:, :], compare_op=ALU.not_equal, fill=1.0, base=0,
                            pattern=[[-1, P]], channel_multiplier=1).then_inc(s_const, 1)
            pool.wait_ge(s_const, 2)
            g.affine_select(out=tri[:, :], in_=ones[:, :], compare_op=ALU.is_gt, fill=0.0, base=0,
                            pattern=[[1, P]], channel_multiplier=-1).then_inc(s_const, 1)
            pool.wait_ge(s_wcopied, len(jobs))
            g.iota(iota_v, pattern=[[1, VISITS]], base=0, channel_multiplier=0,
                   allow_small_or_imprecise_dtypes=True).then_inc(s_iotav, 1)

            pool.wait_ge(s_h, 1)

            def copy_h(i):
                for s in range(2):
                    after2(pool, t_T, s, i, 2)
                    turn(pool, "pool")
                    g.tensor_copy(t_h1[:, s, :], h[:, ds(i * 2 + s, 1), :].rearrange("p a k -> p (a k)")).then_inc(t_h, 1)
            loop(pool, NW // 2, copy_h)

            pool.wait_ge(s_flag, 1)
            flag = pool.value_load(unsorted[0:1, 0:1], min_val=0, max_val=N_EDGES)
            with pool.If(flag > 0):
                def scatter(i):
                    pool.wait_ge(d_attr, 16 * (i + 1))
                    pool.wait_ge(d_ready, i + 1)
                    turn(pool, "pool")
                    for c in range(SORT_COLS):
                        g.indirect_dma_start(
                            out=sorted_d[:, :], out_offset=bass.IndirectOffsetOnAxis(ap=d_pos[:, c:c + 1], axis=0),
                            in_=d_rows[:, c, :], in_offset=None).then_inc(d_sc, 16)
                    pool.wait_ge(d_sc, 16 * SORT_COLS * (i + 1))
                    pool.sem_inc(d_free, 1)
                loop(pool, COLS // SORT_COLS, scatter)
                pool.wait_ge(d_free, COLS // SORT_COLS)
                pool.sem_inc(d_sent, 1)

            for s in range(2):
                pool.wait_ge(t_st[s], 16 * (NW // 2))
            pool.wait_ge(s_vtab, 1)

            def gather(i):
                for s in range(NS):
                    after(pool, a_mm, s, i, NS)
                    pool.wait_ge(a_rec[s], 16 * GV * (i + 1))
                    turn(pool, "pool")
                    for u in range(GV):
                        g.indirect_dma_start(
                            out=A_g[:, s, u, :], out_offset=None, in_=table[:, :],
                            in_offset=bass.IndirectOffsetOnAxis(ap=A_rec[:, s, u, 1:2].bitcast(i32), axis=0)).then_inc(a_g[s], 16)
            loop(pool, LOOPS, gather)

            pool.wait_ge(a_done, 1)
            pool.wait_ge(g_ones, 1)

            def copy_in(i):
                for s in range(2):
                    w = ds(i * 4 + s * 2, 2)
                    after2(pool, g_T, s, i, 2)
                    turn(pool, "pool")
                    g.tensor_copy(G_in[:, s, 0:2, :], acc[:, w, 0:HID]).then_inc(g_in, 1)
                    g.tensor_copy(G_in[:, s, 2:4, :], h[:, w, :]).then_inc(g_in, 1)
            loop(pool, G_LOOPS, copy_in)

            pool.wait_ge(b_padout, 32)

            def send(i):
                for s in range(NS):
                    pool.wait_ge(b_in[s], 32 * GV * (i + 1))
                    after(pool, b_row, s, i)
                    after(pool, b_pos, s, i, incs=2)
                    turn(pool, "pool")
                    for u in range(GV):
                        g.indirect_dma_start(
                            out=rows_d[:, :], out_offset=bass.IndirectOffsetOnAxis(ap=B_pos[:, s, u:u + 1], axis=0),
                            in_=B_row[:, s, u, :], in_offset=None, bounds_check=SLOTS - 1, oob_is_err=False).then_inc(b_sc[s], 16)
            loop(pool, LOOPS, send)
            for s in range(NS):
                pool.wait_ge(b_sc[s], 16 * GV * LOOPS)
            g.iota(iota_v, pattern=[[1, VISITS]], base=0, channel_multiplier=0,
                   allow_small_or_imprecise_dtypes=True).then_inc(s_iotav, 1)
            pool.sem_inc(b_sent, 1)

            pool.wait_ge(s_vtab, 2)
            pool.wait_ge(c_init, 1)

            def tick(i, s, stages):
                if 0 in stages:
                    after(pool, c_kl, s, i)
                    after(pool, c_ag, s, i, NS)
                    turn(pool, "pool")
                    for u in range(GV):
                        m = g.tensor_scalar(C_S[:, s, u, :], iota[:, :], C_kl[:, s, u:u + 1], None, ALU.is_equal)
                        if u < GV - 1:
                            ch.do(m)
                    m.then_inc(c_S, 1)
                    after(pool, c_MKt, s, i, NS)
                    after(pool, c_S, s, i)
                    turn(pool, "pool")
                    g.tensor_scalar(C_MK[:, s, :, :], C_S[:, s, :, :], -1.0, MASKED, ALU.add, ALU.mult).then_inc(c_nb, 1)
                if 3 in stages:
                    t, j = stages[3]
                    after(pool, c_p, t, j)
                    after(pool, c_ag, t, j, 2)
                    g.tensor_tensor(C_W[:, t % 2, :, :], C_V[:, t, :, ATTR:ATTR + HID + 1],
                                    per_group(C_p[:, t, :], HID + 1), ALU.mult).then_inc(c_W, 1)
                if 2 in stages:
                    t, j = stages[2]
                    r = regs(ENG.Pool, wwin, j * BODY + t * GV, N_WIN - 1)
                    after(pool, c_tm, t, j)
                    after(pool, c_cr, t, j, NS)
                    after(pool, c_mg, t, j, NS)
                    for u in range(GV):
                        turn(pool, "pool")
                        ch.link(g.tensor_copy(C_mo[:, t, u:u + 1], mrun[:, ds(r[u], 1)]))
                        turn(pool, "pool")
                        ch.link(g.tensor_scalar(C_mn[:, t, u:u + 1], C_mo[:, t, u:u + 1], C_tm[:, t, u:u + 1], None, ALU.max))
                        turn(pool, "pool")
                        m = g.tensor_copy(mrun[:, ds(r[u], 1)], C_mn[:, t, u:u + 1])
                        if u < GV - 1:
                            ch.link(m)
                    m.then_inc(c_mn, 1)
                    after(pool, c_mn, t, j)
                    g.tensor_tensor(C_df[:, t, :], C_mo[:, t, :], C_mn[:, t, :], ALU.subtract).then_inc(c_df, 1)

            run_ticks(pool, tick, ch, {0: GV - 1, 2: 3 * GV - 1})

            pool.wait_ge(n_ones, 1)

            def copy_h1(i):
                for s in range(2):
                    after2(pool, n_T, s, i, 2)
                    turn(pool, "pool")
                    g.tensor_copy(G_in[:, s, 2:4, :], h[:, ds(i * 4 + s * 2, 2), :]).then_inc(n_in, 1)
            loop(pool, G_LOOPS, copy_h1)

        @block.scalar
        def _(act):
            a = nc.scalar
            act.wait_ge(s_wT, len(jobs))
            for j, (_, m, c, wT) in enumerate(jobs):
                a.copy(wT, bank[j // 4][0:c, (j % 4) * P:(j % 4) * P + m]).then_inc(s_wcopied, 1)
            act.wait_ge(s_const, N_CONST)
            act.wait_ge(s_var, 1)
            a.activation(small[:, NW:2 * NW], small[:, 0:NW], ACT.Sqrt, bias=eps_t[:, :]).then_inc(s_std, 1)

            def table_copies(i):
                for s in range(2):
                    after2(act, t_T, s, i)
                    after2(act, t_mm, s, i, 2)
                    a.copy(t_hT[:, s, :], bank[s][0:HID, 0:P]).then_inc(t_Tc, 1)
                    after2(act, t_mm, s, i)
                    if not first(i):
                        act.wait_ge(t_st[s], 16 * i)
                    a.copy(t_out[:, s, :], bank[2 + s][:, :]).then_inc(t_cp, 1)
            loop(act, NW // 2, table_copies)

            act.wait_ge(g_ones, 1)

            def update0(i):
                for s in range(2):
                    after2(act, g_T, s, i)
                    after2(act, g_mm, s, i, 2)
                    a.copy(G_T[0:HID, s, :, :], four(bank[s], P)[0:HID]).then_inc(g_Tc, 1)
                    after2(act, g_mm, s, i)
                    after2(act, g_x, s, i, 2)
                    a.activation(G_t[:, s, :, :], two(bank[2 + s], 4 * HID)[:, :, 0:2 * HID], ACT.Tanh, scale=0.5).then_inc(g_t, 1)
                    after2(act, g_v, s, i)
                    a.activation(G_n[:, s, :, :], G_v[:, s, :, :], ACT.Tanh).then_inc(g_n, 1)
            loop(act, G_LOOPS, update0)
            act.wait_ge(s_var, 2)
            a.activation(small[:, NW:2 * NW], small[:, 0:NW], ACT.Sqrt, bias=eps_t[:, :]).then_inc(s_std, 1)

            act.wait_ge(s_recB, 16)
            act.wait_ge(b_pad, 5)

            def rows(i, with_table):
                if with_table:
                    act.wait_ge(b_pT, i + 1)
                    if not first(i):
                        act.wait_ge(b_pmm, i)
                    a.copy(B_hT[0:HID, :], bank[4][0:HID, 2 * P:3 * P]).then_inc(b_pTc, 1)
                for s in range(NS):
                    after(act, b_DT, s, i)
                    after(act, b_hr, s, i, NS)
                    a.copy(B_DT[:, s, :, :], four(bank[s], P)).then_inc(b_DTc, 1)
                    after(act, b_hr, s, i)
                    if not first(i):
                        act.wait_ge(b_sc[s], 16 * GV * i)
                    a.copy(B_row[:, s, :, ATTR:ATTR + HID], four(bank[4 + s], HID)).then_inc(b_row, 1)
                    if with_table and s == 0:
                        act.wait_ge(b_pmm, i + 1)
                        a.copy(p_tab[:, ds(i, 1), :], bank[5][:, 2 * P:2 * P + H1].unsqueeze(1)).then_inc(b_pcp, 1)
            loop(act, NW, lambda i: rows(i, True))
            with act.Fori(NW, LOOPS) as i:
                rows(i, False)

            act.wait_ge(s_vtab, 2)

            def tick(i, s, stages):
                if 0 in stages:
                    after(act, c_St, s, i)
                    after(act, c_mg, s, i, NS)
                    a.copy(C_ST[:, s, :, :], four(bank[0], P)).then_inc(c_STc, 1)
                if 3 in stages:
                    t, j = stages[3]
                    after(act, c_d, t, j)
                    after(act, c_W, t, j, NS)
                    a.activation(C_p[:, t, :], C_d[:, t, :], ACT.Exp).then_inc(c_p, 1)
                if 0 in stages:
                    after(act, c_Vt, s, i)
                    after(act, c_pre, s, i, 1)
                    a.copy(C_VT, four(bank[1], P)[0:ATTR + HID]).then_inc(c_VTc, 1)
                if 2 in stages:
                    t, j = stages[2]
                    after(act, c_df, t, j)
                    after(act, c_acc, t, j, NS)
                    a.activation(C_cr[:, t, :], C_df[:, t, :], ACT.Exp).then_inc(c_cr, 1)
            run_ticks(act, tick)

            act.wait_ge(n_ones, 1)

            def update1(i):
                for s in range(2):
                    after2(act, n_T, s, i)
                    after2(act, n_mm, s, i, 2)
                    a.copy(G_T[0:HID + 1, s, 0:2, :], four(bank[s], P)[0:HID + 1, 0:2]).then_inc(n_Tc, 1)
                    a.copy(G_T[0:HID, s, 2:4, :], four(bank[s], P)[0:HID, 2:4]).then_inc(n_Tc, 1)
                    after2(act, n_ms, s, i)
                    after2(act, n_x, s, i, 2)
                    a.copy(G_m[:, s, :, :], two(bank[4 + s], HID)).then_inc(n_msc, 1)
                    a.copy(G_mT[0:HID, s, :, :], two(bank[4 + s][:, 2 * P:4 * P], P)[0:HID]).then_inc(n_msc, 1)
                    after2(act, n_mm, s, i)
                    a.activation(G_t[:, s, :, :], two(bank[2 + s], 4 * HID)[:, :, 0:2 * HID], ACT.Tanh, scale=0.5).then_inc(n_t, 1)
                    after2(act, n_v, s, i)
                    a.activation(G_n[:, s, :, :], G_v[:, s, :, :], ACT.Tanh).then_inc(n_n, 1)
            loop(act, G_LOOPS, update1)

        @block.tensor
        def _(pe):
            mm = nc.tensor.matmul
            tr = nc.tensor.transpose
            pe.wait_ge(s_const, N_CONST)
            pe.wait_ge(s_w, 16 * N_WDMA)
            for j, ((_, m, c, _), r) in enumerate(zip(jobs, raw)):
                tr(bank[j // 4][0:c, (j % 4) * P:(j % 4) * P + m], r, ident[0:m, 0:m]).then_inc(s_wT, 1)

            pe.wait_ge(s_wcopied, len(jobs))
            pe.wait_ge(s_h, 1)

            def make_table(i):
                for s in range(2):
                    after2(pe, t_Tc, s, i, 2)
                    after2(pe, t_h, s, i)
                    turn(pe, "pe")
                    tr(bank[s][0:HID, 0:P], t_h1[:, s, :], ident[:, :]).then_inc(t_T, 1)
                for s in range(2):
                    after2(pe, t_Tc, s, i)
                    after2(pe, t_cp, s, i, 2)
                    mm(bank[2 + s][:, :], t_hT[:, s, :], AT[:, :], start=True, stop=True).then_inc(t_mm, 1)
            loop(pe, NW // 2, make_table)

            def visit_counts(k):
                pe.wait_ge(s_cnt, k + 1)
                mm(bank[4][:, 0:N_KEYS], ones[:, :], cnt[:, :], start=True, stop=True)
                mm(bank[4][:, P:P + N_KEYS], tri[:, :], cnt[:, :], start=True, stop=True)
                if k == 0:
                    pe.wait_ge(s_flagp, 1)
                    mm(bank[4][0:1, 3 * P:3 * P + 1], out_of_order[:, :], ones[:, 0:1], start=True, stop=True)
                mm(bank[4][0:N_KEYS, 2 * P:2 * P + 1], cnt[:, :], ones[:, 0:1], start=True, stop=True).then_inc(s_tot, 1)

            def visit_tables(k):
                K = N_KEYS
                pe.wait_ge(s_cc, k + 1)
                mm(bank[5][0:K, 0:1], tri[0:K, 0:K], cc[k][0:K, :], start=True, stop=True).then_inc(s_start, 1)
                pe.wait_ge(s_nt, k + 1)
                mm(bank[5][0:K, 1:2], tri[0:K, 0:K], nt[0:K, :], start=True, stop=True).then_inc(s_vstart, 1)
                pe.wait_ge(s_off, k + 1)
                mm(bank[5][0:HW, 2:3], ident[0:N_WIN, 1:N_WIN], off[0:N_WIN, :], start=True, stop=True).then_inc(s_shift, 1)
                pe.wait_ge(s_vmask, k + 1)
                for q in range(4):
                    m = vmask[0:HW, q * VCHUNK:(q + 1) * VCHUNK]
                    mm(bank[q][:, 0:VCHUNK], ones[0:HW, :], m, start=True, stop=True)
                    last = mm(bank[4 + q][:, 0:VCHUNK], dbc[0:HW, :], m, start=True, stop=True)
                last.then_inc(s_vsum, 1)

            pe.wait_ge(t_cp, NW)
            visit_counts(0)
            visit_tables(0)

            pe.wait_ge(s_vtab, 1)
            pe.wait_ge(a_zero, 1)

            def sums0(i):
                for s in range(NS):
                    after(pe, a_D, s, i)
                    if not first(i):
                        pe.wait_ge(a_acc, BODY * (i - 1) + GV * (s + 1))
                    pe.wait_ge(a_g[s], 16 * GV * (i + 1))
                    for u in range(GV):
                        last = mm(bank[s][:, u * HID:(u + 1) * HID], A_D[:, s, u, :], A_g[:, s, u, :], start=True, stop=True)
                    last.then_inc(a_mm, 1)
            loop(pe, COUNT_LOOPS, sums0)
            visit_counts(1)
            with pe.Fori(COUNT_LOOPS, LOOPS) as i:
                sums0(i)

            pe.wait_ge(a_done, 1)
            pe.wait_ge(g_ones, 1)

            def update0(i):
                for s in range(2):
                    after2(pe, g_Tc, s, i, 2)
                    after2(pe, g_in, s, i, incs=2)
                    turn(pe, "pe")
                    for u in range(4):
                        last = tr(bank[s][0:HID, u * P:(u + 1) * P], G_in[:, s, u, :], ident[:, :])
                    last.then_inc(g_T, 1)
                for s in range(2):
                    after2(pe, g_Tc, s, i)
                    after2(pe, g_x, s, i, 2)
                    for u in range(2):
                        b = bank[2 + s][:, u * 4 * HID:(u + 1) * 4 * HID]
                        mm(b[:, 0:GATES], G_T[:, s, u, :], wih0T[:, :], start=True, stop=False)
                        mm(b[:, 0:2 * HID], G_T[:, s, 2 + u, :], whh0T[:, 0:2 * HID], start=False, stop=False)
                        last = mm(b[:, GATES:4 * HID], G_T[:, s, 2 + u, :], whh0T[:, 2 * HID:GATES], start=False, stop=True)
                    last.then_inc(g_mm, 1)
            loop(pe, G_LOOPS, update0)

            pe.wait_ge(s_h, 2)
            pe.wait_ge(b_pad, 5)

            def rows(i, with_table):
                if with_table:
                    after(pe, b_row, 0, i, NS)
                    pe.wait_ge(b_hc, i + 1)
                    turn(pe, "pe")
                    tr(bank[4][0:HID, 2 * P:3 * P], B_h, ident[:, :]).then_inc(b_pT, 1)
                for s in range(NS):
                    r = regs(ENG.PE, wwin, i * BODY + s * GV, N_WIN - 1)
                    after(pe, b_D, s, i)
                    after(pe, b_DTc, s, i, NS)
                    for u in range(GV):
                        last = tr(bank[s][:, u * P:(u + 1) * P], B_D[:, s, u, :], ident[:, :])
                    last.then_inc(b_DT, 1)
                    after(pe, b_DTc, s, i)
                    after(pe, b_row, s, i, NS)
                    if with_table and s < 2:
                        pe.wait_ge((b_pTc, b_pcp)[s], i + 1)
                    for u in range(GV):
                        last = mm(bank[4 + s][:, u * HID:(u + 1) * HID], B_DT[:, s, u, :],
                                  h[:, ds(r[u], 1), :].rearrange("p a k -> p (a k)"), start=True, stop=True)
                    last.then_inc(b_hr, 1)
                    if with_table and s == 0:
                        after(pe, b_row, 1, i, NS)
                        mm(bank[5][:, 2 * P:2 * P + H1], B_hT[:, :], waT[:, :], start=True, stop=True).then_inc(b_pmm, 1)
            loop(pe, NW, lambda i: rows(i, True))
            with pe.Fori(NW, LOOPS) as i:
                rows(i, False)
            pe.wait_ge(b_row, NS * LOOPS)
            pe.wait_ge(b_pcp, NW)
            visit_tables(1)

            pe.wait_ge(s_vtab, 2)

            def tick(i, s, stages):
                if 3 in stages:
                    t, j = stages[3]
                    after(pe, c_mn, t, j)
                    after(pe, c_d, t, j, 1)
                    for u in range(GV):
                        last = mm(bank[5][:, u:u + 1], C_ST[:, t, u, :], C_mn[:, t, u:u + 1], start=True, stop=True)
                    last.then_inc(c_mg, 1)
                if 0 in stages:
                    after(pe, c_S, s, i)
                    after(pe, c_STc, s, i, 1)
                    for u in range(GV):
                        last = tr(bank[0][:, u * P:(u + 1) * P], C_S[:, s, u, :], ident[:, :])
                    last.then_inc(c_St, 1)
                    pe.wait_ge(c_in[s], 16 * GV * (i + 1))
                    after(pe, c_VTc, s, i, 1)
                    for u in range(GV):
                        last = tr(bank[1][0:ATTR + HID, u * P:(u + 1) * P], C_V[:, s, u, 0:ATTR + HID], ident[:, :])
                    last.then_inc(c_Vt, 1)
                if 1 in stages:
                    t, j = stages[1]
                    r = regs(ENG.PE, wwin, j * BODY + t * GV, N_WIN - 1)
                    after(pe, c_STc, t, j)
                    after(pe, c_VTc, t, j)
                    after(pe, c_sc, t, j, 1)
                    for u in range(GV):
                        b = bank[2 + u // 2][:, (u % 2) * H1:(u % 2 + 1) * H1]
                        mm(b, C_ST[:, t, u, :], p_tab[:, ds(r[u], 1), :].rearrange("p a k -> p (a k)"), start=True, stop=False)
                        last = mm(b, C_VT[:, u, :], wv[:, :], start=False, stop=True)
                    last.then_inc(c_pre, 1)
                if 2 in stages:
                    t, j = stages[2]
                    after(pe, c_MK, t, j)
                    after(pe, c_tm, t, j, 1)
                    for u in range(GV):
                        last = tr(bank[4][:, u * P:(u + 1) * P], C_MK[:, t, u, :], ident[:, :])
                    last.then_inc(c_MKt, 1)
                if 3 in stages:
                    t, j = stages[3]
                    after(pe, c_W, t, j)
                    after(pe, c_acc, t, j, 2)
                    for u in range(GV):
                        last = mm(bank[6 + t % 2][:, u * (HID + 1):(u + 1) * (HID + 1)], C_S[:, t, u, :], C_W[:, t % 2, u, :],
                                  start=True, stop=True)
                    last.then_inc(c_ag, 1)
            run_ticks(pe, tick)

            pe.wait_ge(n_ones, 1)

            def update1(i):
                for s in range(2):
                    after2(pe, n_c, s, i)
                    after2(pe, n_Tc, s, i, 2, incs=2)
                    after2(pe, n_in, s, i)
                    turn(pe, "pe")
                    for u in range(2):
                        tr(bank[s][0:HID + 1, u * P:(u + 1) * P], G_c[:, s, u, :], ident[:, :])
                        last = tr(bank[s][0:HID, (2 + u) * P:(3 + u) * P], G_in[:, s, 2 + u, :], ident[:, :])
                    last.then_inc(n_T, 1)
                for s in range(2):
                    after2(pe, n_Tc, s, i, incs=2)
                    after2(pe, n_msc, s, i, 2, incs=2)
                    for u in range(2):
                        mm(bank[4 + s][:, u * HID:(u + 1) * HID], G_T[:, s, u, :], wlinT[:, :], start=True, stop=True)
                        last = mm(bank[4 + s][0:HID, (2 + u) * P:(3 + u) * P], wlinT[:, :], G_T[:, s, u, :], start=True, stop=True)
                    last.then_inc(n_ms, 1)
                    after2(pe, n_msc, s, i, incs=2)
                    after2(pe, n_x, s, i, 2)
                    for u in range(2):
                        b = bank[2 + s][:, u * 4 * HID:(u + 1) * 4 * HID]
                        mm(b[:, 0:GATES], G_T[:, s, 2 + u, :], wih1T[:, :], start=True, stop=False)
                        mm(b[:, 0:2 * HID], G_mT[:, s, u, :], whh1T[:, 0:2 * HID], start=False, stop=False)
                        last = mm(b[:, GATES:4 * HID], G_mT[:, s, u, :], whh1T[:, 2 * HID:GATES], start=False, stop=True)
                    last.then_inc(n_mm, 1)
            loop(pe, G_LOOPS, update1)

        @block.vector
        def _(dve):
            v = nc.vector
            ch = Chain(dve, own["dve"])
            lo = P - 32
            for t, val in ((dst_i, PAD_KEY), (src_i, PAD_KEY), (typ_i, 0)):
                v.memset(t[lo:P, LAST_COLS:COLS], val).then_inc(s_padded, 1)
            v.memset(xs[:, N_WIN - 1:NW, :], 0.0).then_inc(s_padded, 1)
            v.memset(before[:, :], 0).then_inc(s_padded, 1)

            dve.wait_ge(s_ids, 96)
            dve.wait_ge(s_padded, 5)
            ch.link(v.tensor_scalar(scan.bitcast(i32), dst_i, 7, None, ALU.arith_shift_right))
            ch.link(v.tensor_copy(win, scan.bitcast(i32)))

            dve.wait_ge(s_before, 16)
            ch.link(v.tensor_tensor(scan[:, 0:1], dst_i[:, 0:1], before[:, :], ALU.is_lt))
            ch.link(v.tensor_tensor(scan[:, 1:COLS], dst_i[:, 1:COLS], dst_i[:, 0:COLS - 1], ALU.is_lt))
            v.tensor_reduce(out_of_order[:, :], scan, AX.X, ALU.add).then_inc(s_flagp, 1)

            def normalise(k):
                flat = NW * HID
                sq = acc[:, :, :].rearrange("p w k -> p (w k)")[:, 0:flat].rearrange("p (w k) -> p w k", k=HID)
                var, std, mean = small[:, 0:NW], small[:, NW:2 * NW], small[:, 2 * NW:3 * NW]

                def bc(t):
                    return t.unsqueeze(2).to_broadcast([P, NW, HID])
                ch.link(v.tensor_reduce(mean, xs[:, :, :], AX.X, ALU.add))
                ch.link(v.tensor_scalar(mean, mean, 1.0 / HID, None, ALU.mult))
                ch.link(v.tensor_tensor(h[:, :, :], xs[:, :, :], bc(mean), ALU.subtract))
                ch.link(v.tensor_tensor(sq, h[:, :, :], h[:, :, :], ALU.mult))
                ch.link(v.tensor_reduce(var, sq, AX.X, ALU.add))
                v.tensor_scalar(var, var, 1.0 / HID, None, ALU.mult).then_inc(s_var, 1)
                dve.wait_ge(s_std, k)
                ch.link(v.reciprocal(std, std))
                ch.link(v.tensor_tensor(h[:, :, :], h[:, :, :], bc(std), ALU.mult))
                v.tensor_scalar(h[:, :, :], h[:, :, :], 0.0, None, ALU.max).then_inc(s_h, 1)

            dve.wait_ge(s_x, 32)
            normalise(1)

            def count(w):
                ch.link(v.tensor_scalar(mask, win, iota[:, ds(w, 1)], None, ALU.is_equal, ALU.add, accum_out=cnt[:, ds(w, 1)]))

            dve.wait_ge(s_const, N_CONST)
            with dve.Fori(0, N_KEYS // 2) as i:
                ch.body(i, 2)
                count(i * 2)
                count(i * 2 + 1)
                ch.end_body()
            ch.end_loop(N_KEYS // 2)
            dve.sem_inc(s_cnt, 1)

            K = N_KEYS

            def totals(k):
                dve.wait_ge(s_tot, k + 1)
                v.tensor_copy(cc[k][0:K, :], bank[4][0:K, 2 * P:2 * P + 1]).then_inc(s_cc, 1)
                tot, incl = small[:, 3 * P:3 * P + K], small[:, 2 * P:2 * P + K]
                ch.link(v.tensor_copy(tot, bank[4][:, 0:K]))
                ch.link(v.tensor_tensor_scan(incl, tot, tot, 0.0, ALU.add, ALU.max))
                ch.link(v.tensor_tensor(incl, incl, tot, ALU.subtract))
                ch.link(v.tensor_tensor(place0[:, :], incl, bank[4][:, P:P + K], ALU.add))
                if k == 0:
                    v.tensor_copy(unsorted[:, :], bank[4][0:1, 3 * P:3 * P + 1]).then_inc(s_flag, 1)

            def visit_table(k):
                e = [small[0:K, j:j + 1] for j in range(20, 30)]
                start, end, ft, lt, hs, vend, t1 = e[0:7]
                si, ei = e[7].bitcast(i32), e[8].bitcast(i32)
                dve.wait_ge(s_start, k + 1)
                ch.link(v.tensor_copy(start, bank[5][0:K, 0:1]))
                ch.link(v.tensor_tensor(end, start, cc[k][0:K, :], ALU.add))
                ch.link(v.tensor_copy(si, start))
                ch.link(v.tensor_scalar(ei, end, -1.0, None, ALU.add))
                ch.link(v.tensor_scalar(si, si, 7, None, ALU.arith_shift_right))
                ch.link(v.tensor_scalar(ei, ei, 7, None, ALU.arith_shift_right))
                ch.link(v.tensor_copy(ft, si))
                ch.link(v.tensor_copy(lt, ei))
                ch.link(v.scalar_tensor_tensor(t1, lt, 1.0, ft, ALU.add, ALU.subtract))
                ch.link(v.tensor_scalar(hs, cc[k][0:K, :], 0.0, None, ALU.is_gt))
                v.tensor_tensor(nt[0:K, :], t1, hs, ALU.mult).then_inc(s_nt, 1)
                dve.wait_ge(s_vstart, k + 1)
                ch.link(v.tensor_tensor(vend, nt[0:K, :], bank[5][0:K, 1:2], ALU.add))
                v.tensor_tensor(off[0:K, :], ft, bank[5][0:K, 1:2], ALU.subtract).then_inc(s_off, 1)
                dve.wait_ge(s_shift, k + 1)
                ch.link(v.tensor_tensor(t1[0:HW], bank[5][0:HW, 2:3], off[0:HW, :], ALU.subtract))
                ch.link(v.tensor_scalar(dbc[0:HW, :], ones[0:HW, :], t1[0:HW], None, ALU.mult))
                dve.wait_ge(s_iotav, k + 1)
                v.tensor_scalar(vmask[0:HW, :], iota_v[0:HW, :], vend[0:HW], None, ALU.is_ge).then_inc(s_vmask, 1)
                dve.wait_ge(s_vsum, k + 1)
                for q in range(4):
                    c = slice(q * VCHUNK, (q + 1) * VCHUNK)
                    ch.do(v.tensor_scalar(wbase[:, c], bank[q][:, 0:VCHUNK], float(P), None, ALU.mult))
                    ch.do(v.tensor_copy(wwin[0:1, c], bank[q][0:1, 0:VCHUNK]))
                    ch.link(v.tensor_tensor(iota_v[0:1, c], iota_v[0:1, c], bank[4 + q][0:1, 0:VCHUNK], ALU.add))
                    ch.link(v.tensor_scalar(wtile[0:1, c], iota_v[0:1, c], float(TILES - 1), None, ALU.min))
                dve.sem_inc(s_vtab, 1)

            totals(0)
            visit_table(0)

            def place(w, where, ch):
                ch.link(v.tensor_scalar(mask, win, iota[:, ds(w, 1)], None, ALU.is_equal))
                ch.link(v.tensor_tensor_scan(scan, mask, mask, place0[:, ds(w, 1)], ALU.add, ALU.max))
                turn(dve, "dve")
                ch.link(v.copy_predicated(where, mask.bitcast(u16), scan))

            dve.wait_ge(s_flag, 1)
            flag = dve.value_load(unsorted[0:1, 0:1], min_val=0, max_val=N_EDGES)
            with dve.If(flag > 0):
                dch = Chain(dve, d_step)
                dch.link(v.memset(d_place, 0.0))
                with dve.Fori(0, N_KEYS) as w:
                    dch.body(w, 3)
                    place(w, d_place, dch)
                    dch.end_body()
                dch.end_loop(N_KEYS)

                def stage(i):
                    dch.body(i, 3)
                    if not first(i):
                        dve.wait_ge(d_free, i)
                    c = ds(i * SORT_COLS, SORT_COLS)
                    for k, t in enumerate((dst_i, src_i, typ_i)):
                        dch.link(v.tensor_copy(d_rows[:, :, ATTR + k].bitcast(i32), t[:, c]))
                    v.tensor_scalar(d_pos, d_place[:, c], -1.0, None, ALU.add).then_inc(d_ready, 1)
                    dch.end_body()
                dch.link(v.memset(d_rows[:, :, SORT_ROW - 1], 0.0))
                loop(dve, COLS // SORT_COLS, stage)
                dch.end_loop(COLS // SORT_COLS)
                dve.wait_ge(d_ids, 16)
                ids = kB_flat.bitcast(i32).rearrange("p (c k) -> p c k", k=REC)
                for k, t in enumerate((dst_i, src_i, scan.bitcast(i32))):
                    dch.link(v.tensor_copy(t, ids[:, :, k]))
                dch.link(v.tensor_copy(typ_i, scan.bitcast(i32)))

            v.tensor_copy(kA[:, :, 0], dst_i).then_inc(s_kA, 1)
            v.scalar_tensor_tensor(kA[:, :, 1].bitcast(i32), src_i, float(TYPES), typ_i, ALU.mult, ALU.add).then_inc(s_kA, 1)

            dve.wait_ge(s_recA, 16)
            ch.link(v.tensor_copy(kB[:, :, 0], dst_i))
            ch.link(v.tensor_copy(kB[:, :, 1], src_i))
            ch.link(v.memset(kB[:, :, 2:4], 0.0))
            ch.link(v.tensor_scalar(scan.bitcast(i32), src_i, 7, None, ALU.arith_shift_right))
            ch.link(v.tensor_copy(win, scan.bitcast(i32)))
            v.memset(acc[:, :, :], 0.0).then_inc(a_zero, 1)
            dve.wait_ge(a_zero, 1)
            for s in range(2):
                dve.wait_ge(t_st[s], 16 * (NW // 2))

            def sums0(i, extra, steps):
                ch.body(i, NS + steps)
                for s in range(NS):
                    r = regs(ENG.DVE, wwin, i * BODY + s * GV, N_WIN - 1)
                    dve.wait_ge(a_rec[s], 16 * GV * (i + 1))
                    after(dve, a_mm, s, i, NS)
                    ch.link(v.tensor_tensor(A_kl[:, s, :], A_rec[:, s, :, 0], wbase[:, ds(i * BODY + s * GV, GV)], ALU.subtract))
                    v.tensor_tensor(A_D[:, s, :, :], iota[:, :].unsqueeze(1).to_broadcast([P, GV, P]),
                                    per_group(A_kl[:, s, :], P), ALU.is_equal).then_inc(a_D, 1)
                    if s in (0, 2) and extra:
                        extra(i, s // 2)
                    after(dve, a_mm, s, i)
                    for u in range(GV):
                        if not (first(i) and s == 0 and u == 0):
                            dve.wait_ge(a_acc, i * BODY + s * GV + u)
                        t = acc[:, ds(r[u], 1), 0:HID].rearrange("p a k -> p (a k)")
                        v.tensor_tensor(t, t, bank[s][:, u * HID:(u + 1) * HID], ALU.add).then_inc(a_acc, 1)
                ch.end_body()

            loop(dve, COUNT_LOOPS, lambda i: sums0(i, lambda i, j: count(i * 2 + j), 2))
            ch.end_loop(COUNT_LOOPS)
            ch.per = 0
            dve.sem_inc(s_cnt, 1)
            totals(1)
            ch.base += ch.k
            ch.k = 0
            ch.base -= COUNT_LOOPS * (NS + 6)
            with dve.Fori(COUNT_LOOPS, COUNT_LOOPS + PLACE_LOOPS) as i:
                sums0(i, lambda i, j: place((i - COUNT_LOOPS) * 2 + j, kB[:, :, 2], ch), 6)
            ch.base += (COUNT_LOOPS + PLACE_LOOPS) * (NS + 6)
            ch.base -= (COUNT_LOOPS + PLACE_LOOPS) * NS
            with dve.Fori(COUNT_LOOPS + PLACE_LOOPS, LOOPS) as i:
                sums0(i, None, 0)
            ch.base += LOOPS * NS
            ch.i = ch.per = ch.k = 0
            v.tensor_scalar(kB[:, :, 2], kB[:, :, 2], -1.0, None, ALU.add).then_inc(s_kB, 1)

            dve.wait_ge(a_acc, LOOPS * BODY)
            dve.sem_inc(a_done, 1)
            v.memset(G_T[HID:HID + 1, :, :, :], 1.0).then_inc(g_ones, 1)

            def gru(i, s, sT, sV, sN, hid):
                b = two(bank[2 + s], 4 * HID)
                after2(dve, sT, s, i)
                ch.link(v.scalar_tensor_tensor(G_u[:, s, :, :], G_t[:, s, :, 0:HID], 1.0, b[:, :, GATES:4 * HID], ALU.add, ALU.mult))
                v.scalar_tensor_tensor(G_v[:, s, :, :], G_u[:, s, :, :], 0.5, b[:, :, 2 * HID:GATES], ALU.mult, ALU.add).then_inc(sV, 1)
                after2(dve, sN, s, i)
                ch.link(v.tensor_tensor(G_d[:, s, :, :], hid, G_n[:, s, :, :], ALU.subtract))
                ch.link(v.scalar_tensor_tensor(G_e[:, s, :, :], G_t[:, s, :, HID:2 * HID], 1.0, G_d[:, s, :, :], ALU.add, ALU.mult))
                ch.link(v.scalar_tensor_tensor(G_d[:, s, :, :], G_e[:, s, :, :], 0.5, G_n[:, s, :, :], ALU.mult, ALU.add))

            def update0(i):
                ch.body(i, 8)
                for s in range(2):
                    w = ds(i * 4 + s * 2, 2)
                    gru(i, s, g_t, g_v, g_n, h[:, w, :])
                    v.tensor_tensor(xs[:, w, :], xs[:, w, :], G_d[:, s, :, :], ALU.add).then_inc(g_x, 1)
                ch.end_body()
            loop(dve, G_LOOPS, update0)
            ch.end_loop(G_LOOPS)
            dve.wait_ge(g_x, 2 * G_LOOPS)
            normalise(2)
            dve.wait_ge(s_h, 2)

            v.memset(B_hT[HID:HID + 1, :], 1.0).then_inc(b_pad, 1)
            v.memset(B_row[:, :, :, ATTR + HID:ROW], 0.0).then_inc(b_pad, 1)
            v.memset(padrows, 0.0).then_inc(b_pad, 1)
            dve.wait_ge(b_pad, 3)
            v.memset(B_row[:, :, :, ROW_ONE], 1.0).then_inc(b_pad, 1)
            v.memset(padrows[:, :, ROW_SRC], float(PAD_KEY)).then_inc(b_pad, 1)

            def rows(i, with_table=False):
                ch.body(i, 3 * NS)
                if with_table:
                    if not first(i):
                        dve.wait_ge(b_pT, i)
                    v.tensor_copy(B_h, h[:, ds(i, 1), :].rearrange("p a k -> p (a k)")).then_inc(b_hc, 1)
                for s in range(NS):
                    dve.wait_ge(b_in[s], 32 * GV * (i + 1))
                    v.tensor_tensor(B_kl[:, s, :], B_rec[:, s, :, 0], wbase[:, ds(i * BODY + s * GV, GV)], ALU.subtract).then_inc(b_kl, 1)
                    after(dve, b_kl, s, i)
                    after(dve, b_DT, s, i, NS)
                    v.tensor_tensor(B_D[:, s, :, :], iota[:, :].unsqueeze(1).to_broadcast([P, GV, P]),
                                    per_group(B_kl[:, s, :], P), ALU.is_equal).then_inc(b_D, 1)
                    ch.link(v.tensor_scalar(B_ge[:, s, :], B_kl[:, s, :], 0.0, None, ALU.is_ge))
                    ch.link(v.scalar_tensor_tensor(B_in[:, s, :], B_kl[:, s, :], float(P), B_ge[:, s, :], ALU.is_lt, ALU.mult))
                    ch.link(v.scalar_tensor_tensor(B_sh[:, s, :], B_rec[:, s, :, 2], -BIG, B_in[:, s, :], ALU.add, ALU.mult))
                    if not first(i):
                        dve.wait_ge(b_sc[s], 16 * GV * i)
                    v.tensor_copy(B_row[:, s, :, ROW_SRC], B_rec[:, s, :, 1]).then_inc(b_pos, 1)
                    v.tensor_scalar(B_pos[:, s, :], B_sh[:, s, :], BIG, None, ALU.add).then_inc(b_pos, 1)
                ch.end_body()
            dve.wait_ge(b_pad, 5)
            loop(dve, NW, lambda i: rows(i, True))
            with dve.Fori(NW, LOOPS) as i:
                rows(i)
            ch.end_loop(LOOPS)

            dve.wait_ge(b_sent, 1)
            visit_table(1)
            v.memset(acc[:, :, :], 0.0).then_inc(c_init, 1)
            dve.wait_ge(c_init, 1)

            def tick(i, s, stages):
                if 0 in stages:
                    dve.wait_ge(c_in[s], 16 * GV * (i + 1))
                    after(dve, c_S, s, i, NS)
                    v.tensor_tensor(C_kl[:, s, :], C_V[:, s, :, ROW_SRC], wbase[:, ds(i * BODY + s * GV, GV)], ALU.subtract).then_inc(c_kl, 1)
                if 3 in stages:
                    t, j = stages[3]
                    after(dve, c_mg, t, j)
                    after(dve, c_p, t, j, NS)
                    ch.link(v.scalar_tensor_tensor(C_z[:, 0:GV], bank[5][:, 0:GV], -1.0, C_s[:, t, :], ALU.mult, ALU.add))
                    v.tensor_scalar(C_d[:, t, :], C_z[:, 0:GV], 0.0, None, ALU.min).then_inc(c_d, 1)
                if 1 in stages:
                    t, j = stages[1]
                    after(dve, c_pre, t, j)
                    for u in range(GV):
                        b = bank[2 + u // 2][:, (u % 2) * H1:(u % 2 + 1) * H1]
                        m = v.scalar_tensor_tensor(b, b, 0.0, w2bc[:, :], ALU.max, ALU.mult, accum_out=C_s[:, t, u:u + 1])
                        if u < GV - 1:
                            ch.do(m)
                    m.then_inc(c_sc, 1)
                    after(dve, c_sc, t, j)
                    ch.link(v.tensor_scalar(C_s[:, t, :], C_s[:, t, :], b2bc[:, :], None, ALU.add))
                    after(dve, c_nb, t, j)
                    for u in range(GV):
                        m = v.tensor_scalar(C_MK[:, t, u, :], C_MK[:, t, u, :], C_s[:, t, u:u + 1], None, ALU.add)
                        if u < GV - 1:
                            ch.do(m)
                    m.then_inc(c_MK, 1)
                if 2 in stages:
                    t, j = stages[2]
                    after(dve, c_MKt, t, j)
                    after(dve, c_mn, t, j, NS)
                    v.tensor_reduce(C_tm[:, t, :], four(bank[4], P), AX.X, ALU.max).then_inc(c_tm, 1)
                if 3 in stages:
                    t, j = stages[3]
                    r = regs(ENG.DVE, wwin, j * BODY + t * GV, N_WIN - 1)
                    after(dve, c_ag, t, j)
                    after(dve, c_cr, t, j)
                    after(dve, c_acc, t, j, 1)
                    for u in range(GV):
                        k = acc[:, ds(r[u], 1), :].rearrange("p a k -> p (a k)")
                        m = v.scalar_tensor_tensor(k, k, C_cr[:, t, u:u + 1], bank[6 + t % 2][:, u * (HID + 1):(u + 1) * (HID + 1)],
                                                   ALU.mult, ALU.add)
                        if u < GV - 1:
                            ch.link(m)
                    m.then_inc(c_acc, 1)
            run_ticks(dve, tick, ch, {3: 1 + GV - 1, 1: 2 * (GV - 1) + 1})

            dve.wait_ge(c_acc, NS * LOOPS)
            v.memset(G_T[HID:HID + 1, :, 2:4, :], 1.0).then_inc(n_ones, 1)
            ch.link(v.memset(G_mT[HID:HID + 1, :, :, :], 1.0))
            ch.link(v.tensor_scalar(has, acc[:, :, HID], 0.0, None, ALU.is_gt))
            ch.link(v.tensor_scalar(tmp_w, has, -1.0, 1.0, ALU.mult, ALU.add))
            ch.link(v.tensor_tensor(tmp_w, tmp_w, acc[:, :, HID], ALU.add))
            ch.link(v.reciprocal(rden, tmp_w))

            def update1(i):
                ch.body(i, 8 + 6)
                for s in range(2):
                    w = ds(i * 4 + s * 2, 2)
                    after2(dve, n_T, s, i, 2)
                    v.tensor_tensor(G_c[:, s, :, :], acc[:, w, :], rden[:, w].unsqueeze(2).to_broadcast([P, 2, HID + 1]),
                                    ALU.mult).then_inc(n_c, 1)
                for s in range(2):
                    w = ds(i * 4 + s * 2, 2)
                    after2(dve, n_msc, s, i, incs=2)
                    gru(i, s, n_t, n_v, n_n, G_m[:, s, :, :])
                    ch.link(v.tensor_tensor(G_e[:, s, :, :], G_d[:, s, :, :], h[:, w, :], ALU.subtract))
                    ch.link(v.tensor_tensor(G_d[:, s, :, :], G_e[:, s, :, :], has[:, w].unsqueeze(2).to_broadcast([P, 2, HID]), ALU.mult))
                    ch.link(v.tensor_tensor(G_e[:, s, :, :], G_d[:, s, :, :], h[:, w, :], ALU.add))
                    v.tensor_tensor(xs[:, w, :], xs[:, w, :], G_e[:, s, :, :], ALU.add).then_inc(n_x, 1)
                ch.end_body()
            loop(dve, G_LOOPS, update1)


_INS = ['x', 'src', 'dst', 'edge_attr_16', 'edge_type_8', 'L0_gnn_edge_matrix', 'L0_gnn_w_ih', 'L0_gnn_w_hh',
        'L0_gnn_b_ih', 'L0_gnn_b_hh', 'L1_gnn_W_att1', 'L1_gnn_b_att1', 'L1_gnn_W_att2', 'L1_gnn_b_att2',
        'L1_gnn_W_lin', 'L1_gnn_b_lin', 'L1_gnn_W_ih', 'L1_gnn_b_ih', 'L1_gnn_W_hh', 'L1_gnn_b_hh']
_OUTS = [((12500, 64), 'float32')]


def kernel(**inputs):
    import numpy as _np
    import concourse.bacc as _bacc
    from concourse import mybir as _mybir
    from concourse.bass_utils import run_bass_kernel_spmd as _run

    nc = _bacc.Bacc("TRN2", target_bir_lowering=False, num_devices=1)
    arrays, args = {}, []
    for name in _INS:
        a = _np.ascontiguousarray(inputs[name])
        arrays[f"in_{name}_dram"] = a
        args.append(nc.dram_tensor(f"in_{name}_dram", a.shape, _mybir.dt.from_np(a.dtype), kind="ExternalInput").ap())
    for i, (shape, dtype) in enumerate(_OUTS):
        dt = _mybir.dt.from_np(_np.dtype(dtype))
        args.append(nc.dram_tensor(f"out_{i}_dram", shape, dt, kind="ExternalOutput").ap())
    build(nc, *args)
    r = _run(nc, [arrays], core_ids=[0])
    return r.results[0]["out_0_dram"]
```

```python
import concourse.bass as bass
from concourse import mybir
from contextlib import ExitStack

P = 128
N_NODES = 12500
N_EDGES = 212500
HID = 64
ATTR = 16
TYPES = 8
GATES = 3 * HID
H1 = 2 * HID + ATTR
BANK = 512
N_WIN = -(-N_NODES // P)
NW = 4 * -(-N_WIN // 4)
N_KEYS = NW
LAST_NODES = N_NODES - (N_WIN - 1) * P
COLS = 1664
SLOTS = P * COLS
TILES = SLOTS // P
LAST_COLS = N_EDGES - (P - 1) * COLS
N_PAD = SLOTS - N_EDGES
PAD_KEY = N_WIN * P
GV = 4
NS = 4
BODY = GV * NS
VISITS = BODY * -(-(-(-N_EDGES // P) + N_WIN - 1) // BODY)
LOOPS = VISITS // BODY
VCHUNK = VISITS // 4
HW = N_WIN - 1
ROW_ONE = H1 + HID
ROW_SRC = ROW_ONE + 1
ROW = ROW_SRC + 1
REC = 4
BIG = float(1 << 20)
MASKED = float(1 << 100)
PARTS = 3
AT_BLOCK = P // ATTR
AT_BLOCKS = TILES // AT_BLOCK
AT_LOOPS = AT_BLOCKS // 2
EPS = 1.0e-5
SORT_COLS = 16
SORT_ROW = ATTR + 4
COUNT_LOOPS = N_KEYS // 2
PLACE_LOOPS = N_KEYS // 2
G_LOOPS = NW // 4


class Chain:

    def __init__(self, eng, sem):
        self.eng, self.sem = eng, sem
        self.base = self.k = self.i = self.per = 0

    def body(self, i, per):
        if not self.per:
            self.base += self.k
        self.i, self.per, self.k = i, per, 0

    def end_body(self):
        assert self.k == self.per, (self.k, self.per)
        self.k = 0

    def end_loop(self, n):
        self.base += n * self.per
        self.i = self.per = self.k = 0

    def do(self, ins):
        self.k += 1
        ins.then_inc(self.sem, 1)
        return self.base + self.i * self.per + self.k

    def need(self, mark):
        self.eng.wait_ge(self.sem, mark)

    def link(self, ins):
        self.need(self.do(ins))


def first(i):
    return isinstance(i, int) and i == 0


def build(nc, x, src, dst, attr, etype, edge_matrix, w_ih0, w_hh0, b_ih0, b_hh0,
          w_att1, b_att1, w_att2, b_att2, w_lin, b_lin, w_ih1, b_ih1, w_hh1, b_hh1, out):
    f32, i32, bf16, u16 = mybir.dt.float32, mybir.dt.int32, mybir.dt.bfloat16, mybir.dt.uint16
    ALU = mybir.AluOpType
    ACT = mybir.ActivationFunctionType
    AX = mybir.AxisListType
    ENG = mybir.EngineType
    ds = bass.ds
    ctx = ExitStack()

    def sb(name, shape, dt=f32):
        return ctx.enter_context(nc.sbuf_tensor(name, shape, dt))

    def sem(name):
        return ctx.enter_context(nc.semaphore(name))

    def sems(name, n):
        return [sem(f"{name}{j}") for j in range(n)]

    def dram(name, shape):
        return nc.dram_tensor(name, shape, f32, kind="Internal").ap()

    def regs(engine, tab, v, top):
        _, r = nc.values_load_multi_w_load_instructions(
            tab[0:1, ds(v, GV)], engines=(engine,), min_val=0, max_val=top,
            skip_runtime_bounds_check_because="the table's entries are bounded when it is made")
        return r

    def per_group(t, a):
        return t.unsqueeze(2).to_broadcast([P, GV, a])

    with ctx:
        table = dram("msg_table", [NW * P * TYPES, HID])
        recA = dram("rec0_by_dst", [SLOTS, 2])
        recB = dram("rec1_by_dst", [SLOTS, REC])
        attr_d = dram("attr_by_dst", [SLOTS, ATTR])
        attrT_d = dram("attr_turned", [TILES * ATTR, P])
        p_d = dram("src_part", [P, NW * H1])
        rows_d = dram("rows_by_src", [SLOTS, ROW])

        sorted_d = dram("edges_by_dst", [SLOTS, SORT_ROW])

        xs = sb("xs", [P, NW, HID])
        h = sb("h", [P, NW, HID])
        acc = sb("acc", [P, NW, HID + 1])
        big = sb("big", [P, NW * H1])
        wbase_all = sb("wbase", [P, 1 + VISITS])
        wbase = wbase_all[:, 1:1 + VISITS]
        wwin = sb("wwin", [1, VISITS], i32)
        wtile = sb("wtile", [1, VISITS], i32)
        RING = 9980
        ring = sb("ring", [P, RING])
        ident = sb("ident", [P, P])
        iota = sb("iota", [P, P])
        ones = sb("ones", [P, P])
        tri = sb("tri", [P, P])
        cnt = sb("cnt", [P, N_KEYS])
        place0 = sb("place0", [P, N_KEYS])
        small = sb("small", [P, 512])
        zeros = sb("zeros", [P, 3 * ATTR])
        AT = sb("AT", [HID, TYPES * HID])
        wih0T = sb("wih0T", [HID + 1, GATES])
        whh0T = sb("whh0T", [HID + 1, GATES])
        wih1T = sb("wih1T", [HID + 1, GATES])
        whh1T = sb("whh1T", [HID + 1, GATES])
        wlinT = sb("wlinT", [HID + 1, HID])
        waT = sb("waT", [HID + 1, H1])
        wbT = sb("wbT", [HID + 1, H1])
        wattr = sb("wattr", [ATTR, H1])
        iota_b = sb("iota_b", [P, P], bf16)
        ident_b = sb("ident_b", [P, P], bf16)
        big_b = sb("big_b", [P, P], bf16)
        sel_a = sb("sel_a", [PARTS * GV, GV])
        sel = sb("sel", [PARTS * GV, GV * P], bf16)
        w2bc = sb("w2bc", [P, H1])
        b2bc = sb("b2bc", [P, 1])
        eps_t = sb("eps_t", [P, 1])
        cc = [sb(f"cc{k}", [P, 1]) for k in range(2)]
        nt = sb("nt", [P, 1])
        off = sb("off", [P, 1])
        dbc = sb("dbc", [P, P])
        unsorted = sb("unsorted", [1, 1], i32)
        before = sb("before", [P, 1], i32)
        out_of_order = sb("out_of_order", [P, 1])

        at = [0]

        def part(t, n, limit):
            at[0] += n
            assert at[0] <= limit, at[0]
            return t[:, at[0] - n:at[0]]

        dst_i = part(big, COLS, NW * H1).bitcast(i32)
        src_i = part(big, COLS, NW * H1).bitcast(i32)
        kB_flat = part(big, REC * COLS, NW * H1)
        kB = kB_flat.rearrange("p (c k) -> p c k", k=REC)
        kA_flat = kB_flat[:, 0:2 * COLS]
        kA = kA_flat.rearrange("p (c k) -> p c k", k=2)
        typ_i = kB_flat[:, 2 * COLS:3 * COLS].bitcast(i32)
        win = part(big, COLS // 2, NW * H1).bitcast(bf16)
        mask = part(big, COLS // 2, NW * H1).bitcast(bf16)
        scan = part(big, COLS, NW * H1)
        q_tab = big[:, :].rearrange("p (w j) -> p w j", j=H1)
        p_tab = q_tab

        iota_v = ring[:, 0:VISITS]
        vmask = ring[:, VISITS:2 * VISITS]
        t0 = 2 * VISITS
        t_hT = ring[0:HID, t0:t0 + 2 * P].rearrange("p (s n) -> p s n", s=2)
        t_out = ring[:, t0 + 2 * P:t0 + 2 * P + 2 * BANK].rearrange("p (s n) -> p s n", s=2)

        d_place = kB_flat[:, 3 * COLS:4 * COLS]
        d_rows = ring[:, 6000:6000 + SORT_COLS * SORT_ROW].rearrange("p (c k) -> p c k", k=SORT_ROW)
        d_pos = ring[:, 6400:6400 + SORT_COLS].bitcast(i32)

        def groups(t, n, k):
            return part(t, n * GV * k, RING).rearrange("p (s u k) -> p s u k", s=n, u=GV)

        def marks(n=NS):
            return part(ring, n * GV, RING).rearrange("p (s u) -> p s u", s=n)

        def onehots():
            return part(ring, NS * GV * P // 2, RING).bitcast(bf16).rearrange("p (s u k) -> p s u k", s=NS, u=GV)

        t_h1 = ring[:, t0 + 2 * P + 2 * BANK:t0 + 3 * P + 2 * BANK].rearrange("p (s n) -> p s n", s=2)

        at[0] = 0
        A_D = groups(ring, NS, P)
        A_g = groups(ring, NS, HID)
        A_rec = groups(ring, NS, 2)
        A_kl = marks()
        A_at = part(ring, 2 * P, RING).rearrange("p (j n) -> p j n", j=2)
        A_atT = part(ring, 2 * P, RING).rearrange("p (j n) -> p j n", j=2)

        at[0] = 0
        B_D = onehots()
        B_DT = groups(ring, NS, P)
        B_row = groups(ring, NS, ROW)
        B_rec = groups(ring, NS, REC)
        B_kl, B_ge, B_in, B_sh = marks(), marks(), marks(), marks()
        B_pos = marks().bitcast(i32)
        B_at = groups(ring, NS, P)[0:ATTR]
        padrows = part(ring, 3 * ROW, RING).rearrange("p (a k) -> p a k", k=ROW)

        at[0] = 0
        C_N = onehots()
        C_S = groups(ring, NS, P)
        C_ST = groups(ring, NS, P)
        C_V = groups(ring, NS, ROW)
        C_W = groups(ring, 2, HID + 1)
        C_pre = part(ring, GV * H1, RING).rearrange("p (u k) -> p u k", u=GV)
        C_parts = part(ring, NS * PARTS * GV // 2, RING).bitcast(bf16).rearrange("p (s k) -> p s k", s=NS)
        C_PT = part(ring, P, RING)[0:PARTS * GV].bitcast(bf16).rearrange("p (s n) -> p s n", s=2)
        C_kl, C_raw, C_s, C_r, C_tm, C_pen, C_mo, C_df, C_cr, C_z, C_d, C_p = (marks() for _ in range(12))
        C_mn = part(ring, 1 + NS * GV, RING)

        spare = acc[:, :, :].rearrange("p w k -> p (w k)")
        at[0] = 0
        P_in = part(spare, 4 * HID, NW * HID).rearrange("p (s u k) -> p s u k", s=2, u=2)
        P_hT = part(spare, 4 * P, NW * HID)[0:HID + 1].rearrange("p (s u k) -> p s u k", s=2, u=2)
        P_out = part(spare, 4 * H1, NW * HID).rearrange("p (s u k) -> p s u k", s=2, u=2)

        at[0] = 0
        G_T = part(ring, 8 * P, RING)[0:HID + 1, :].rearrange("p (s u n) -> p s u n", s=2, u=4)
        G_mT = part(ring, 4 * P, RING)[0:HID + 1, :].rearrange("p (s u n) -> p s u n", s=2, u=2)

        def pairs(n):
            return part(ring, 4 * n, RING).rearrange("p (s u n) -> p s u n", s=2, u=2)

        G_t = pairs(2 * HID)
        G_n, G_u, G_v, G_d, G_e, G_m = (pairs(HID) for _ in range(6))
        G_c = pairs(HID + 1)
        G_in = part(ring, 8 * HID, RING).rearrange("p (s u n) -> p s u n", s=2, u=4)
        has = part(ring, NW, RING)
        rden = part(ring, NW, RING)
        tmp_w = part(ring, NW, RING)

        bank = [ctx.enter_context(nc.psum_tensor(f"bank{j}", [P, BANK], f32)) for j in range(8)]

        bank_b = [b[:, :].bitcast(bf16) for b in bank]

        def four(b, k):
            return b[:, 0:4 * k].rearrange("p (u k) -> p u k", u=4)

        def two(b, k):
            return b[:, 0:2 * k].rearrange("p (u k) -> p u k", u=2)

        block = ctx.enter_context(nc.Block())

        own = {e: sem(f"{e}_step") for e in ("dve", "pool")}
        turns = {e: sem(f"{e}_turns") for e in ("dve", "pool", "pe")}
        s_const, s_padded, s_ids, s_x, s_w, s_attr = (sem(f"s_{k}") for k in ("const", "padded", "ids", "x", "w", "attr"))
        s_wT, s_wcopied = sem("s_wT"), sem("s_wcopied")
        s_var, s_std, s_h = sem("s_var"), sem("s_std"), sem("s_h")
        s_kA, s_recA, s_kB, s_recB = sem("s_kA"), sem("s_recA"), sem("s_kB"), sem("s_recB")
        s_iotav = sem("s_iotav")
        s_cnt, s_tot, s_cc, s_start, s_nt, s_vstart, s_off, s_shift, s_vmask, s_vsum, s_vtab = (
            sem(f"s_{k}") for k in ("cnt", "tot", "cc", "start", "nt", "vstart", "off", "shift", "vmask", "vsum", "vtab"))
        s_before, s_flagp, s_flag = sem("s_before"), sem("s_flagp"), sem("s_flag")
        d_step, d_attr, d_ready, d_sc, d_free, d_sent, d_back, d_ids = (
            sem(f"d_{k}") for k in ("step", "attr", "ready", "sc", "free", "sent", "back", "ids"))
        t_st, a_rec, a_g = sems("t_st", 2), sems("a_rec", NS), sems("a_g", NS)
        b_in, b_sc, c_in = sems("b_in", NS), sems("b_sc", NS), sems("c_in", NS)
        at_in, at_st = sems("at_in", 2), sems("at_st", 2)
        at_T, at_cp, s_constb = sem("at_T"), sem("at_cp"), sem("s_constb")
        p_h, p_ones, p_T, p_Tc, p_mm, p_q, p_p, p_back = (sem(f"p_{k}") for k in ("h", "ones", "T", "Tc", "mm", "q", "p", "back"))
        p_st = sems("p_st", 2)
        t_h, t_T, t_Tc, t_mm, t_cp = (sem(f"t_{k}") for k in ("h", "T", "Tc", "mm", "cp"))
        g_in, n_in = sem("g0_in"), sem("g1_in")
        a_D, a_mm = sem("a_D"), sem("a_mm")
        a_acc, a_zero, a_done = sem("a_acc"), sem("a_zero"), sem("a_done")
        b_kl, b_D, b_pos, b_DT, b_DTc, b_hr, b_row = (sem(f"b_{k}") for k in ("kl", "D", "pos", "DT", "DTc", "hr", "row"))
        b_pad, b_padout, b_sent = sem("b_pad"), sem("b_padout"), sem("b_sent")
        c_N, c_kl, c_S, c_St, c_STc, c_pre, c_sp, c_pt, c_pc, c_MKt, c_df, c_cr, c_mg, c_d, c_p, c_W, c_ag, c_acc = (
            sem(f"c_{k}") for k in ("N", "kl", "S", "St", "STc", "pre", "sp", "pt", "pc", "MKt", "df", "cr", "mg", "d", "p", "W", "ag", "acc"))
        c_init = sem("c_init")
        g_T, g_Tc, g_mm, g_t, g_v, g_n, g_x = (sem(f"g0_{k}") for k in ("T", "Tc", "mm", "t", "v", "n", "x"))
        n_c, n_T, n_Tc, n_ms, n_msc, n_mm, n_t, n_v, n_n, n_x = (
            sem(f"g1_{k}") for k in ("c", "T", "Tc", "ms", "msc", "mm", "t", "v", "n", "x"))
        g_ones, n_ones, s_final = sem("g_ones"), sem("n_ones"), sem("s_final")
        N_CONST = 6
        N_CONSTB = 5

        def turn(eng, name):
            eng.sem_inc(turns[name], 1)

        jobs = []
        em = edge_matrix.rearrange("t (m k) -> (t m) k", k=HID)
        for w, wT in ((em, AT), (w_ih0, wih0T), (w_hh0, whh0T), (w_lin, wlinT), (w_ih1, wih1T),
                      (w_hh1, whh1T), (w_att1[:, 0:HID], waT), (w_att1[:, HID:HID + ATTR], wattr),
                      (w_att1[:, HID + ATTR:H1], wbT)):
            n, c = w.shape
            for r in range(0, n, P):
                m = min(P, n - r)
                jobs.append((w[r:r + m, :], m, c, wT[0:c, r:r + m]))
        biases = [(b_ih0, wih0T), (b_hh0, whh0T), (b_lin, wlinT), (b_ih1, wih1T), (b_hh1, whh1T), (b_att1, waT)]
        WR = HID
        raw = [ring[0:m, WR * j:WR * j + c] for j, (_, m, c, _) in enumerate(jobs)]
        N_WDMA = len(jobs) + len(biases) + 2

        recA_t = recA.rearrange("(t p) k -> t p k", p=P)
        recB_t = recB.rearrange("(t p) k -> t p k", p=P)
        attrT_t = attrT_d.rearrange("(t k) p -> t k p", k=ATTR)
        rows_t = rows_d.rearrange("(t p) k -> t p k", p=P)

        def tile_of(t, r):
            return t[ds(r, 1), :, :].rearrange("a p k -> (a p) k")

        def run_ticks(eng, tick, depth, ch=None, per=0):
            def body(i, slots, alive):
                for s in slots:
                    tick(i, s, {k: ((s - k) % NS, i if s >= k else i - 1) for k in range(depth) if alive(s, k)})

            def straight(i, slots, alive):
                body(i, slots, alive)
                if ch:
                    ch.base, ch.k = ch.base + ch.k, 0
            straight(0, range(NS), lambda s, k: s >= k)
            straight(1, range(NS), lambda s, k: True)
            if ch:
                ch.base -= 2 * per
            with eng.Fori(2, LOOPS) as i:
                if ch:
                    ch.body(i, per)
                body(i, range(NS), lambda s, k: True)
                if ch:
                    ch.end_body()
            if ch:
                ch.end_loop(LOOPS)
            straight(LOOPS, range(depth - 1), lambda s, k: s < k)

        def loop(eng, n, body, start=0):
            if start == 0:
                body(0)
                start = 1
            with eng.Fori(start, n) as i:
                body(i)

        def after(eng, s, t, j, back=0, slots=NS, incs=1):
            v = j * slots + (t + 1 - back)
            if not (isinstance(v, int) and v < 1):
                eng.wait_ge(s, v * incs)

        def after2(eng, s, t, j, back=0, incs=1):
            after(eng, s, t, j, back, 2, incs)

        @block.sync
        def _(sp):
            sp.wait_ge(s_padded, 5)
            for v, t in ((dst, dst_i), (src, src_i), (etype, typ_i)):
                sp.dma_start(t[0:P - 1, :], v[0:(P - 1) * COLS].rearrange("(p c) -> p c", c=COLS)).then_inc(s_ids, 16)
                sp.dma_start(t[P - 1:P, 0:LAST_COLS],
                             v[(P - 1) * COLS:N_EDGES].rearrange("(a c) -> a c", a=1)).then_inc(s_ids, 16)
            ends = dst[0:(P - 1) * COLS].rearrange("(p c) -> p c", c=COLS)[:, COLS - 1:COLS]
            sp.dma_start(before[1:P, :], ends, allow_slow_non_contiguous=True).then_inc(s_before, 16)
            whole = (N_WIN - 1) * P
            sp.dma_start(xs[:, 0:N_WIN - 1, :], x[0:whole, :].rearrange("(w p) f -> p w f", p=P)).then_inc(s_x, 16)
            sp.dma_start(xs[0:LAST_NODES, N_WIN - 1, :], x[whole:N_NODES, :]).then_inc(s_x, 16)
            for (w, _, _, _), r in zip(jobs, raw):
                sp.dma_start(r, w).then_inc(s_w, 16)
            for b, t in biases:
                sp.dma_start(t[HID:HID + 1, :], b.rearrange("(a n) -> a n", a=1)).then_inc(s_w, 16)
            sp.dma_start(w2bc[:, :], w_att2[0:1, :].to_broadcast([P, H1])).then_inc(s_w, 16)
            sp.dma_start(b2bc[:, :], b_att2.rearrange("(a n) -> a n", a=1).to_broadcast([P, 1])).then_inc(s_w, 16)
            sp.dma_start(attr_d[0:N_EDGES, :].rearrange("(a b) k -> a (b k)", a=500),
                         attr.rearrange("(a b) k -> a (b k)", a=500)).then_inc(s_attr, 16)
            sp.wait_ge(s_const, N_CONST)
            sp.dma_start(attr_d[N_EDGES:N_EDGES + 3 * P, :].rearrange("(p a) k -> p (a k)", a=3), zeros[:, :]).then_inc(s_attr, 16)
            sp.dma_start(attr_d[N_EDGES + 3 * P:SLOTS, :], zeros[0:N_PAD - 3 * P, 0:ATTR]).then_inc(s_attr, 16)
            table_w = table.rearrange("(w p t) m -> w p (t m)", p=P, t=TYPES)

            def store_table(i):
                for s in range(2):
                    after2(sp, t_cp, s, i)
                    sp.dma_start(tile_of(table_w, i * 2 + s), t_out[:, s, :]).then_inc(t_st[s], 16)
            loop(sp, NW // 2, store_table)

            sp.wait_ge(s_flag, 1)
            flag = sp.value_load(unsorted[0:1, 0:1], min_val=0, max_val=N_EDGES)
            with sp.If(flag > 0):
                sp.wait_ge(s_attr, 48)
                attr_p = attr_d.rearrange("(p c) k -> p c k", p=P)

                def load_attr(i):
                    if not first(i):
                        sp.wait_ge(d_free, i)
                    sp.dma_start(d_rows[:, :, 0:ATTR], attr_p[:, ds(i * SORT_COLS, SORT_COLS), :]).then_inc(d_attr, 16)
                loop(sp, COLS // SORT_COLS, load_attr)
                sp.wait_ge(d_sent, 1)
                sp.dma_start(attr_d[:, :], sorted_d[:, 0:ATTR]).then_inc(d_back, 16)
                sp.dma_start(kB, sorted_d.rearrange("(p c) k -> p c k", p=P)[:, :, ATTR:SORT_ROW]).then_inc(d_ids, 16)
                sp.wait_ge(d_back, 16)

            sp.wait_ge(s_kA, 2)
            sp.dma_start(recA.rearrange("(p c) k -> p (c k)", p=P), kA_flat).then_inc(s_recA, 16)

            sp.wait_ge(s_recA, 16)
            sp.wait_ge(s_vtab, 1)

            def load_recA(i):
                for s in range(NS):
                    r = regs(ENG.SP, wtile, i * BODY + s * GV, TILES - 1)
                    after(sp, a_mm, s, i, NS)
                    for u in range(GV):
                        sp.dma_start(A_rec[:, s, u, :], tile_of(recA_t, r[u])).then_inc(a_rec[s], 16)
            loop(sp, LOOPS, load_recA)

            def store_p(i):
                for s in range(2):
                    after2(sp, p_p, s, i)
                    sp.dma_start(p_d[:, ds((i * 2 + s) * 2 * H1, 2 * H1)], P_out[:, s, :, :].rearrange("p u k -> p (u k)")).then_inc(p_st[s], 16)

            sp.wait_ge(s_kB, 1)
            sp.dma_start(recB.rearrange("(p c) k -> p (c k)", p=P), kB_flat).then_inc(s_recB, 16)
            sp.wait_ge(b_pad, 3)
            sp.dma_start(rows_d[N_EDGES:N_EDGES + 3 * P, :].rearrange("(p a) k -> p (a k)", a=3),
                         padrows.rearrange("p a k -> p (a k)")).then_inc(b_padout, 16)
            sp.dma_start(rows_d[N_EDGES + 3 * P:SLOTS, :], padrows[0:N_PAD - 3 * P, 0, :]).then_inc(b_padout, 16)
            loop(sp, G_LOOPS, store_p)
            sp.wait_ge(s_recB, 16)
            for j in range(2):
                sp.wait_ge(at_st[j], 16 * AT_LOOPS)

            def load_recB(i):
                for s in range(NS):
                    r = regs(ENG.SP, wtile, i * BODY + s * GV, TILES - 1)
                    if not first(i):
                        sp.wait_ge(b_sc[s], 16 * GV * i)
                    for u in range(GV):
                        sp.dma_start(B_rec[:, s, u, :], tile_of(recB_t, r[u])).then_inc(b_in[s], 16)
                        sp.dma_start(B_at[:, s, u, :], tile_of(attrT_t, r[u])).then_inc(b_in[s], 16)
            loop(sp, LOOPS, load_recB)

            sp.wait_ge(b_sent, 1)
            sp.wait_ge(b_padout, 32)
            for s in range(2):
                sp.wait_ge(p_st[s], 16 * G_LOOPS)
            sp.dma_start(big[:, :], p_d[:, :]).then_inc(p_back, 16)
            sp.wait_ge(s_vtab, 2)

            def load_rows(i):
                for s in range(NS):
                    r = regs(ENG.SP, wtile, i * BODY + s * GV, TILES - 1)
                    after(sp, c_W, s, i, NS)
                    for u in range(GV):
                        sp.dma_start(C_V[:, s, u, :], tile_of(rows_t, r[u])).then_inc(c_in[s], 16)
            loop(sp, LOOPS, load_rows)

            sp.wait_ge(n_x, 2 * G_LOOPS)
            sp.dma_start(out[0:whole, :].rearrange("(w p) f -> p w f", p=P), xs[:, 0:N_WIN - 1, :]).then_inc(s_final, 16)
            sp.dma_start(out[whole:N_NODES, :], xs[0:LAST_NODES, N_WIN - 1, :]).then_inc(s_final, 16)
            sp.wait_ge(s_final, 32)

        @block.gpsimd
        def _(pool):
            g = nc.gpsimd
            ch = Chain(pool, own["pool"])
            g.memset(zeros[:, :], 0.0).then_inc(s_const, 1)
            g.memset(ones[:, :], 1.0).then_inc(s_const, 1)
            ch.link(g.memset(ident[:, :], 0.0))
            g.memset(eps_t[:, :], EPS).then_inc(s_const, 1)
            g.iota(iota[:, :], pattern=[[1, P]], base=0, channel_multiplier=0,
                   allow_small_or_imprecise_dtypes=True).then_inc(s_const, 1)
            g.affine_select(out=ident[:, :], in_=ident[:, :], compare_op=ALU.not_equal, fill=1.0, base=0,
                            pattern=[[-1, P]], channel_multiplier=1).then_inc(s_const, 1)
            pool.wait_ge(s_const, 2)
            g.affine_select(out=tri[:, :], in_=ones[:, :], compare_op=ALU.is_gt, fill=0.0, base=0,
                            pattern=[[1, P]], channel_multiplier=-1).then_inc(s_const, 1)
            pool.wait_ge(s_wcopied, len(jobs))
            g.iota(iota_v, pattern=[[1, VISITS]], base=0, channel_multiplier=0,
                   allow_small_or_imprecise_dtypes=True).then_inc(s_iotav, 1)

            pool.wait_ge(s_h, 1)

            def copy_h(i):
                for s in range(2):
                    after2(pool, t_T, s, i, 2)
                    turn(pool, "pool")
                    g.tensor_copy(t_h1[:, s, :], h[:, ds(i * 2 + s, 1), :].rearrange("p a k -> p (a k)")).then_inc(t_h, 1)
            loop(pool, NW // 2, copy_h)

            pool.wait_ge(s_flag, 1)
            flag = pool.value_load(unsorted[0:1, 0:1], min_val=0, max_val=N_EDGES)
            with pool.If(flag > 0):
                def scatter(i):
                    pool.wait_ge(d_attr, 16 * (i + 1))
                    pool.wait_ge(d_ready, i + 1)
                    turn(pool, "pool")
                    for c in range(SORT_COLS):
                        g.indirect_dma_start(
                            out=sorted_d[:, :], out_offset=bass.IndirectOffsetOnAxis(ap=d_pos[:, c:c + 1], axis=0),
                            in_=d_rows[:, c, :], in_offset=None).then_inc(d_sc, 16)
                    pool.wait_ge(d_sc, 16 * SORT_COLS * (i + 1))
                    pool.sem_inc(d_free, 1)
                loop(pool, COLS // SORT_COLS, scatter)
                pool.wait_ge(d_free, COLS // SORT_COLS)
                pool.sem_inc(d_sent, 1)

            for s in range(2):
                pool.wait_ge(t_st[s], 16 * (NW // 2))
            pool.wait_ge(s_vtab, 1)

            def gather(i):
                for s in range(NS):
                    after(pool, a_mm, s, i, NS)
                    pool.wait_ge(a_rec[s], 16 * GV * (i + 1))
                    turn(pool, "pool")
                    for u in range(GV):
                        g.indirect_dma_start(
                            out=A_g[:, s, u, :], out_offset=None, in_=table[:, :],
                            in_offset=bass.IndirectOffsetOnAxis(ap=A_rec[:, s, u, 1:2].bitcast(i32), axis=0)).then_inc(a_g[s], 16)
            loop(pool, LOOPS, gather)

            pool.wait_ge(a_done, 1)
            pool.wait_ge(g_ones, 1)

            def copy_in(i):
                for s in range(2):
                    w = ds(i * 4 + s * 2, 2)
                    after2(pool, g_T, s, i, 2)
                    turn(pool, "pool")
                    g.tensor_copy(G_in[:, s, 0:2, :], acc[:, w, 0:HID]).then_inc(g_in, 1)
                    g.tensor_copy(G_in[:, s, 2:4, :], h[:, w, :]).then_inc(g_in, 1)
            loop(pool, G_LOOPS, copy_in)

            pool.wait_ge(s_h, 2)

            def copy_h2(i):
                for s in range(2):
                    after2(pool, p_T, s, i, 2)
                    turn(pool, "pool")
                    g.tensor_copy(P_in[:, s, :, :], h[:, ds(i * 4 + s * 2, 2), :]).then_inc(p_h, 1)
            loop(pool, G_LOOPS, copy_h2)

            pool.wait_ge(b_padout, 32)

            def send(i):
                for s in range(NS):
                    after(pool, b_row, s, i, incs=2)
                    after(pool, b_pos, s, i, incs=2)
                    turn(pool, "pool")
                    for u in range(GV):
                        g.indirect_dma_start(
                            out=rows_d[:, :], out_offset=bass.IndirectOffsetOnAxis(ap=B_pos[:, s, u:u + 1], axis=0),
                            in_=B_row[:, s, u, :], in_offset=None, bounds_check=SLOTS - 1, oob_is_err=False).then_inc(b_sc[s], 16)
            loop(pool, LOOPS, send)
            for s in range(NS):
                pool.wait_ge(b_sc[s], 16 * GV * LOOPS)
            g.iota(iota_v, pattern=[[1, VISITS]], base=0, channel_multiplier=0,
                   allow_small_or_imprecise_dtypes=True).then_inc(s_iotav, 1)
            pool.sem_inc(b_sent, 1)

            def tick(i, s, stages):
                if 3 in stages:
                    t, j = stages[3]
                    after(pool, c_p, t, j)
                    after(pool, c_ag, t, j, 2)
                    g.tensor_tensor(C_W[:, t % 2, :, :], C_V[:, t, :, H1:ROW_SRC],
                                    per_group(C_p[:, t, :], HID + 1), ALU.mult).then_inc(c_W, 1)
            run_ticks(pool, tick, 5)

            pool.wait_ge(n_ones, 1)

            def copy_h1(i):
                for s in range(2):
                    after2(pool, n_T, s, i, 2)
                    turn(pool, "pool")
                    g.tensor_copy(G_in[:, s, 2:4, :], h[:, ds(i * 4 + s * 2, 2), :]).then_inc(n_in, 1)
            loop(pool, G_LOOPS, copy_h1)

        @block.scalar
        def _(act):
            a = nc.scalar
            act.wait_ge(s_wT, len(jobs))
            for j, (_, m, c, wT) in enumerate(jobs):
                a.copy(wT, bank[j // 4][0:c, (j % 4) * P:(j % 4) * P + m]).then_inc(s_wcopied, 1)
            act.wait_ge(s_const, N_CONST)
            act.wait_ge(s_var, 1)
            a.activation(small[:, NW:2 * NW], small[:, 0:NW], ACT.Sqrt, bias=eps_t[:, :]).then_inc(s_std, 1)

            def table_copies(i):
                for s in range(2):
                    after2(act, t_T, s, i)
                    after2(act, t_mm, s, i, 2)
                    a.copy(t_hT[:, s, :], bank[s][0:HID, 0:P]).then_inc(t_Tc, 1)
                    after2(act, t_mm, s, i)
                    if not first(i):
                        act.wait_ge(t_st[s], 16 * i)
                    a.copy(t_out[:, s, :], bank[2 + s][:, :]).then_inc(t_cp, 1)
            loop(act, NW // 2, table_copies)

            act.wait_ge(s_attr, 48)
            act.wait_ge(s_recA, 16)
            act.wait_ge(s_vtab, 1)
            at_src = attr_d.rearrange("(b t p) k -> b p t k", t=AT_BLOCK, p=P)
            at_dst = attrT_d.rearrange("(b q) p -> b q p", q=P)

            def load_block(i):
                for j in range(2):
                    after2(act, at_T, j, i, 2)
                    act.dma_start(A_at[:, j, :].rearrange("p (t k) -> p t k", k=ATTR),
                                  at_src[ds(i * 2 + j, 1)].rearrange("a p t k -> (a p) t k")).then_inc(at_in[j], 16)

            def turn_block(i):
                for j in range(2):
                    after2(act, at_T, j, i)
                    if not first(i):
                        act.wait_ge(at_st[j], 16 * i)
                    a.copy(A_atT[:, j, :], bank[6 + j][:, 0:P]).then_inc(at_cp, 1)
                for j in range(2):
                    after2(act, at_cp, j, i)
                    act.dma_start(tile_of(at_dst, i * 2 + j), A_atT[:, j, :]).then_inc(at_st[j], 16)

            def at_body(i):
                load_block(i)
                turn_block(i)
            loop(act, AT_LOOPS, at_body)

            act.wait_ge(g_ones, 1)

            def update0(i):
                for s in range(2):
                    after2(act, g_T, s, i)
                    after2(act, g_mm, s, i, 2)
                    a.copy(G_T[0:HID, s, :, :], four(bank[s], P)[0:HID]).then_inc(g_Tc, 1)
                    after2(act, g_mm, s, i)
                    after2(act, g_x, s, i, 2)
                    a.activation(G_t[:, s, :, :], two(bank[2 + s], 4 * HID)[:, :, 0:2 * HID], ACT.Tanh, scale=0.5).then_inc(g_t, 1)
                    after2(act, g_v, s, i)
                    a.activation(G_n[:, s, :, :], G_v[:, s, :, :], ACT.Tanh).then_inc(g_n, 1)
            loop(act, G_LOOPS, update0)
            act.wait_ge(s_var, 2)
            a.activation(small[:, NW:2 * NW], small[:, 0:NW], ACT.Sqrt, bias=eps_t[:, :]).then_inc(s_std, 1)

            act.wait_ge(s_recB, 16)
            act.wait_ge(p_ones, 1)

            def tables1(i):
                for s in range(2):
                    after2(act, p_T, s, i)
                    after2(act, p_mm, s, i, 2)
                    a.copy(P_hT[0:HID, s, :, :], two(bank[s], P)[0:HID]).then_inc(p_Tc, 1)
                    after2(act, p_mm, s, i)
                    a.copy(q_tab[:, ds(i * 4 + s * 2, 2), :], two(bank[4 + s], H1)).then_inc(p_q, 1)
            loop(act, G_LOOPS, tables1)

            act.wait_ge(b_pad, 3)

            def rows(i, s, stages):
                if 0 in stages:
                    after(act, b_DT, s, i)
                    after(act, b_hr, s, i, NS)
                    a.copy(B_DT[:, s, :, :], four(bank_b[s % 2], P)).then_inc(b_DTc, 1)
                if 1 in stages:
                    t, j = stages[1]
                    after(act, b_hr, t, j)
                    if not first(j):
                        act.wait_ge(b_sc[t], 16 * GV * j)
                    for half in range(2):
                        a.copy(B_row[:, t, 2 * half:2 * half + 2, 0:ROW_ONE],
                               two(bank[2 + 2 * (t % 2) + half], ROW_ONE)).then_inc(b_row, 1)
            run_ticks(act, rows, 2)

            act.wait_ge(s_vtab, 2)

            def tick(i, s, stages):
                if 0 in stages:
                    after(act, c_St, s, i)
                    after(act, c_mg, s, i, NS)
                    a.activation(C_ST[:, s, :, :], four(bank_b[0], P), ACT.Identity, bias=ones[:, 0:1], scale=-1.0).then_inc(c_STc, 1)
                if 2 in stages:
                    t, j = stages[2]
                    after(act, c_pt, t, j)
                    after(act, c_MKt, t, j, 2)
                    a.copy(C_PT[:, t % 2, :], bank_b[1][0:PARTS * GV, 0:P]).then_inc(c_pc, 1)
                if 3 in stages:
                    t, j = stages[3]
                    after(act, c_d, t, j)
                    after(act, c_W, t, j, NS)
                    a.activation(C_p[:, t, :], C_d[:, t, :], ACT.Exp).then_inc(c_p, 1)
                if 2 in stages:
                    t, j = stages[2]
                    after(act, c_df, t, j)
                    after(act, c_acc, t, j, NS)
                    a.activation(C_cr[:, t, :], C_df[:, t, :], ACT.Exp).then_inc(c_cr, 1)
            run_ticks(act, tick, 5)

            act.wait_ge(n_ones, 1)

            def update1(i):
                for s in range(2):
                    after2(act, n_T, s, i)
                    after2(act, n_mm, s, i, 2)
                    a.copy(G_T[0:HID + 1, s, 0:2, :], four(bank[s], P)[0:HID + 1, 0:2]).then_inc(n_Tc, 1)
                    a.copy(G_T[0:HID, s, 2:4, :], four(bank[s], P)[0:HID, 2:4]).then_inc(n_Tc, 1)
                    after2(act, n_ms, s, i)
                    after2(act, n_x, s, i, 2)
                    a.copy(G_m[:, s, :, :], two(bank[4 + s], HID)).then_inc(n_msc, 1)
                    a.copy(G_mT[0:HID, s, :, :], two(bank[4 + s][:, 2 * P:4 * P], P)[0:HID]).then_inc(n_msc, 1)
                    after2(act, n_mm, s, i)
                    a.activation(G_t[:, s, :, :], two(bank[2 + s], 4 * HID)[:, :, 0:2 * HID], ACT.Tanh, scale=0.5).then_inc(n_t, 1)
                    after2(act, n_v, s, i)
                    a.activation(G_n[:, s, :, :], G_v[:, s, :, :], ACT.Tanh).then_inc(n_n, 1)
            loop(act, G_LOOPS, update1)

        @block.tensor
        def _(pe):
            mm = nc.tensor.matmul
            tr = nc.tensor.transpose
            pe.wait_ge(s_const, N_CONST)
            pe.wait_ge(s_w, 16 * N_WDMA)
            for j, ((_, m, c, _), r) in enumerate(zip(jobs, raw)):
                tr(bank[j // 4][0:c, (j % 4) * P:(j % 4) * P + m], r, ident[0:m, 0:m]).then_inc(s_wT, 1)

            pe.wait_ge(s_wcopied, len(jobs))
            pe.wait_ge(s_h, 1)

            def make_table(i):
                for s in range(2):
                    after2(pe, t_Tc, s, i, 2)
                    after2(pe, t_h, s, i)
                    turn(pe, "pe")
                    tr(bank[s][0:HID, 0:P], t_h1[:, s, :], ident[:, :]).then_inc(t_T, 1)
                for s in range(2):
                    after2(pe, t_Tc, s, i)
                    after2(pe, t_cp, s, i, 2)
                    mm(bank[2 + s][:, :], t_hT[:, s, :], AT[:, :], start=True, stop=True).then_inc(t_mm, 1)
            loop(pe, NW // 2, make_table)

            def visit_counts(k):
                pe.wait_ge(s_cnt, k + 1)
                mm(bank[4][:, 0:N_KEYS], ones[:, :], cnt[:, :], start=True, stop=True)
                mm(bank[4][:, P:P + N_KEYS], tri[:, :], cnt[:, :], start=True, stop=True)
                if k == 0:
                    pe.wait_ge(s_flagp, 1)
                    mm(bank[4][0:1, 3 * P:3 * P + 1], out_of_order[:, :], ones[:, 0:1], start=True, stop=True)
                mm(bank[4][0:N_KEYS, 2 * P:2 * P + 1], cnt[:, :], ones[:, 0:1], start=True, stop=True).then_inc(s_tot, 1)

            def visit_tables(k):
                K = N_KEYS
                pe.wait_ge(s_cc, k + 1)
                mm(bank[5][0:K, 0:1], tri[0:K, 0:K], cc[k][0:K, :], start=True, stop=True).then_inc(s_start, 1)
                pe.wait_ge(s_nt, k + 1)
                mm(bank[5][0:K, 1:2], tri[0:K, 0:K], nt[0:K, :], start=True, stop=True).then_inc(s_vstart, 1)
                pe.wait_ge(s_off, k + 1)
                mm(bank[5][0:HW, 2:3], ident[0:N_WIN, 1:N_WIN], off[0:N_WIN, :], start=True, stop=True).then_inc(s_shift, 1)
                pe.wait_ge(s_vmask, k + 1)
                for q in range(4):
                    m = vmask[0:HW, q * VCHUNK:(q + 1) * VCHUNK]
                    mm(bank[q][:, 0:VCHUNK], ones[0:HW, :], m, start=True, stop=True)
                    last = mm(bank[4 + q][:, 0:VCHUNK], dbc[0:HW, :], m, start=True, stop=True)
                last.then_inc(s_vsum, 1)

            pe.wait_ge(t_cp, NW)
            visit_counts(0)
            visit_tables(0)

            pe.wait_ge(s_vtab, 1)
            pe.wait_ge(a_zero, 1)

            def sums0(i):
                for s in range(NS):
                    after(pe, a_D, s, i)
                    if not first(i):
                        pe.wait_ge(a_acc, BODY * (i - 1) + GV * (s + 1))
                    pe.wait_ge(a_g[s], 16 * GV * (i + 1))
                    for u in range(GV):
                        last = mm(bank[s][:, u * HID:(u + 1) * HID], A_D[:, s, u, :], A_g[:, s, u, :], start=True, stop=True)
                    last.then_inc(a_mm, 1)
            def sums_and_turns(i):
                for j in range(2):
                    pe.wait_ge(at_in[j], 16 * (i + 1))
                    after2(pe, at_cp, j, i, 2)
                    tr(bank[6 + j][:, 0:P], A_at[:, j, :], ident[:, :]).then_inc(at_T, 1)
                sums0(i)
            loop(pe, COUNT_LOOPS, sums_and_turns)
            visit_counts(1)
            with pe.Fori(COUNT_LOOPS, AT_LOOPS) as i:
                sums_and_turns(i)
            with pe.Fori(AT_LOOPS, LOOPS) as i:
                sums0(i)

            pe.wait_ge(a_done, 1)
            pe.wait_ge(g_ones, 1)

            def update0(i):
                for s in range(2):
                    after2(pe, g_Tc, s, i, 2)
                    after2(pe, g_in, s, i, incs=2)
                    turn(pe, "pe")
                    for u in range(4):
                        last = tr(bank[s][0:HID, u * P:(u + 1) * P], G_in[:, s, u, :], ident[:, :])
                    last.then_inc(g_T, 1)
                for s in range(2):
                    after2(pe, g_Tc, s, i)
                    after2(pe, g_x, s, i, 2)
                    for u in range(2):
                        b = bank[2 + s][:, u * 4 * HID:(u + 1) * 4 * HID]
                        mm(b[:, 0:GATES], G_T[:, s, u, :], wih0T[:, :], start=True, stop=False)
                        mm(b[:, 0:2 * HID], G_T[:, s, 2 + u, :], whh0T[:, 0:2 * HID], start=False, stop=False)
                        last = mm(b[:, GATES:4 * HID], G_T[:, s, 2 + u, :], whh0T[:, 2 * HID:GATES], start=False, stop=True)
                    last.then_inc(g_mm, 1)
            loop(pe, G_LOOPS, update0)

            pe.wait_ge(p_ones, 1)

            def tables1(i):
                for s in range(2):
                    after2(pe, p_Tc, s, i, 2)
                    after2(pe, p_h, s, i)
                    turn(pe, "pe")
                    for u in range(2):
                        last = tr(bank[s][0:HID, u * P:(u + 1) * P], P_in[:, s, u, :], ident[:, :])
                    last.then_inc(p_T, 1)
                for s in range(2):
                    after2(pe, p_Tc, s, i)
                    after2(pe, p_q, s, i, 2)
                    after2(pe, p_p, s, i, 2)
                    for u in range(2):
                        mm(bank[2 + s][:, u * H1:(u + 1) * H1], P_hT[:, s, u, :], waT[:, :], start=True, stop=True)
                        last = mm(bank[4 + s][:, u * H1:(u + 1) * H1], P_hT[:, s, u, :], wbT[:, :], start=True, stop=True)
                    last.then_inc(p_mm, 1)
            loop(pe, G_LOOPS, tables1)

            pe.wait_ge(p_q, 2 * G_LOOPS)
            pe.wait_ge(p_p, 2 * G_LOOPS)
            pe.wait_ge(s_constb, N_CONSTB)

            def rows(i, s, stages):
                if 0 in stages:
                    after(pe, b_D, s, i)
                    after(pe, b_DTc, s, i, 2)
                    for u in range(GV):
                        last = tr(bank_b[s % 2][:, u * P:(u + 1) * P], B_D[:, s, u, :], ident_b[:, :])
                    last.then_inc(b_DT, 1)
                if 1 in stages:
                    t, j = stages[1]
                    r = regs(ENG.PE, wwin, j * BODY + t * GV, N_WIN - 1)
                    pe.wait_ge(b_in[t], 32 * GV * (j + 1))
                    after(pe, b_DTc, t, j)
                    after(pe, b_row, t, j, 2, incs=2)
                    for u in range(GV):
                        b = bank[2 + 2 * (t % 2) + u // 2][:, (u % 2) * ROW_ONE:(u % 2 + 1) * ROW_ONE]
                        w = ds(r[u], 1)
                        mm(b[:, 0:H1], B_DT[:, t, u, :], q_tab[:, w, :].rearrange("p a k -> p (a k)"), start=True, stop=False)
                        mm(b[:, 0:H1], B_at[:, t, u, :], wattr[:, :], start=False, stop=True)
                        last = mm(b[:, H1:ROW_ONE], B_DT[:, t, u, :], h[:, w, :].rearrange("p a k -> p (a k)"), start=True, stop=True)
                    last.then_inc(b_hr, 1)
            run_ticks(pe, rows, 2)
            pe.wait_ge(b_row, 2 * NS * LOOPS)
            visit_tables(1)

            pe.wait_ge(s_vtab, 2)
            pe.wait_ge(p_back, 16)

            def tick(i, s, stages):
                if 3 in stages:
                    t, j = stages[3]
                    after(pe, c_df, t, j)
                    after(pe, c_d, t, j, 1)
                    for u in range(GV):
                        k = 1 + t * GV + u
                        last = mm(bank[5][:, u:u + 1], C_ST[:, t, u, :], C_mn[:, k:k + 1], start=True, stop=True)
                    last.then_inc(c_mg, 1)
                if 2 in stages:
                    t, j = stages[2]
                    after(pe, c_sp, t, j)
                    after(pe, c_pc, t, j, 1)
                    turn(pe, "pe")
                    tr(bank_b[1][0:PARTS * GV, 0:P], C_parts[:, t, :], ident_b[:, :]).then_inc(c_pt, 1)
                if 0 in stages:
                    after(pe, c_N, s, i)
                    after(pe, c_STc, s, i, 1)
                    for u in range(GV):
                        last = tr(bank_b[0][:, u * P:(u + 1) * P], C_N[:, s, u, :], ident_b[:, :])
                    last.then_inc(c_St, 1)
                if 1 in stages:
                    t, j = stages[1]
                    r = regs(ENG.PE, wwin, j * BODY + t * GV, N_WIN - 1)
                    after(pe, c_STc, t, j)
                    after(pe, c_sp, t, j, 1)
                    for u in range(GV):
                        b = bank[2 + u // 2][:, (u % 2) * H1:(u % 2 + 1) * H1]
                        last = mm(b, C_ST[:, t, u, :], p_tab[:, ds(r[u], 1), :].rearrange("p a k -> p (a k)"), start=True, stop=True)
                    last.then_inc(c_pre, 1)
                if 2 in stages:
                    t, j = stages[2]
                    after(pe, c_pc, t, j)
                    after(pe, c_df, t, j, 1)
                    turn(pe, "pe")
                    for u in range(GV):
                        b = bank[4][:, u * P:(u + 1) * P]
                        mm(b, C_N[:, t, u, :], big_b[:, :], start=True, stop=False)
                        last = mm(b, sel[:, u * P:(u + 1) * P], C_PT[:, t % 2, :], start=False, stop=True)
                    last.then_inc(c_MKt, 1)
                if 3 in stages:
                    t, j = stages[3]
                    after(pe, c_W, t, j)
                    after(pe, c_acc, t, j, 2)
                    after(pe, c_S, t, j)
                    for u in range(GV):
                        last = mm(bank[6 + t % 2][:, u * (HID + 1):(u + 1) * (HID + 1)], C_S[:, t, u, :], C_W[:, t % 2, u, :],
                                  start=True, stop=True)
                    last.then_inc(c_ag, 1)
            run_ticks(pe, tick, 5)

            pe.wait_ge(n_ones, 1)

            def update1(i):
                for s in range(2):
                    after2(pe, n_c, s, i)
                    after2(pe, n_Tc, s, i, 2, incs=2)
                    after2(pe, n_in, s, i)
                    turn(pe, "pe")
                    for u in range(2):
                        tr(bank[s][0:HID + 1, u * P:(u + 1) * P], G_c[:, s, u, :], ident[:, :])
                        last = tr(bank[s][0:HID, (2 + u) * P:(3 + u) * P], G_in[:, s, 2 + u, :], ident[:, :])
                    last.then_inc(n_T, 1)
                for s in range(2):
                    after2(pe, n_Tc, s, i, incs=2)
                    after2(pe, n_msc, s, i, 2, incs=2)
                    for u in range(2):
                        mm(bank[4 + s][:, u * HID:(u + 1) * HID], G_T[:, s, u, :], wlinT[:, :], start=True, stop=True)
                        last = mm(bank[4 + s][0:HID, (2 + u) * P:(3 + u) * P], wlinT[:, :], G_T[:, s, u, :], start=True, stop=True)
                    last.then_inc(n_ms, 1)
                    after2(pe, n_msc, s, i, incs=2)
                    after2(pe, n_x, s, i, 2)
                    for u in range(2):
                        b = bank[2 + s][:, u * 4 * HID:(u + 1) * 4 * HID]
                        mm(b[:, 0:GATES], G_T[:, s, 2 + u, :], wih1T[:, :], start=True, stop=False)
                        mm(b[:, 0:2 * HID], G_mT[:, s, u, :], whh1T[:, 0:2 * HID], start=False, stop=False)
                        last = mm(b[:, GATES:4 * HID], G_mT[:, s, u, :], whh1T[:, 2 * HID:GATES], start=False, stop=True)
                    last.then_inc(n_mm, 1)
            loop(pe, G_LOOPS, update1)

        @block.vector
        def _(dve):
            v = nc.vector
            ch = Chain(dve, own["dve"])
            lo = P - 32
            for t, val in ((dst_i, PAD_KEY), (src_i, PAD_KEY), (typ_i, 0)):
                v.memset(t[lo:P, LAST_COLS:COLS], val).then_inc(s_padded, 1)
            v.memset(xs[:, N_WIN - 1:NW, :], 0.0).then_inc(s_padded, 1)
            v.memset(before[:, :], 0).then_inc(s_padded, 1)

            dve.wait_ge(s_ids, 96)
            dve.wait_ge(s_padded, 5)
            ch.link(v.tensor_scalar(scan.bitcast(i32), dst_i, 7, None, ALU.arith_shift_right))
            ch.link(v.tensor_copy(win, scan.bitcast(i32)))

            dve.wait_ge(s_before, 16)
            ch.link(v.tensor_tensor(scan[:, 0:1], dst_i[:, 0:1], before[:, :], ALU.is_lt))
            ch.link(v.tensor_tensor(scan[:, 1:COLS], dst_i[:, 1:COLS], dst_i[:, 0:COLS - 1], ALU.is_lt))
            v.tensor_reduce(out_of_order[:, :], scan, AX.X, ALU.add).then_inc(s_flagp, 1)

            def normalise(k):
                flat = NW * HID
                sq = acc[:, :, :].rearrange("p w k -> p (w k)")[:, 0:flat].rearrange("p (w k) -> p w k", k=HID)
                var, std, mean = small[:, 0:NW], small[:, NW:2 * NW], small[:, 2 * NW:3 * NW]

                def bc(t):
                    return t.unsqueeze(2).to_broadcast([P, NW, HID])
                ch.link(v.tensor_reduce(mean, xs[:, :, :], AX.X, ALU.add))
                ch.link(v.tensor_scalar(mean, mean, 1.0 / HID, None, ALU.mult))
                ch.link(v.tensor_tensor(h[:, :, :], xs[:, :, :], bc(mean), ALU.subtract))
                ch.link(v.tensor_tensor(sq, h[:, :, :], h[:, :, :], ALU.mult))
                ch.link(v.tensor_reduce(var, sq, AX.X, ALU.add))
                v.tensor_scalar(var, var, 1.0 / HID, None, ALU.mult).then_inc(s_var, 1)
                dve.wait_ge(s_std, k)
                ch.link(v.reciprocal(std, std))
                ch.link(v.tensor_tensor(h[:, :, :], h[:, :, :], bc(std), ALU.mult))
                v.tensor_scalar(h[:, :, :], h[:, :, :], 0.0, None, ALU.max).then_inc(s_h, 1)

            dve.wait_ge(s_x, 32)
            normalise(1)

            def count(w):
                ch.link(v.tensor_scalar(mask, win, iota[:, ds(w, 1)], None, ALU.is_equal, ALU.add, accum_out=cnt[:, ds(w, 1)]))

            dve.wait_ge(s_const, N_CONST)
            v.memset(wbT[HID:HID + 1, :], 0.0).then_inc(s_constb, 1)
            v.tensor_copy(iota_b[:, :], iota[:, :]).then_inc(s_constb, 1)
            v.tensor_copy(ident_b[:, :], ident[:, :]).then_inc(s_constb, 1)
            v.tensor_scalar(big_b[:, :], ident[:, :], -MASKED, None, ALU.mult).then_inc(s_constb, 1)
            pr = PARTS * GV
            ch.link(v.tensor_tensor(sel_a[:, :], ident[0:pr, 0:GV], ident[0:pr, GV:2 * GV], ALU.add))
            ch.link(v.tensor_tensor(sel_a[:, :], sel_a[:, :], ident[0:pr, 2 * GV:3 * GV], ALU.add))
            v.tensor_copy(sel[:, :].rearrange("p (u n) -> p u n", u=GV),
                          sel_a[:, :].unsqueeze(2).to_broadcast([pr, GV, P])).then_inc(s_constb, 1)
            with dve.Fori(0, N_KEYS // 2) as i:
                ch.body(i, 2)
                count(i * 2)
                count(i * 2 + 1)
                ch.end_body()
            ch.end_loop(N_KEYS // 2)
            dve.sem_inc(s_cnt, 1)

            K = N_KEYS

            def totals(k):
                dve.wait_ge(s_tot, k + 1)
                v.tensor_copy(cc[k][0:K, :], bank[4][0:K, 2 * P:2 * P + 1]).then_inc(s_cc, 1)
                tot, incl = small[:, 3 * P:3 * P + K], small[:, 2 * P:2 * P + K]
                ch.link(v.tensor_copy(tot, bank[4][:, 0:K]))
                ch.link(v.tensor_tensor_scan(incl, tot, tot, 0.0, ALU.add, ALU.max))
                ch.link(v.tensor_tensor(incl, incl, tot, ALU.subtract))
                ch.link(v.tensor_tensor(place0[:, :], incl, bank[4][:, P:P + K], ALU.add))
                if k == 0:
                    v.tensor_copy(unsorted[:, :], bank[4][0:1, 3 * P:3 * P + 1]).then_inc(s_flag, 1)

            def visit_table(k):
                e = [small[0:K, j:j + 1] for j in range(20, 30)]
                start, end, ft, lt, hs, vend, t1 = e[0:7]
                si, ei = e[7].bitcast(i32), e[8].bitcast(i32)
                dve.wait_ge(s_start, k + 1)
                ch.link(v.tensor_copy(start, bank[5][0:K, 0:1]))
                ch.link(v.tensor_tensor(end, start, cc[k][0:K, :], ALU.add))
                ch.link(v.tensor_copy(si, start))
                ch.link(v.tensor_scalar(ei, end, -1.0, None, ALU.add))
                ch.link(v.tensor_scalar(si, si, 7, None, ALU.arith_shift_right))
                ch.link(v.tensor_scalar(ei, ei, 7, None, ALU.arith_shift_right))
                ch.link(v.tensor_copy(ft, si))
                ch.link(v.tensor_copy(lt, ei))
                ch.link(v.scalar_tensor_tensor(t1, lt, 1.0, ft, ALU.add, ALU.subtract))
                ch.link(v.tensor_scalar(hs, cc[k][0:K, :], 0.0, None, ALU.is_gt))
                v.tensor_tensor(nt[0:K, :], t1, hs, ALU.mult).then_inc(s_nt, 1)
                dve.wait_ge(s_vstart, k + 1)
                ch.link(v.tensor_tensor(vend, nt[0:K, :], bank[5][0:K, 1:2], ALU.add))
                v.tensor_tensor(off[0:K, :], ft, bank[5][0:K, 1:2], ALU.subtract).then_inc(s_off, 1)
                dve.wait_ge(s_shift, k + 1)
                ch.link(v.tensor_tensor(t1[0:HW], bank[5][0:HW, 2:3], off[0:HW, :], ALU.subtract))
                ch.link(v.tensor_scalar(dbc[0:HW, :], ones[0:HW, :], t1[0:HW], None, ALU.mult))
                dve.wait_ge(s_iotav, k + 1)
                v.tensor_scalar(vmask[0:HW, :], iota_v[0:HW, :], vend[0:HW], None, ALU.is_ge).then_inc(s_vmask, 1)
                dve.wait_ge(s_vsum, k + 1)
                for q in range(4):
                    c = slice(q * VCHUNK, (q + 1) * VCHUNK)
                    ch.do(v.tensor_scalar(wbase[:, c], bank[q][:, 0:VCHUNK], float(P), None, ALU.mult))
                    ch.do(v.tensor_copy(wwin[0:1, c], bank[q][0:1, 0:VCHUNK]))
                    ch.link(v.tensor_tensor(iota_v[0:1, c], iota_v[0:1, c], bank[4 + q][0:1, 0:VCHUNK], ALU.add))
                    ch.link(v.tensor_scalar(wtile[0:1, c], iota_v[0:1, c], float(TILES - 1), None, ALU.min))
                dve.sem_inc(s_vtab, 1)

            totals(0)
            visit_table(0)

            def place(w, where, ch):
                ch.link(v.tensor_scalar(mask, win, iota[:, ds(w, 1)], None, ALU.is_equal))
                ch.link(v.tensor_tensor_scan(scan, mask, mask, place0[:, ds(w, 1)], ALU.add, ALU.max))
                turn(dve, "dve")
                ch.link(v.copy_predicated(where, mask.bitcast(u16), scan))

            dve.wait_ge(s_flag, 1)
            flag = dve.value_load(unsorted[0:1, 0:1], min_val=0, max_val=N_EDGES)
            with dve.If(flag > 0):
                dch = Chain(dve, d_step)
                dch.link(v.memset(d_place, 0.0))
                with dve.Fori(0, N_KEYS) as w:
                    dch.body(w, 3)
                    place(w, d_place, dch)
                    dch.end_body()
                dch.end_loop(N_KEYS)

                def stage(i):
                    dch.body(i, 3)
                    if not first(i):
                        dve.wait_ge(d_free, i)
                    c = ds(i * SORT_COLS, SORT_COLS)
                    for k, t in enumerate((dst_i, src_i, typ_i)):
                        dch.link(v.tensor_copy(d_rows[:, :, ATTR + k].bitcast(i32), t[:, c]))
                    v.tensor_scalar(d_pos, d_place[:, c], -1.0, None, ALU.add).then_inc(d_ready, 1)
                    dch.end_body()
                dch.link(v.memset(d_rows[:, :, SORT_ROW - 1], 0.0))
                loop(dve, COLS // SORT_COLS, stage)
                dch.end_loop(COLS // SORT_COLS)
                dve.wait_ge(d_ids, 16)
                ids = kB_flat.bitcast(i32).rearrange("p (c k) -> p c k", k=REC)
                for k, t in enumerate((dst_i, src_i, scan.bitcast(i32))):
                    dch.link(v.tensor_copy(t, ids[:, :, k]))
                dch.link(v.tensor_copy(typ_i, scan.bitcast(i32)))

            v.tensor_copy(kA[:, :, 0], dst_i).then_inc(s_kA, 1)
            v.scalar_tensor_tensor(kA[:, :, 1].bitcast(i32), src_i, float(TYPES), typ_i, ALU.mult, ALU.add).then_inc(s_kA, 1)

            dve.wait_ge(s_recA, 16)
            ch.link(v.tensor_copy(kB[:, :, 0], dst_i))
            ch.link(v.tensor_copy(kB[:, :, 1], src_i))
            ch.link(v.memset(kB[:, :, 2:4], 0.0))
            ch.link(v.tensor_scalar(scan.bitcast(i32), src_i, 7, None, ALU.arith_shift_right))
            ch.link(v.tensor_copy(win, scan.bitcast(i32)))
            v.memset(acc[:, :, :], 0.0).then_inc(a_zero, 1)
            dve.wait_ge(a_zero, 1)
            for s in range(2):
                dve.wait_ge(t_st[s], 16 * (NW // 2))

            def sums0(i, extra, steps):
                ch.body(i, NS + steps)
                for s in range(NS):
                    r = regs(ENG.DVE, wwin, i * BODY + s * GV, N_WIN - 1)
                    dve.wait_ge(a_rec[s], 16 * GV * (i + 1))
                    after(dve, a_mm, s, i, NS)
                    ch.link(v.tensor_tensor(A_kl[:, s, :], A_rec[:, s, :, 0], wbase[:, ds(i * BODY + s * GV, GV)], ALU.subtract))
                    v.tensor_tensor(A_D[:, s, :, :], iota[:, :].unsqueeze(1).to_broadcast([P, GV, P]),
                                    per_group(A_kl[:, s, :], P), ALU.is_equal).then_inc(a_D, 1)
                    if s in (0, 2) and extra:
                        extra(i, s // 2)
                    after(dve, a_mm, s, i)
                    for u in range(GV):
                        if not (first(i) and s == 0 and u == 0):
                            dve.wait_ge(a_acc, i * BODY + s * GV + u)
                        t = acc[:, ds(r[u], 1), 0:HID].rearrange("p a k -> p (a k)")
                        v.tensor_tensor(t, t, bank[s][:, u * HID:(u + 1) * HID], ALU.add).then_inc(a_acc, 1)
                ch.end_body()

            loop(dve, COUNT_LOOPS, lambda i: sums0(i, lambda i, j: count(i * 2 + j), 2))
            ch.end_loop(COUNT_LOOPS)
            ch.per = 0
            dve.sem_inc(s_cnt, 1)
            totals(1)
            ch.base += ch.k
            ch.k = 0
            ch.base -= COUNT_LOOPS * (NS + 6)
            with dve.Fori(COUNT_LOOPS, COUNT_LOOPS + PLACE_LOOPS) as i:
                sums0(i, lambda i, j: place((i - COUNT_LOOPS) * 2 + j, kB[:, :, 2], ch), 6)
            ch.base += (COUNT_LOOPS + PLACE_LOOPS) * (NS + 6)
            ch.base -= (COUNT_LOOPS + PLACE_LOOPS) * NS
            with dve.Fori(COUNT_LOOPS + PLACE_LOOPS, LOOPS) as i:
                sums0(i, None, 0)
            ch.base += LOOPS * NS
            ch.i = ch.per = ch.k = 0
            v.tensor_scalar(kB[:, :, 2], kB[:, :, 2], -1.0, None, ALU.add).then_inc(s_kB, 1)

            dve.wait_ge(a_acc, LOOPS * BODY)
            for j in range(2):
                dve.wait_ge(at_st[j], 16 * AT_LOOPS)
            dve.sem_inc(a_done, 1)
            v.memset(G_T[HID:HID + 1, :, :, :], 1.0).then_inc(g_ones, 1)

            def gru(i, s, sT, sV, sN, hid):
                b = two(bank[2 + s], 4 * HID)
                after2(dve, sT, s, i)
                ch.link(v.scalar_tensor_tensor(G_u[:, s, :, :], G_t[:, s, :, 0:HID], 1.0, b[:, :, GATES:4 * HID], ALU.add, ALU.mult))
                v.scalar_tensor_tensor(G_v[:, s, :, :], G_u[:, s, :, :], 0.5, b[:, :, 2 * HID:GATES], ALU.mult, ALU.add).then_inc(sV, 1)
                after2(dve, sN, s, i)
                ch.link(v.tensor_tensor(G_d[:, s, :, :], hid, G_n[:, s, :, :], ALU.subtract))
                ch.link(v.scalar_tensor_tensor(G_e[:, s, :, :], G_t[:, s, :, HID:2 * HID], 1.0, G_d[:, s, :, :], ALU.add, ALU.mult))
                ch.link(v.scalar_tensor_tensor(G_d[:, s, :, :], G_e[:, s, :, :], 0.5, G_n[:, s, :, :], ALU.mult, ALU.add))

            def update0(i):
                ch.body(i, 8)
                for s in range(2):
                    w = ds(i * 4 + s * 2, 2)
                    gru(i, s, g_t, g_v, g_n, h[:, w, :])
                    v.tensor_tensor(xs[:, w, :], xs[:, w, :], G_d[:, s, :, :], ALU.add).then_inc(g_x, 1)
                ch.end_body()
            loop(dve, G_LOOPS, update0)
            ch.end_loop(G_LOOPS)
            dve.wait_ge(g_x, 2 * G_LOOPS)
            normalise(2)
            dve.wait_ge(s_h, 2)

            v.memset(P_hT[HID:HID + 1, :, :, :], 1.0).then_inc(p_ones, 1)

            v.memset(B_row[:, :, :, ROW_ONE:ROW], 1.0).then_inc(b_pad, 1)
            v.memset(padrows, 0.0).then_inc(b_pad, 1)
            dve.wait_ge(b_pad, 2)
            v.memset(padrows[:, :, ROW_SRC], float(PAD_KEY)).then_inc(b_pad, 1)

            def tables1(i):
                for s in range(2):
                    after2(dve, p_mm, s, i)
                    if not first(i):
                        dve.wait_ge(p_st[s], 16 * i)
                    v.tensor_copy(P_out[:, s, :, :], two(bank[2 + s], H1)).then_inc(p_p, 1)
            loop(dve, G_LOOPS, tables1)
            dve.wait_ge(s_constb, N_CONSTB)

            def rows(i):
                ch.body(i, 3 * NS)
                for s in range(NS):
                    dve.wait_ge(b_in[s], 32 * GV * (i + 1))
                    v.tensor_tensor(B_kl[:, s, :], B_rec[:, s, :, 0], wbase[:, ds(i * BODY + s * GV, GV)], ALU.subtract).then_inc(b_kl, 1)
                    after(dve, b_kl, s, i)
                    after(dve, b_DT, s, i, NS)
                    v.tensor_tensor(B_D[:, s, :, :], iota[:, :].unsqueeze(1).to_broadcast([P, GV, P]),
                                    per_group(B_kl[:, s, :], P), ALU.is_equal).then_inc(b_D, 1)
                    ch.link(v.tensor_scalar(B_ge[:, s, :], B_kl[:, s, :], 0.0, None, ALU.is_ge))
                    ch.link(v.scalar_tensor_tensor(B_in[:, s, :], B_kl[:, s, :], float(P), B_ge[:, s, :], ALU.is_lt, ALU.mult))
                    ch.link(v.scalar_tensor_tensor(B_sh[:, s, :], B_rec[:, s, :, 2], -BIG, B_in[:, s, :], ALU.add, ALU.mult))
                    if not first(i):
                        dve.wait_ge(b_sc[s], 16 * GV * i)
                    v.tensor_copy(B_row[:, s, :, ROW_SRC], B_rec[:, s, :, 1]).then_inc(b_pos, 1)
                    v.tensor_scalar(B_pos[:, s, :], B_sh[:, s, :], BIG, None, ALU.add).then_inc(b_pos, 1)
                ch.end_body()
            dve.wait_ge(b_pad, 3)
            loop(dve, LOOPS, rows)
            ch.end_loop(LOOPS)

            dve.wait_ge(b_sent, 1)
            visit_table(1)
            for s in range(2):
                dve.wait_ge(p_st[s], 16 * G_LOOPS)
            v.memset(acc[:, :, :], 0.0).then_inc(c_init, 1)
            v.memset(wbase_all[:, 0:1], -float(P)).then_inc(c_init, 1)
            v.memset(C_mn[:, 0:1], 0.0).then_inc(c_init, 1)
            dve.wait_ge(c_init, 3)

            def tick(i, s, stages):
                if 0 in stages:
                    dve.wait_ge(c_in[s], 16 * GV * (i + 1))
                    a = i * BODY + s * GV
                    ch.link(v.tensor_tensor(C_kl[:, s, :], C_V[:, s, :, ROW_SRC], wbase[:, ds(a, GV)], ALU.subtract))
                    after(dve, c_MKt, s, i, NS)
                    for t, op, sig in ((C_N, ALU.not_equal, c_N), (C_S, ALU.is_equal, c_S)):
                        if sig is c_S:
                            after(dve, c_ag, s, i, NS)
                        v.tensor_tensor(t[:, s, :, :], iota[:, :].unsqueeze(1).to_broadcast([P, GV, P]),
                                        per_group(C_kl[:, s, :], P), op).then_inc(sig, 1)
                    ch.link(v.tensor_tensor(C_pen[:, s, :], wbase_all[:, ds(a, GV)], wbase[:, ds(a, GV)], ALU.subtract))
                    ch.do(v.tensor_scalar(C_pen[:, s, :], C_pen[:, s, :], MASKED / P, None, ALU.mult))
                if 3 in stages:
                    t, j = stages[3]
                    after(dve, c_mg, t, j)
                    ch.link(v.scalar_tensor_tensor(C_z[:, t, :], bank[5][:, 0:GV], -1.0, C_s[:, t, :], ALU.mult, ALU.add))
                    v.tensor_scalar(C_d[:, t, :], C_z[:, t, :], 0.0, None, ALU.min).then_inc(c_d, 1)
                if 1 in stages:
                    t, j = stages[1]
                    after(dve, c_pre, t, j)
                    for half in range(2):
                        c = slice(2 * half, 2 * half + 2)
                        m = v.tensor_tensor(C_pre[:, c, :], two(bank[2 + half], H1), C_V[:, t, c, 0:H1], ALU.add)
                        (ch.link if half else ch.do)(m)
                    for u in range(GV):
                        m = v.scalar_tensor_tensor(C_pre[:, u, :], C_pre[:, u, :], 0.0, w2bc[:, :], ALU.max, ALU.mult,
                                                   accum_out=C_raw[:, t, u:u + 1])
                        (ch.link if u == GV - 1 else ch.do)(m)
                    part_of = [C_parts[:, t, k * GV:(k + 1) * GV] for k in range(PARTS)]
                    ch.do(v.tensor_scalar(part_of[0], C_raw[:, t, :], b2bc[:, :], None, ALU.add))
                    ch.link(v.tensor_scalar(C_s[:, t, :], C_raw[:, t, :], b2bc[:, :], None, ALU.add))
                    ch.link(v.tensor_tensor(C_r[:, t, :], C_s[:, t, :], part_of[0], ALU.subtract))
                    ch.link(v.tensor_copy(part_of[1], C_r[:, t, :]))
                    v.tensor_tensor(part_of[2], C_r[:, t, :], part_of[1], ALU.subtract).then_inc(c_sp, 1)
                if 2 in stages:
                    t, j = stages[2]
                    a = t * GV
                    after(dve, c_MKt, t, j)
                    ch.link(v.tensor_reduce(C_tm[:, t, :], four(bank[4], P), AX.X, ALU.max))
                    ch.link(v.tensor_tensor_scan(C_mn[:, 1 + a:1 + a + GV], C_pen[:, t, :], C_tm[:, t, :], C_mn[:, a:a + 1], ALU.add, ALU.max))
                    ch.link(v.tensor_tensor(C_mo[:, t, :], C_mn[:, a:a + GV], C_pen[:, t, :], ALU.add))
                    v.tensor_tensor(C_df[:, t, :], C_mo[:, t, :], C_mn[:, 1 + a:1 + a + GV], ALU.subtract).then_inc(c_df, 1)
                    if t == NS - 1:
                        ch.link(v.tensor_copy(C_mn[:, 0:1], C_mn[:, NS * GV:1 + NS * GV]))
                if 4 in stages:
                    t, j = stages[4]
                    r = regs(ENG.DVE, wwin, j * BODY + t * GV, N_WIN - 1)
                    after(dve, c_ag, t, j)
                    after(dve, c_cr, t, j)
                    after(dve, c_acc, t, j, 1)
                    for u in range(GV):
                        k = acc[:, ds(r[u], 1), :].rearrange("p a k -> p (a k)")
                        m = v.scalar_tensor_tensor(k, k, C_cr[:, t, u:u + 1], bank[6 + t % 2][:, u * (HID + 1):(u + 1) * (HID + 1)],
                                                   ALU.mult, ALU.add)
                        if u < GV - 1:
                            ch.link(m)
                    m.then_inc(c_acc, 1)
            run_ticks(dve, tick, 5, ch, NS * (3 + 1 + 2 + GV + 4 + 3 + GV - 1) + 1)

            dve.wait_ge(c_acc, NS * LOOPS)
            v.memset(G_T[HID:HID + 1, :, 2:4, :], 1.0).then_inc(n_ones, 1)
            ch.link(v.memset(G_mT[HID:HID + 1, :, :, :], 1.0))
            ch.link(v.tensor_scalar(has, acc[:, :, HID], 0.0, None, ALU.is_gt))
            ch.link(v.tensor_scalar(tmp_w, has, -1.0, 1.0, ALU.mult, ALU.add))
            ch.link(v.tensor_tensor(tmp_w, tmp_w, acc[:, :, HID], ALU.add))
            ch.link(v.reciprocal(rden, tmp_w))

            def update1(i):
                ch.body(i, 8 + 6)
                for s in range(2):
                    w = ds(i * 4 + s * 2, 2)
                    after2(dve, n_T, s, i, 2)
                    v.tensor_tensor(G_c[:, s, :, :], acc[:, w, :], rden[:, w].unsqueeze(2).to_broadcast([P, 2, HID + 1]),
                                    ALU.mult).then_inc(n_c, 1)
                for s in range(2):
                    w = ds(i * 4 + s * 2, 2)
                    after2(dve, n_msc, s, i, incs=2)
                    gru(i, s, n_t, n_v, n_n, G_m[:, s, :, :])
                    ch.link(v.tensor_tensor(G_e[:, s, :, :], G_d[:, s, :, :], h[:, w, :], ALU.subtract))
                    ch.link(v.tensor_tensor(G_d[:, s, :, :], G_e[:, s, :, :], has[:, w].unsqueeze(2).to_broadcast([P, 2, HID]), ALU.mult))
                    ch.link(v.tensor_tensor(G_e[:, s, :, :], G_d[:, s, :, :], h[:, w, :], ALU.add))
                    v.tensor_tensor(xs[:, w, :], xs[:, w, :], G_e[:, s, :, :], ALU.add).then_inc(n_x, 1)
                ch.end_body()
            loop(dve, G_LOOPS, update1)


_INS = ['x', 'src', 'dst', 'edge_attr_16', 'edge_type_8', 'L0_gnn_edge_matrix', 'L0_gnn_w_ih', 'L0_gnn_w_hh',
        'L0_gnn_b_ih', 'L0_gnn_b_hh', 'L1_gnn_W_att1', 'L1_gnn_b_att1', 'L1_gnn_W_att2', 'L1_gnn_b_att2',
        'L1_gnn_W_lin', 'L1_gnn_b_lin', 'L1_gnn_W_ih', 'L1_gnn_b_ih', 'L1_gnn_W_hh', 'L1_gnn_b_hh']
_OUTS = [((12500, 64), 'float32')]


def kernel(**inputs):
    import numpy as _np
    import concourse.bacc as _bacc
    from concourse import mybir as _mybir
    from concourse.bass_utils import run_bass_kernel_spmd as _run

    nc = _bacc.Bacc("TRN2", target_bir_lowering=False, num_devices=1)
    arrays, args = {}, []
    for name in _INS:
        a = _np.ascontiguousarray(inputs[name])
        arrays[f"in_{name}_dram"] = a
        args.append(nc.dram_tensor(f"in_{name}_dram", a.shape, _mybir.dt.from_np(a.dtype), kind="ExternalInput").ap())
    for i, (shape, dtype) in enumerate(_OUTS):
        dt = _mybir.dt.from_np(_np.dtype(dtype))
        args.append(nc.dram_tensor(f"out_{i}_dram", shape, dt, kind="ExternalOutput").ap())
    build(nc, *args)
    r = _run(nc, [arrays], core_ids=[0])
    return r.results[0]["out_0_dram"]
```

```python
import concourse.bass as bass
from concourse import mybir
from contextlib import ExitStack

P = 128
N_NODES = 12500
N_EDGES = 212500
HID = 64
ATTR = 16
TYPES = 8
GATES = 3 * HID
H1 = 2 * HID + ATTR
BANK = 512
N_WIN = -(-N_NODES // P)
NW = 4 * -(-N_WIN // 4)
N_KEYS = NW
LAST_NODES = N_NODES - (N_WIN - 1) * P
COLS = 1664
SLOTS = P * COLS
TILES = SLOTS // P
LAST_COLS = N_EDGES - (P - 1) * COLS
N_PAD = SLOTS - N_EDGES
PAD_KEY = N_WIN * P
GV = 4
NS = 4
BODY = GV * NS
VISITS = BODY * -(-(-(-N_EDGES // P) + N_WIN - 1) // BODY)
LOOPS = VISITS // BODY
VCHUNK = VISITS // 4
HW = N_WIN - 1
ROW_ONE = H1 + HID
ROW_SRC = ROW_ONE + 1
ROW = ROW_SRC + 1
REC0 = 2
REC1 = 3
BLOCKS = COLS // P
IDS = 4
BIG = float(1 << 20)
MASKED = float(1 << 100)
PARTS = 3
PAIRS = [(a, w) for a in range(PARTS) for w in range(PARTS)][:-1]
AT_BLOCK = P // ATTR
AT_BLOCKS = TILES // AT_BLOCK
AT_LOOPS = AT_BLOCKS // 2
EPS = 1.0e-5
SORT_COLS = 16
SORT_ROW = ATTR + IDS
COUNT_LOOPS = N_KEYS // 2
PLACE_LOOPS = N_KEYS // 2
G_LOOPS = NW // 4


class Chain:

    def __init__(self, eng, sem):
        self.eng, self.sem = eng, sem
        self.base = self.k = self.i = self.per = 0

    def body(self, i, per):
        if not self.per:
            self.base += self.k
        self.i, self.per, self.k = i, per, 0

    def end_body(self):
        assert self.k == self.per, (self.k, self.per)
        self.k = 0

    def end_loop(self, n):
        self.base += n * self.per
        self.i = self.per = self.k = 0

    def do(self, ins):
        self.k += 1
        ins.then_inc(self.sem, 1)
        return self.base + self.i * self.per + self.k

    def need(self, mark):
        self.eng.wait_ge(self.sem, mark)

    def link(self, ins):
        self.need(self.do(ins))


def first(i):
    return isinstance(i, int) and i == 0


def build(nc, x, src, dst, attr, etype, edge_matrix, w_ih0, w_hh0, b_ih0, b_hh0,
          w_att1, b_att1, w_att2, b_att2, w_lin, b_lin, w_ih1, b_ih1, w_hh1, b_hh1, out):
    f32, i32, bf16, u16 = mybir.dt.float32, mybir.dt.int32, mybir.dt.bfloat16, mybir.dt.uint16
    ALU = mybir.AluOpType
    ACT = mybir.ActivationFunctionType
    AX = mybir.AxisListType
    ENG = mybir.EngineType
    ds = bass.ds
    ctx = ExitStack()

    def sb(name, shape, dt=f32):
        return ctx.enter_context(nc.sbuf_tensor(name, shape, dt))

    def sem(name):
        return ctx.enter_context(nc.semaphore(name))

    def sems(name, n):
        return [sem(f"{name}{j}") for j in range(n)]

    def dram(name, shape, dt=f32):
        return nc.dram_tensor(name, shape, dt, kind="Internal").ap()

    def regs(engine, tab, v, top):
        _, r = nc.values_load_multi_w_load_instructions(
            tab[0:1, ds(v, GV)], engines=(engine,), min_val=0, max_val=top,
            skip_runtime_bounds_check_because="the table's entries are bounded when it is made")
        return r

    def per_group(t, a):
        return t.unsqueeze(2).to_broadcast([P, GV, a])

    with ctx:
        table = dram("msg_table", [NW * P * TYPES, HID])
        attr_d = dram("attr_by_dst", [SLOTS, ATTR])
        attrT_d = dram("attr_turned", [TILES * ATTR * len(PAIRS), P], bf16)
        wpair_d = dram("w_attr_parts", [ATTR, len(PAIRS) * H1], bf16)
        p_d = dram("src_part", [P, NW * H1])
        rows_d = dram("rows_by_src", [SLOTS, ROW])

        sorted_d = dram("edges_by_dst", [SLOTS, SORT_ROW])

        xs = sb("xs", [P, NW, HID])
        h = sb("h", [P, NW, HID])
        acc = sb("acc", [P, NW, HID + 1])
        big = sb("big", [P, NW * H1])
        wbase_all = sb("wbase", [P, 1 + VISITS])
        wbase = wbase_all[:, 1:1 + VISITS]
        wwin = sb("wwin", [1, VISITS], i32)
        wtile = sb("wtile", [1, VISITS], i32)
        RING = 10444
        ring = sb("ring", [P, RING])
        ident = sb("ident", [P, P])
        iota = sb("iota", [P, P])
        ones = sb("ones", [P, P])
        tri = sb("tri", [P, P])
        cnt = sb("cnt", [P, N_KEYS])
        place0 = sb("place0", [P, N_KEYS])
        small = sb("small", [P, 512])
        zeros = sb("zeros", [P, 3 * ATTR])
        AT = sb("AT", [HID, TYPES * HID])
        wih0T = sb("wih0T", [HID + 1, GATES])
        whh0T = sb("whh0T", [HID + 1, GATES])
        wih1T = sb("wih1T", [HID + 1, GATES])
        whh1T = sb("whh1T", [HID + 1, GATES])
        wlinT = sb("wlinT", [HID + 1, HID])
        waT = sb("waT", [HID + 1, H1])
        wbT = sb("wbT", [HID + 1, H1])
        wattr = sb("wattr", [ATTR, H1])
        wpair = sb("wpair", [P, H1], bf16)
        iota_b = sb("iota_b", [P, P], bf16)
        ident_b = sb("ident_b", [P, P], bf16)
        minus_b = sb("minus_b", [P, P], bf16)
        big_b = sb("big_b", [P, P], bf16)
        sel_a = sb("sel_a", [PARTS * GV, GV])
        sel = AT[0:PARTS * GV, 0:GV * P // 2].bitcast(bf16)
        w2bc = sb("w2bc", [P, H1])
        b2bc = sb("b2bc", [P, 1])
        eps_t = sb("eps_t", [P, 1])
        cc = [sb(f"cc{k}", [P, 1]) for k in range(2)]
        nt = sb("nt", [P, 1])
        off = sb("off", [P, 1])
        dbc = sb("dbc", [P, P])
        unsorted = sb("unsorted", [1, 1], i32)
        before = sb("before", [P, 1], i32)
        out_of_order = sb("out_of_order", [P, 1])

        at = [0]

        def part(t, n, limit):
            at[0] += n
            assert at[0] <= limit, at[0]
            return t[:, at[0] - n:at[0]]

        dst_i = part(big, COLS, NW * H1).bitcast(i32)
        src_i = part(big, COLS, NW * H1).bitcast(i32)
        kB_flat = part(big, 4 * COLS, NW * H1)
        planes = [kB_flat[:, k * COLS:(k + 1) * COLS] for k in range(4)]
        dst_f, row_f = planes[0:REC0]
        src_f, place_f = planes[1:REC1]
        typ_i = planes[2].bitcast(i32)
        win = part(big, COLS // 2, NW * H1).bitcast(bf16)
        mask = part(big, COLS // 2, NW * H1).bitcast(bf16)
        scan = part(big, COLS, NW * H1)
        q_tab = big[:, :].rearrange("p (w j) -> p w j", j=H1)
        p_tab = q_tab

        iota_v = ring[:, 0:VISITS]
        vmask = ring[:, VISITS:2 * VISITS]
        t0 = 2 * VISITS
        t_hT = ring[0:HID, t0:t0 + 2 * P].rearrange("p (s n) -> p s n", s=2)
        t_out = ring[:, t0 + 2 * P:t0 + 2 * P + 2 * BANK].rearrange("p (s n) -> p s n", s=2)

        w_rest = ring[0:ATTR, 7000:7000 + H1]
        w_parts = ring[0:ATTR, 7200:7200 + PARTS * H1 // 2].bitcast(bf16).rearrange("k (a n) -> k a n", a=PARTS)
        w_stage = ring[0:ATTR, 7500:7500 + len(PAIRS) * H1 // 2].bitcast(bf16).rearrange("k (c n) -> k c n", c=len(PAIRS))

        d_place = planes[3]
        d_rows = ring[:, 6000:6000 + SORT_COLS * SORT_ROW].rearrange("p (c k) -> p c k", k=SORT_ROW)
        d_pos = ring[:, 6400:6400 + SORT_COLS].bitcast(i32)

        def groups(t, n, k):
            return part(t, n * GV * k, RING).rearrange("p (s u k) -> p s u k", s=n, u=GV)

        def marks(n=NS):
            return part(ring, n * GV, RING).rearrange("p (s u) -> p s u", s=n)

        def onehots():
            return part(ring, NS * GV * P // 2, RING).bitcast(bf16).rearrange("p (s u k) -> p s u k", s=NS, u=GV)

        t_h1 = ring[:, t0 + 2 * P + 2 * BANK:t0 + 3 * P + 2 * BANK].rearrange("p (s n) -> p s n", s=2)

        at[0] = 0
        A_D = groups(ring, NS, P)
        A_g = groups(ring, NS, HID)
        A_rec = groups(ring, NS, REC0)
        A_idx = marks().bitcast(i32)
        recs0 = part(ring, TILES * REC0, RING).rearrange("p (t k) -> p t k", k=REC0)
        A_kl = marks()
        A_at = part(ring, 2 * P, RING).rearrange("p (j n) -> p j n", j=2)
        A_atT = part(ring, PARTS * P, RING).bitcast(bf16).rearrange("p (j a n) -> p j a n", j=2, a=PARTS)

        at[0] = 0
        B_D = onehots()
        B_DT = groups(ring, NS, P)
        B_row = groups(ring, NS, ROW)
        B_rec = groups(ring, NS, REC1)
        B_kl, B_ge, B_in, B_sh = marks(), marks(), marks(), marks()
        B_pos = marks().bitcast(i32)
        B_at = onehots()
        padrows = part(ring, 3 * ROW, RING).rearrange("p (a k) -> p a k", k=ROW)

        at[0] = 0
        C_N = onehots()
        C_S = groups(ring, NS, P)
        C_ST = groups(ring, NS, P)
        C_STb = onehots()
        C_V = groups(ring, NS, ROW)
        C_W = groups(ring, 2, HID + 1)
        C_parts = part(ring, NS * PARTS * GV // 2, RING).bitcast(bf16).rearrange("p (s k) -> p s k", s=NS)
        C_PT = part(ring, P, RING)[0:PARTS * GV].bitcast(bf16).rearrange("p (s n) -> p s n", s=2)
        C_kl = part(ring, NS * GV // 2, RING).bitcast(bf16).rearrange("p (s u) -> p s u", s=NS)
        C_mp = part(ring, NS * GV * PARTS // 2, RING).bitcast(bf16).rearrange("p (s u k) -> p s u k", s=NS, u=GV)
        C_raw, C_s, C_r, C_tm, C_pen, C_mo, C_mr, C_df, C_cr, C_mg, C_z, C_d, C_p = (marks() for _ in range(13))
        C_zero, C_step = part(ring, GV, RING), part(ring, GV, RING)
        C_mn = part(ring, 1 + NS * GV, RING)

        spare = acc[:, :, :].rearrange("p w k -> p (w k)")
        at[0] = 0
        recs1 = part(spare, TILES * REC1, NW * HID).rearrange("p (t k) -> p t k", k=REC1)
        P_in = part(spare, 4 * HID, NW * HID).rearrange("p (s u k) -> p s u k", s=2, u=2)
        P_hT = part(spare, 4 * P, NW * HID)[0:HID + 1].rearrange("p (s u k) -> p s u k", s=2, u=2)
        P_out = part(spare, 4 * H1, NW * HID).rearrange("p (s u k) -> p s u k", s=2, u=2)

        at[0] = 0
        G_T = part(ring, 8 * P, RING)[0:HID + 1, :].rearrange("p (s u n) -> p s u n", s=2, u=4)
        G_mT = part(ring, 4 * P, RING)[0:HID + 1, :].rearrange("p (s u n) -> p s u n", s=2, u=2)

        def pairs(n):
            return part(ring, 4 * n, RING).rearrange("p (s u n) -> p s u n", s=2, u=2)

        G_t = pairs(2 * HID)
        G_n, G_u, G_v, G_d, G_e, G_m = (pairs(HID) for _ in range(6))
        G_c = pairs(HID + 1)
        G_in = part(ring, 8 * HID, RING).rearrange("p (s u n) -> p s u n", s=2, u=4)
        has = part(ring, NW, RING)
        rden = part(ring, NW, RING)
        tmp_w = part(ring, NW, RING)

        bank = [ctx.enter_context(nc.psum_tensor(f"bank{j}", [P, BANK], f32)) for j in range(8)]

        bank_b = [b[:, :].bitcast(bf16) for b in bank]

        def four(b, k):
            return b[:, 0:4 * k].rearrange("p (u k) -> p u k", u=4)

        def two(b, k):
            return b[:, 0:2 * k].rearrange("p (u k) -> p u k", u=2)

        block = ctx.enter_context(nc.Block())

        own = {e: sem(f"{e}_step") for e in ("dve", "pool")}
        turns = {e: sem(f"{e}_turns") for e in ("dve", "pool", "pe", "act")}
        w_split, w_out, w_back, at_sub = sem("w_split"), sem("w_out"), sem("w_back"), sem("at_sub")
        r_T, r_c = sem("r_T"), sem("r_c")
        a_rec, a_idx = sem("a_rec"), sem("a_idx")
        s_const, s_padded, s_ids, s_x, s_w, s_attr = (sem(f"s_{k}") for k in ("const", "padded", "ids", "x", "w", "attr"))
        s_wT, s_wcopied = sem("s_wT"), sem("s_wcopied")
        s_var, s_std, s_h = sem("s_var"), sem("s_std"), sem("s_h")
        s_kA, s_kB = sem("s_kA"), sem("s_kB")
        s_iotav = sem("s_iotav")
        s_cnt, s_tot, s_cc, s_start, s_nt, s_vstart, s_off, s_shift, s_vmask, s_vsum, s_vtab = (
            sem(f"s_{k}") for k in ("cnt", "tot", "cc", "start", "nt", "vstart", "off", "shift", "vmask", "vsum", "vtab"))
        s_before, s_flagp, s_flag = sem("s_before"), sem("s_flagp"), sem("s_flag")
        d_step, d_attr, d_ready, d_sc, d_free, d_sent, d_back, d_ids = (
            sem(f"d_{k}") for k in ("step", "attr", "ready", "sc", "free", "sent", "back", "ids"))
        t_st, a_g = sems("t_st", 2), sems("a_g", NS)
        b_in, b_sc, c_in = sems("b_in", NS), sems("b_sc", NS), sems("c_in", NS)
        at_in, at_st = sems("at_in", 2), sems("at_st", 2 * PARTS)
        at_T, at_cp, s_constb = sem("at_T"), sem("at_cp"), sem("s_constb")
        p_h, p_ones, p_T, p_Tc, p_mm, p_q, p_p, p_back = (sem(f"p_{k}") for k in ("h", "ones", "T", "Tc", "mm", "q", "p", "back"))
        p_st = sems("p_st", 2)
        t_h, t_T, t_Tc, t_mm, t_cp = (sem(f"t_{k}") for k in ("h", "T", "Tc", "mm", "cp"))
        g_in, n_in = sem("g0_in"), sem("g1_in")
        a_D, a_mm = sem("a_D"), sem("a_mm")
        a_acc, a_zero, a_done = sem("a_acc"), sem("a_zero"), sem("a_done")
        b_kl, b_D, b_pos, b_DT, b_DTc, b_hr, b_row = (sem(f"b_{k}") for k in ("kl", "D", "pos", "DT", "DTc", "hr", "row"))
        b_pad, b_padout, b_sent = sem("b_pad"), sem("b_padout"), sem("b_sent")
        c_add, c_mn, c_N, c_kl, c_S, c_St, c_STc, c_pre, c_sp, c_pt, c_pc, c_MKt, c_df, c_cr, c_mg, c_d, c_p, c_W, c_ag, c_acc = (
            sem(f"c_{k}") for k in ("add", "mn", "N", "kl", "S", "St", "STc", "pre", "sp", "pt", "pc", "MKt", "df", "cr", "mg", "d", "p", "W", "ag", "acc"))
        c_init, c_new, c_pen = sem("c_init"), sem("c_new"), sem("c_pen")
        g_T, g_Tc, g_mm, g_t, g_v, g_n, g_x = (sem(f"g0_{k}") for k in ("T", "Tc", "mm", "t", "v", "n", "x"))
        n_c, n_T, n_Tc, n_ms, n_msc, n_mm, n_t, n_v, n_n, n_x = (
            sem(f"g1_{k}") for k in ("c", "T", "Tc", "ms", "msc", "mm", "t", "v", "n", "x"))
        g_ones, n_ones, s_final = sem("g_ones"), sem("n_ones"), sem("s_final")
        N_CONST = 6
        N_CONSTB = 5
        N_CINIT = 6

        def turn(eng, name):
            eng.sem_inc(turns[name], 1)

        jobs = []
        em = edge_matrix.rearrange("t (m k) -> (t m) k", k=HID)
        for w, wT in ((em, AT), (w_ih0, wih0T), (w_hh0, whh0T), (w_lin, wlinT), (w_ih1, wih1T),
                      (w_hh1, whh1T), (w_att1[:, 0:HID], waT), (w_att1[:, HID:HID + ATTR], wattr),
                      (w_att1[:, HID + ATTR:H1], wbT)):
            n, c = w.shape
            for r in range(0, n, P):
                m = min(P, n - r)
                jobs.append((w[r:r + m, :], m, c, wT[0:c, r:r + m]))
        biases = [(b_ih0, wih0T), (b_hh0, whh0T), (b_lin, wlinT), (b_ih1, wih1T), (b_hh1, whh1T), (b_att1, waT)]
        WR = HID
        raw = [ring[0:m, WR * j:WR * j + c] for j, (_, m, c, _) in enumerate(jobs)]
        N_WDMA = len(jobs) + len(biases) + 2

        attrT_t = attrT_d.rearrange("(t k) p -> t k p", k=P)
        rows_t = rows_d.rearrange("(t p) k -> t p k", p=P)

        def tile_of(t, r):
            return t[ds(r, 1), :, :].rearrange("a p k -> (a p) k")

        def run_ticks(eng, tick, depth, ch=None, per=0):
            def body(i, slots, alive):
                for s in slots:
                    tick(i, s, {k: ((s - k) % NS, i if s >= k else i - 1) for k in range(depth) if alive(s, k)})

            def straight(i, slots, alive):
                body(i, slots, alive)
                if ch:
                    ch.base, ch.k = ch.base + ch.k, 0
            straight(0, range(NS), lambda s, k: s >= k)
            straight(1, range(NS), lambda s, k: True)
            if ch:
                ch.base -= 2 * per
            with eng.Fori(2, LOOPS) as i:
                if ch:
                    ch.body(i, per)
                body(i, range(NS), lambda s, k: True)
                if ch:
                    ch.end_body()
            if ch:
                ch.end_loop(LOOPS)
            straight(LOOPS, range(depth - 1), lambda s, k: s < k)

        def loop(eng, n, body, start=0):
            if start == 0:
                body(0)
                start = 1
            with eng.Fori(start, n) as i:
                body(i)

        def after(eng, s, t, j, back=0, slots=NS, incs=1):
            v = j * slots + (t + 1 - back)
            if not (isinstance(v, int) and v < 1):
                eng.wait_ge(s, v * incs)

        def after2(eng, s, t, j, back=0, incs=1):
            after(eng, s, t, j, back, 2, incs)

        @block.sync
        def _(sp):
            sp.wait_ge(s_padded, 5)
            for v, t in ((dst, dst_i), (src, src_i), (etype, typ_i)):
                sp.dma_start(t[0:P - 1, :], v[0:(P - 1) * COLS].rearrange("(p c) -> p c", c=COLS)).then_inc(s_ids, 16)
                sp.dma_start(t[P - 1:P, 0:LAST_COLS],
                             v[(P - 1) * COLS:N_EDGES].rearrange("(a c) -> a c", a=1)).then_inc(s_ids, 16)
            ends = dst[0:(P - 1) * COLS].rearrange("(p c) -> p c", c=COLS)[:, COLS - 1:COLS]
            sp.dma_start(before[1:P, :], ends, allow_slow_non_contiguous=True).then_inc(s_before, 16)
            whole = (N_WIN - 1) * P
            sp.dma_start(xs[:, 0:N_WIN - 1, :], x[0:whole, :].rearrange("(w p) f -> p w f", p=P)).then_inc(s_x, 16)
            sp.dma_start(xs[0:LAST_NODES, N_WIN - 1, :], x[whole:N_NODES, :]).then_inc(s_x, 16)
            for (w, _, _, _), r in zip(jobs, raw):
                sp.dma_start(r, w).then_inc(s_w, 16)
            for b, t in biases:
                sp.dma_start(t[HID:HID + 1, :], b.rearrange("(a n) -> a n", a=1)).then_inc(s_w, 16)
            sp.dma_start(w2bc[:, :], w_att2[0:1, :].to_broadcast([P, H1])).then_inc(s_w, 16)
            sp.dma_start(b2bc[:, :], b_att2.rearrange("(a n) -> a n", a=1).to_broadcast([P, 1])).then_inc(s_w, 16)
            sp.dma_start(attr_d[0:N_EDGES, :].rearrange("(a b) k -> a (b k)", a=500),
                         attr.rearrange("(a b) k -> a (b k)", a=500)).then_inc(s_attr, 16)
            sp.wait_ge(s_const, N_CONST)
            sp.dma_start(attr_d[N_EDGES:N_EDGES + 3 * P, :].rearrange("(p a) k -> p (a k)", a=3), zeros[:, :]).then_inc(s_attr, 16)
            sp.dma_start(attr_d[N_EDGES + 3 * P:SLOTS, :], zeros[0:N_PAD - 3 * P, 0:ATTR]).then_inc(s_attr, 16)
            table_w = table.rearrange("(w p t) m -> w p (t m)", p=P, t=TYPES)

            def store_table(i):
                for s in range(2):
                    after2(sp, t_cp, s, i)
                    sp.dma_start(tile_of(table_w, i * 2 + s), t_out[:, s, :]).then_inc(t_st[s], 16)
            loop(sp, NW // 2, store_table)

            sp.wait_ge(s_flag, 1)
            flag = sp.value_load(unsorted[0:1, 0:1], min_val=0, max_val=N_EDGES)
            with sp.If(flag > 0):
                sp.wait_ge(s_attr, 48)
                attr_p = attr_d.rearrange("(p c) k -> p c k", p=P)

                def load_attr(i):
                    if not first(i):
                        sp.wait_ge(d_free, i)
                    sp.dma_start(d_rows[:, :, 0:ATTR], attr_p[:, ds(i * SORT_COLS, SORT_COLS), :]).then_inc(d_attr, 16)
                loop(sp, COLS // SORT_COLS, load_attr)
                sp.wait_ge(d_sent, 1)
                sp.dma_start(attr_d[:, :], sorted_d[:, 0:ATTR]).then_inc(d_back, 16)
                sp.dma_start(kB_flat.rearrange("p (c k) -> p c k", k=IDS), sorted_d.rearrange("(p c) k -> p c k", p=P)[:, :, ATTR:SORT_ROW]).then_inc(d_ids, 16)
                sp.wait_ge(d_back, 16)

            sp.wait_ge(s_attr, 48)
            sp.wait_ge(s_vtab, 1)
            at_src = attr_d.rearrange("(b t p) k -> b p t k", t=AT_BLOCK, p=P)
            sp.wait_ge(w_split, 1)
            sp.dma_start(wpair_d[:, :], w_stage.rearrange("k c n -> k (c n)")).then_inc(w_out, 16)
            sp.wait_ge(w_out, 16)
            sp.dma_start(wpair[:, :], wpair_d.rearrange("k (c n) -> (k c) n", n=H1)).then_inc(w_back, 16)

            def load_blocks(i):
                for j in range(2):
                    if not first(i):
                        sp.wait_ge(at_T, i * 2 * PARTS)
                    sp.dma_start(A_at[:, j, :].rearrange("p (t k) -> p t k", k=ATTR),
                                 at_src[ds(i * 2 + j, 1)].rearrange("a p t k -> (a p) t k")).then_inc(at_in[j], 16)
            loop(sp, AT_LOOPS, load_blocks)

            def store_p(i):
                for s in range(2):
                    after2(sp, p_p, s, i)
                    sp.dma_start(p_d[:, ds((i * 2 + s) * 2 * H1, 2 * H1)], P_out[:, s, :, :].rearrange("p u k -> p (u k)")).then_inc(p_st[s], 16)

            sp.wait_ge(b_pad, 3)
            sp.dma_start(rows_d[N_EDGES:N_EDGES + 3 * P, :].rearrange("(p a) k -> p (a k)", a=3),
                         padrows.rearrange("p a k -> p (a k)")).then_inc(b_padout, 16)
            sp.dma_start(rows_d[N_EDGES + 3 * P:SLOTS, :], padrows[0:N_PAD - 3 * P, 0, :]).then_inc(b_padout, 16)
            loop(sp, G_LOOPS, store_p)
            for stored in at_st:
                sp.wait_ge(stored, 16 * AT_LOOPS)

            def load_attrT(i):
                for s in range(NS):
                    r = regs(ENG.SP, wtile, i * BODY + s * GV, TILES - 1)
                    if not first(i):
                        sp.wait_ge(b_sc[s], 16 * GV * i)
                    for u in range(GV):
                        sp.dma_start(B_at[:, s, u, :], tile_of(attrT_t, r[u])).then_inc(b_in[s], 16)
            loop(sp, LOOPS, load_attrT)

            sp.wait_ge(b_sent, 1)
            sp.wait_ge(b_padout, 32)
            for s in range(2):
                sp.wait_ge(p_st[s], 16 * G_LOOPS)
            sp.dma_start(big[:, :], p_d[:, :]).then_inc(p_back, 16)
            sp.wait_ge(s_vtab, 2)

            def load_rows(i):
                for s in range(NS):
                    r = regs(ENG.SP, wtile, i * BODY + s * GV, TILES - 1)
                    after(sp, c_W, s, i, NS)
                    for u in range(GV):
                        sp.dma_start(C_V[:, s, u, :], tile_of(rows_t, r[u])).then_inc(c_in[s], 16)
            loop(sp, LOOPS, load_rows)

            sp.wait_ge(n_x, 2 * G_LOOPS)
            sp.dma_start(out[0:whole, :].rearrange("(w p) f -> p w f", p=P), xs[:, 0:N_WIN - 1, :]).then_inc(s_final, 16)
            sp.dma_start(out[whole:N_NODES, :], xs[0:LAST_NODES, N_WIN - 1, :]).then_inc(s_final, 16)
            sp.wait_ge(s_final, 32)

        @block.gpsimd
        def _(pool):
            g = nc.gpsimd
            ch = Chain(pool, own["pool"])
            g.memset(zeros[:, :], 0.0).then_inc(s_const, 1)
            g.memset(ones[:, :], 1.0).then_inc(s_const, 1)
            ch.link(g.memset(ident[:, :], 0.0))
            g.memset(eps_t[:, :], EPS).then_inc(s_const, 1)
            g.iota(iota[:, :], pattern=[[1, P]], base=0, channel_multiplier=0,
                   allow_small_or_imprecise_dtypes=True).then_inc(s_const, 1)
            g.affine_select(out=ident[:, :], in_=ident[:, :], compare_op=ALU.not_equal, fill=1.0, base=0,
                            pattern=[[-1, P]], channel_multiplier=1).then_inc(s_const, 1)
            pool.wait_ge(s_const, 2)
            g.affine_select(out=tri[:, :], in_=ones[:, :], compare_op=ALU.is_gt, fill=0.0, base=0,
                            pattern=[[1, P]], channel_multiplier=-1).then_inc(s_const, 1)
            pool.wait_ge(s_wcopied, len(jobs))
            g.iota(iota_v, pattern=[[1, VISITS]], base=0, channel_multiplier=0,
                   allow_small_or_imprecise_dtypes=True).then_inc(s_iotav, 1)

            pool.wait_ge(s_h, 1)

            def copy_h(i):
                for s in range(2):
                    after2(pool, t_T, s, i, 2)
                    turn(pool, "pool")
                    g.tensor_copy(t_h1[:, s, :], h[:, ds(i * 2 + s, 1), :].rearrange("p a k -> p (a k)")).then_inc(t_h, 1)
            loop(pool, NW // 2, copy_h)

            pool.wait_ge(s_flag, 1)
            flag = pool.value_load(unsorted[0:1, 0:1], min_val=0, max_val=N_EDGES)
            with pool.If(flag > 0):
                def scatter(i):
                    pool.wait_ge(d_attr, 16 * (i + 1))
                    pool.wait_ge(d_ready, i + 1)
                    turn(pool, "pool")
                    for c in range(SORT_COLS):
                        g.indirect_dma_start(
                            out=sorted_d[:, :], out_offset=bass.IndirectOffsetOnAxis(ap=d_pos[:, c:c + 1], axis=0),
                            in_=d_rows[:, c, :], in_offset=None).then_inc(d_sc, 16)
                    pool.wait_ge(d_sc, 16 * SORT_COLS * (i + 1))
                    pool.sem_inc(d_free, 1)
                loop(pool, COLS // SORT_COLS, scatter)
                pool.wait_ge(d_free, COLS // SORT_COLS)
                pool.sem_inc(d_sent, 1)

            for s in range(2):
                pool.wait_ge(t_st[s], 16 * (NW // 2))
            pool.wait_ge(s_vtab, 1)

            def gather(i):
                for s in range(NS):
                    after(pool, a_mm, s, i, NS)
                    after(pool, a_idx, s, i)
                    turn(pool, "pool")
                    for u in range(GV):
                        g.indirect_dma_start(
                            out=A_g[:, s, u, :], out_offset=None, in_=table[:, :],
                            in_offset=bass.IndirectOffsetOnAxis(ap=A_idx[:, s, u:u + 1], axis=0)).then_inc(a_g[s], 16)
            loop(pool, LOOPS, gather)

            pool.wait_ge(a_done, 1)
            pool.wait_ge(g_ones, 1)

            def copy_in(i):
                for s in range(2):
                    w = ds(i * 4 + s * 2, 2)
                    after2(pool, g_T, s, i, 2)
                    turn(pool, "pool")
                    g.tensor_copy(G_in[:, s, 0:2, :], acc[:, w, 0:HID]).then_inc(g_in, 1)
                    g.tensor_copy(G_in[:, s, 2:4, :], h[:, w, :]).then_inc(g_in, 1)
            loop(pool, G_LOOPS, copy_in)

            pool.wait_ge(s_h, 2)

            def copy_h2(i):
                for s in range(2):
                    after2(pool, p_T, s, i, 2)
                    turn(pool, "pool")
                    g.tensor_copy(P_in[:, s, :, :], h[:, ds(i * 4 + s * 2, 2), :]).then_inc(p_h, 1)
            loop(pool, G_LOOPS, copy_h2)

            pool.wait_ge(b_padout, 32)

            def send(i):
                for s in range(NS):
                    after(pool, b_row, s, i, incs=2)
                    after(pool, b_pos, s, i, incs=2)
                    turn(pool, "pool")
                    for u in range(GV):
                        g.indirect_dma_start(
                            out=rows_d[:, :], out_offset=bass.IndirectOffsetOnAxis(ap=B_pos[:, s, u:u + 1], axis=0),
                            in_=B_row[:, s, u, :], in_offset=None, bounds_check=SLOTS - 1, oob_is_err=False).then_inc(b_sc[s], 16)
            loop(pool, LOOPS, send)
            for s in range(NS):
                pool.wait_ge(b_sc[s], 16 * GV * LOOPS)
            g.iota(iota_v, pattern=[[1, VISITS]], base=0, channel_multiplier=0,
                   allow_small_or_imprecise_dtypes=True).then_inc(s_iotav, 1)
            pool.sem_inc(b_sent, 1)

            pool.wait_ge(c_init, N_CINIT)
            pool.wait_ge(s_vtab, 2)

            def tick(i, s, stages):
                if 0 in stages:
                    n = i * BODY + s * GV
                    pool.wait_ge(c_in[s], 16 * GV * (i + 1))
                    after(pool, c_N, s, i, NS)
                    g.tensor_tensor(C_kl[:, s, :], C_V[:, s, :, ROW_SRC], wbase[:, ds(n, GV)], ALU.subtract).then_inc(c_kl, 1)
                    m_pen = ch.do(g.tensor_tensor(C_pen[:, s, :], wbase_all[:, ds(n, GV)], wbase[:, ds(n, GV)], ALU.subtract))
                if 3 in stages:
                    t, j = stages[3]
                    after(pool, c_p, t, j)
                    after(pool, c_ag, t, j, 2)
                    g.tensor_tensor(C_W[:, t % 2, :, :], C_V[:, t, :, H1:ROW_SRC],
                                    per_group(C_p[:, t, :], HID + 1), ALU.mult).then_inc(c_W, 1)
                if 0 in stages:
                    ch.need(m_pen)
                    g.tensor_tensor(C_pen[:, s, :], C_pen[:, s, :], C_step, ALU.mult).then_inc(c_pen, 1)
                if 2 in stages:
                    t, j = stages[2]
                    old, new = C_mn[:, t * GV:t * GV + GV], C_mn[:, 1 + t * GV:1 + t * GV + GV]
                    mp = [C_mp[:, t, :, k] for k in range(PARTS)]
                    after(pool, c_new, t, j)
                    after(pool, c_mg, t, j, NS)
                    m_hi = ch.do(g.tensor_tensor(mp[0], new, C_zero, ALU.add))
                    m_mo = ch.do(g.tensor_tensor(C_mo[:, t, :], old, C_pen[:, t, :], ALU.add))
                    ch.need(m_hi)
                    m_r = ch.do(g.tensor_tensor(C_mr[:, t, :], new, mp[0], ALU.subtract))
                    ch.need(m_mo)
                    after(pool, c_cr, t, j, NS)
                    g.tensor_tensor(C_df[:, t, :], C_mo[:, t, :], new, ALU.subtract).then_inc(c_df, 1)
                    ch.need(m_r)
                    ch.link(g.tensor_tensor(mp[1], C_mr[:, t, :], C_zero, ALU.add))
                    g.tensor_tensor(mp[2], C_mr[:, t, :], mp[1], ALU.subtract).then_inc(c_mn, 1)
            run_ticks(pool, tick, 5, ch, NS * (1 + 4))

            pool.wait_ge(n_ones, 1)

            def copy_h1(i):
                for s in range(2):
                    after2(pool, n_T, s, i, 2)
                    turn(pool, "pool")
                    g.tensor_copy(G_in[:, s, 2:4, :], h[:, ds(i * 4 + s * 2, 2), :]).then_inc(n_in, 1)
            loop(pool, G_LOOPS, copy_h1)

        @block.scalar
        def _(act):
            a = nc.scalar
            act.wait_ge(s_wT, len(jobs))
            for j, (_, m, c, wT) in enumerate(jobs):
                a.copy(wT, bank[j // 4][0:c, (j % 4) * P:(j % 4) * P + m]).then_inc(s_wcopied, 1)
            act.wait_ge(s_const, N_CONST)
            act.wait_ge(s_var, 1)
            a.activation(small[:, NW:2 * NW], small[:, 0:NW], ACT.Sqrt, bias=eps_t[:, :]).then_inc(s_std, 1)

            def table_copies(i):
                for s in range(2):
                    after2(act, t_T, s, i)
                    after2(act, t_mm, s, i, 2)
                    a.copy(t_hT[:, s, :], bank[s][0:HID, 0:P]).then_inc(t_Tc, 1)
                for s in range(2):
                    after2(act, t_mm, s, i)
                    if not first(i):
                        act.wait_ge(t_st[s], 16 * i)
                    a.copy(t_out[:, s, :], bank[2 + s][:, :]).then_inc(t_cp, 1)
            loop(act, NW // 2, table_copies)

            def copy_planes(n, recs, done):
                to = recs.rearrange("q (p j) k -> q k j p", j=BLOCKS)
                for k in range(n):
                    act.wait_ge(r_T, done + k + 1)
                    for m in range(0, BLOCKS, 4):
                        c = min(4, BLOCKS - m)
                        last = a.copy(to[:, k, m:m + c, :], four(bank[(k % 2) * 4 + m // 4], P)[:, 0:c])
                    last.then_inc(r_c, 1)
            for s in range(2):
                act.wait_ge(t_st[s], 16 * (NW // 2))
            copy_planes(REC0, recs0, 0)
            act.wait_ge(r_c, REC0)

            at_dst = attrT_d.rearrange("(b q c) p -> b q c p", q=P, c=len(PAIRS))

            def pick(i, k=None):
                for s in range(NS):
                    r = regs(ENG.Activation, wtile, i * BODY + s * GV, TILES - 1)
                    after(act, a_mm, s, i, NS)
                    turn(act, "act")
                    for u in range(GV):
                        last = a.copy(A_rec[:, s, u, :], recs0[:, ds(r[u], 1), :].rearrange("p a k -> p (a k)"))
                    last.then_inc(a_rec, 1)
                    after(act, a_rec, s, i)
                    a.copy(A_idx[:, s, :], A_rec[:, s, :, 1]).then_inc(a_idx, 1)
                    if k is not None and s < PARTS:
                        for j in range(2):
                            act.wait_ge(at_T, k * 2 * PARTS + 2 * s + j + 1)
                            if not first(k):
                                act.wait_ge(at_st[j * PARTS + s], 16 * k)
                            a.copy(A_atT[:, j, s, :], bank[6 + j][:, 0:P]).then_inc(at_cp, 1)
                        c = [n for n, pair in enumerate(PAIRS) if pair[0] == s]
                        for j in range(2):
                            act.wait_ge(at_cp, k * 2 * PARTS + 2 * s + j + 1)
                            act.dma_start(at_dst[ds(k * 2 + j, 1), :, c[0]:c[-1] + 1, :].rearrange("b q c p -> (b q) c p"),
                                          A_atT[:, j, s, :].unsqueeze(1).to_broadcast([P, len(c), P])).then_inc(at_st[j * PARTS + s], 16)
            pick(0)
            pick(1, 0)
            with act.Fori(2, AT_LOOPS + 1) as i:
                pick(i, i - 1)
            with act.Fori(AT_LOOPS + 1, LOOPS) as i:
                pick(i)

            act.wait_ge(g_ones, 1)

            def update0(i):
                for s in range(2):
                    after2(act, g_T, s, i)
                    after2(act, g_mm, s, i, 2)
                    a.copy(G_T[0:HID, s, :, :], four(bank[s], P)[0:HID]).then_inc(g_Tc, 1)
                for s in range(2):
                    after2(act, g_mm, s, i)
                    after2(act, g_x, s, i, 2)
                    a.activation(G_t[:, s, :, :], two(bank[2 + s], 4 * HID)[:, :, 0:2 * HID], ACT.Tanh, scale=0.5).then_inc(g_t, 1)
                    after2(act, g_v, s, i)
                    a.activation(G_n[:, s, :, :], G_v[:, s, :, :], ACT.Tanh).then_inc(g_n, 1)
            loop(act, G_LOOPS, update0)
            act.wait_ge(s_var, 2)
            a.activation(small[:, NW:2 * NW], small[:, 0:NW], ACT.Sqrt, bias=eps_t[:, :]).then_inc(s_std, 1)

            act.wait_ge(p_ones, 1)
            copy_planes(REC1, recs1, REC0)

            def tables1(i):
                for s in range(2):
                    after2(act, p_T, s, i)
                    after2(act, p_mm, s, i, 2)
                    a.copy(P_hT[0:HID, s, :, :], two(bank[s], P)[0:HID]).then_inc(p_Tc, 1)
                for s in range(2):
                    after2(act, p_mm, s, i)
                    a.copy(q_tab[:, ds(i * 4 + s * 2, 2), :], two(bank[4 + s], H1)).then_inc(p_q, 1)
            loop(act, G_LOOPS, tables1)

            act.wait_ge(b_pad, 3)

            def rows(i, s, stages):
                if 0 in stages:
                    after(act, b_DT, s, i)
                    after(act, b_hr, s, i, NS)
                    a.copy(B_DT[:, s, :, :], four(bank_b[s % 2], P)).then_inc(b_DTc, 1)
                if 1 in stages:
                    t, j = stages[1]
                    after(act, b_hr, t, j)
                    if not first(j):
                        act.wait_ge(b_sc[t], 16 * GV * j)
                    for half in range(2):
                        a.copy(B_row[:, t, 2 * half:2 * half + 2, 0:ROW_ONE],
                               two(bank[2 + 2 * (t % 2) + half], ROW_ONE)).then_inc(b_row, 1)
            run_ticks(act, rows, 2)

            act.wait_ge(s_vtab, 2)

            def tick(i, s, stages):
                if 2 in stages:
                    t, j = stages[2]
                    after(act, c_pt, t, j)
                    after(act, c_MKt, t, j, 2)
                    a.copy(C_PT[:, t % 2, :], bank_b[1][0:PARTS * GV, 0:P]).then_inc(c_pc, 1)
                if 3 in stages:
                    t, j = stages[3]
                    after(act, c_d, t, j)
                    after(act, c_W, t, j, NS)
                    a.activation(C_p[:, t, :], C_d[:, t, :], ACT.Exp).then_inc(c_p, 1)
                if 0 in stages:
                    after(act, c_St, s, i)
                    after(act, c_mg, s, i, NS)
                    a.activation(C_ST[:, s, :, :], four(bank_b[0], P), ACT.Identity, bias=ones[:, 0:1], scale=-1.0).then_inc(c_STc, 1)
                    a.activation(C_STb[:, s, :, :], four(bank_b[0], P), ACT.Identity, bias=ones[:, 0:1], scale=-1.0).then_inc(c_STc, 1)
                    after(act, c_ag, s, i, NS)
                    a.activation(C_S[:, s, :, :], C_N[:, s, :, :], ACT.Identity, bias=ones[:, 0:1], scale=-1.0).then_inc(c_S, 1)
                if 2 in stages:
                    t, j = stages[2]
                    after(act, c_df, t, j)
                    after(act, c_acc, t, j, NS)
                    a.activation(C_cr[:, t, :], C_df[:, t, :], ACT.Exp).then_inc(c_cr, 1)
            run_ticks(act, tick, 5)

            act.wait_ge(n_ones, 1)

            def update1(i):
                for s in range(2):
                    after2(act, n_T, s, i)
                    after2(act, n_mm, s, i, 2)
                    a.copy(G_T[0:HID + 1, s, 0:2, :], four(bank[s], P)[0:HID + 1, 0:2]).then_inc(n_Tc, 1)
                    a.copy(G_T[0:HID, s, 2:4, :], four(bank[s], P)[0:HID, 2:4]).then_inc(n_Tc, 1)
                for s in range(2):
                    after2(act, n_ms, s, i)
                    after2(act, n_x, s, i, 2)
                    a.copy(G_m[:, s, :, :], two(bank[4 + s], HID)).then_inc(n_msc, 1)
                    a.copy(G_mT[0:HID, s, :, :], two(bank[4 + s][:, 2 * P:4 * P], P)[0:HID]).then_inc(n_msc, 1)
                for s in range(2):
                    after2(act, n_mm, s, i)
                    a.activation(G_t[:, s, :, :], two(bank[2 + s], 4 * HID)[:, :, 0:2 * HID], ACT.Tanh, scale=0.5).then_inc(n_t, 1)
                    after2(act, n_v, s, i)
                    a.activation(G_n[:, s, :, :], G_v[:, s, :, :], ACT.Tanh).then_inc(n_n, 1)
            loop(act, G_LOOPS, update1)

        @block.tensor
        def _(pe):
            mm = nc.tensor.matmul
            tr = nc.tensor.transpose
            pe.wait_ge(s_const, N_CONST)
            pe.wait_ge(s_w, 16 * N_WDMA)
            for j, ((_, m, c, _), r) in enumerate(zip(jobs, raw)):
                tr(bank[j // 4][0:c, (j % 4) * P:(j % 4) * P + m], r, ident[0:m, 0:m]).then_inc(s_wT, 1)

            pe.wait_ge(s_wcopied, len(jobs))
            pe.wait_ge(s_h, 1)

            def make_table(i):
                for s in range(2):
                    after2(pe, t_Tc, s, i, 2)
                    after2(pe, t_h, s, i)
                    turn(pe, "pe")
                    tr(bank[s][0:HID, 0:P], t_h1[:, s, :], ident[:, :]).then_inc(t_T, 1)
                for s in range(2):
                    after2(pe, t_Tc, s, i)
                    after2(pe, t_cp, s, i, 2)
                    mm(bank[2 + s][:, :], t_hT[:, s, :], AT[:, :], start=True, stop=True).then_inc(t_mm, 1)
            loop(pe, NW // 2, make_table)

            def visit_counts(k):
                pe.wait_ge(s_cnt, k + 1)
                mm(bank[4][:, 0:N_KEYS], ones[:, :], cnt[:, :], start=True, stop=True)
                mm(bank[4][:, P:P + N_KEYS], tri[:, :], cnt[:, :], start=True, stop=True)
                if k == 0:
                    pe.wait_ge(s_flagp, 1)
                    mm(bank[4][0:1, 3 * P:3 * P + 1], out_of_order[:, :], ones[:, 0:1], start=True, stop=True)
                mm(bank[4][0:N_KEYS, 2 * P:2 * P + 1], cnt[:, :], ones[:, 0:1], start=True, stop=True).then_inc(s_tot, 1)

            def visit_tables(k):
                K = N_KEYS
                pe.wait_ge(s_cc, k + 1)
                mm(bank[5][0:K, 0:1], tri[0:K, 0:K], cc[k][0:K, :], start=True, stop=True).then_inc(s_start, 1)
                pe.wait_ge(s_nt, k + 1)
                mm(bank[5][0:K, 1:2], tri[0:K, 0:K], nt[0:K, :], start=True, stop=True).then_inc(s_vstart, 1)
                pe.wait_ge(s_off, k + 1)
                mm(bank[5][0:HW, 2:3], ident[0:N_WIN, 1:N_WIN], off[0:N_WIN, :], start=True, stop=True).then_inc(s_shift, 1)
                pe.wait_ge(s_vmask, k + 1)
                for q in range(4):
                    m = vmask[0:HW, q * VCHUNK:(q + 1) * VCHUNK]
                    mm(bank[q][:, 0:VCHUNK], ones[0:HW, :], m, start=True, stop=True)
                    last = mm(bank[4 + q][:, 0:VCHUNK], dbc[0:HW, :], m, start=True, stop=True)
                last.then_inc(s_vsum, 1)

            pe.wait_ge(t_cp, NW)
            visit_counts(0)
            visit_tables(0)

            def turn_planes(n, done):
                for k in range(n):
                    if k >= 2:
                        pe.wait_ge(r_c, done + k - 1)
                    for j in range(BLOCKS):
                        last = tr(bank[(k % 2) * 4 + j // 4][:, (j % 4) * P:(j % 4 + 1) * P], planes[k][:, j * P:(j + 1) * P], ident[:, :])
                    last.then_inc(r_T, 1)

            pe.wait_ge(s_vtab, 1)
            pe.wait_ge(s_kA, REC0)
            turn_planes(REC0, 0)

            pe.wait_ge(r_c, REC0)
            pe.wait_ge(s_constb, N_CONSTB)
            pe.wait_ge(a_zero, 1)

            def turn_blocks(i, a):
                for j in range(2):
                    if a == 0:
                        pe.wait_ge(at_in[j], 16 * (i + 1))
                    if not (first(i) and a == 0):
                        pe.wait_ge(at_cp, i * 2 * PARTS + 2 * (a - 1) + j + 1)
                    last = mm(bank[6 + j][:, 0:P], A_at[:, j, :], ident[:, :], start=True, stop=a == 0)
                    for b in range(a):
                        last = mm(bank[6 + j][:, 0:P], minus_b[:, :], A_atT[:, j, b, :], start=False, stop=b == a - 1)
                    last.then_inc(at_T, 1)

            def sums0(i, blocks=False):
                for s in range(NS):
                    if blocks and s < PARTS:
                        turn_blocks(i, s)
                    after(pe, a_D, s, i)
                    if not first(i):
                        pe.wait_ge(a_acc, BODY * (i - 1) + GV * (s + 1))
                    pe.wait_ge(a_g[s], 16 * GV * (i + 1))
                    for u in range(GV):
                        last = mm(bank[s][:, u * HID:(u + 1) * HID], A_D[:, s, u, :], A_g[:, s, u, :], start=True, stop=True)
                    last.then_inc(a_mm, 1)
            def sums_and_turns(i):
                sums0(i, True)
            loop(pe, COUNT_LOOPS, sums_and_turns)
            visit_counts(1)
            with pe.Fori(COUNT_LOOPS, AT_LOOPS) as i:
                sums_and_turns(i)
            with pe.Fori(AT_LOOPS, LOOPS) as i:
                sums0(i)

            pe.wait_ge(a_done, 1)
            pe.wait_ge(g_ones, 1)

            def update0(i):
                for s in range(2):
                    after2(pe, g_Tc, s, i, 2)
                    after2(pe, g_in, s, i, incs=2)
                    turn(pe, "pe")
                    for u in range(4):
                        last = tr(bank[s][0:HID, u * P:(u + 1) * P], G_in[:, s, u, :], ident[:, :])
                    last.then_inc(g_T, 1)
                for s in range(2):
                    after2(pe, g_Tc, s, i)
                    after2(pe, g_x, s, i, 2)
                    for u in range(2):
                        b = bank[2 + s][:, u * 4 * HID:(u + 1) * 4 * HID]
                        mm(b[:, 0:GATES], G_T[:, s, u, :], wih0T[:, :], start=True, stop=False)
                        mm(b[:, 0:2 * HID], G_T[:, s, 2 + u, :], whh0T[:, 0:2 * HID], start=False, stop=False)
                        last = mm(b[:, GATES:4 * HID], G_T[:, s, 2 + u, :], whh0T[:, 2 * HID:GATES], start=False, stop=True)
                    last.then_inc(g_mm, 1)
            loop(pe, G_LOOPS, update0)

            pe.wait_ge(s_kB, 1)
            pe.wait_ge(p_ones, 1)
            turn_planes(REC1, REC0)
            pe.wait_ge(r_c, REC0 + REC1)


            def tables1(i):
                for s in range(2):
                    after2(pe, p_Tc, s, i, 2)
                    after2(pe, p_h, s, i)
                    turn(pe, "pe")
                    for u in range(2):
                        last = tr(bank[s][0:HID, u * P:(u + 1) * P], P_in[:, s, u, :], ident[:, :])
                    last.then_inc(p_T, 1)
                for s in range(2):
                    after2(pe, p_Tc, s, i)
                    after2(pe, p_q, s, i, 2)
                    after2(pe, p_p, s, i, 2)
                    for u in range(2):
                        mm(bank[2 + s][:, u * H1:(u + 1) * H1], P_hT[:, s, u, :], waT[:, :], start=True, stop=True)
                        last = mm(bank[4 + s][:, u * H1:(u + 1) * H1], P_hT[:, s, u, :], wbT[:, :], start=True, stop=True)
                    last.then_inc(p_mm, 1)
            loop(pe, G_LOOPS, tables1)

            pe.wait_ge(p_q, 2 * G_LOOPS)
            pe.wait_ge(p_p, 2 * G_LOOPS)
            pe.wait_ge(w_back, 16)

            def rows(i, s, stages):
                if 0 in stages:
                    after(pe, b_D, s, i)
                    after(pe, b_DTc, s, i, 2)
                    for u in range(GV):
                        last = tr(bank_b[s % 2][:, u * P:(u + 1) * P], B_D[:, s, u, :], ident_b[:, :])
                    last.then_inc(b_DT, 1)
                if 1 in stages:
                    t, j = stages[1]
                    r = regs(ENG.PE, wwin, j * BODY + t * GV, N_WIN - 1)
                    pe.wait_ge(b_in[t], 16 * GV * (j + 1))
                    after(pe, b_DTc, t, j)
                    after(pe, b_row, t, j, 2, incs=2)
                    for u in range(GV):
                        b = bank[2 + 2 * (t % 2) + u // 2][:, (u % 2) * ROW_ONE:(u % 2 + 1) * ROW_ONE]
                        w = ds(r[u], 1)
                        mm(b[:, 0:H1], B_DT[:, t, u, :], q_tab[:, w, :].rearrange("p a k -> p (a k)"), start=True, stop=False)
                        mm(b[:, 0:H1], B_at[:, t, u, :], wpair[:, :], start=False, stop=True)
                        last = mm(b[:, H1:ROW_ONE], B_DT[:, t, u, :], h[:, w, :].rearrange("p a k -> p (a k)"), start=True, stop=True)
                    last.then_inc(b_hr, 1)
            run_ticks(pe, rows, 2)
            pe.wait_ge(b_row, 2 * NS * LOOPS)
            visit_tables(1)

            pe.wait_ge(s_vtab, 2)
            pe.wait_ge(p_back, 16)
            pe.wait_ge(c_init, N_CINIT)

            def tick(i, s, stages):
                if 1 in stages:
                    t1, j1 = stages[1]
                    r = regs(ENG.PE, wwin, j1 * BODY + t1 * GV, N_WIN - 1)

                    def source_part(u):
                        b = bank[2 + u // 2][:, (u % 2) * H1:(u % 2 + 1) * H1]
                        return mm(b, C_ST[:, t1, u, :], p_tab[:, ds(r[u], 1), :].rearrange("p a k -> p (a k)"), start=True, stop=True)
                    after(pe, c_STc, t1, j1, incs=2)
                    after(pe, c_add, t1, j1, 1, incs=2)
                    for u in range(GV - 1):
                        source_part(u)
                if 3 in stages:
                    t, j = stages[3]
                    after(pe, c_mn, t, j)
                    after(pe, c_d, t, j, 1)
                    for u in range(GV):
                        last = mm(bank[5][:, u * PARTS:(u + 1) * PARTS], C_STb[:, t, u, :], C_mp[:, t, u, :], start=True, stop=True)
                    last.then_inc(c_mg, 1)
                if 2 in stages:
                    t, j = stages[2]
                    after(pe, c_sp, t, j)
                    after(pe, c_pc, t, j, 1)
                    turn(pe, "pe")
                    tr(bank_b[1][0:PARTS * GV, 0:P], C_parts[:, t, :], ident_b[:, :]).then_inc(c_pt, 1)
                if 1 in stages:
                    source_part(GV - 1).then_inc(c_pre, 1)
                if 2 in stages:
                    t, j = stages[2]
                    after(pe, c_pc, t, j)
                    after(pe, c_new, t, j, 1)
                    turn(pe, "pe")
                    for u in range(GV):
                        b = bank[4][:, u * P:(u + 1) * P]
                        mm(b, C_N[:, t, u, :], big_b[:, :], start=True, stop=False)
                        last = mm(b, sel[:, u * P:(u + 1) * P], C_PT[:, t % 2, :], start=False, stop=True)
                    last.then_inc(c_MKt, 1)
                if 0 in stages:
                    after(pe, c_N, s, i)
                    after(pe, c_STc, s, i, 1, incs=2)
                    for u in range(GV):
                        last = tr(bank_b[0][:, u * P:(u + 1) * P], C_N[:, s, u, :], ident_b[:, :])
                    last.then_inc(c_St, 1)
                if 3 in stages:
                    t, j = stages[3]
                    after(pe, c_W, t, j)
                    after(pe, c_acc, t, j, 2)
                    after(pe, c_S, t, j)
                    for u in range(GV):
                        last = mm(bank[6 + t % 2][:, u * (HID + 1):(u + 1) * (HID + 1)], C_S[:, t, u, :], C_W[:, t % 2, u, :],
                                  start=True, stop=True)
                    last.then_inc(c_ag, 1)
            run_ticks(pe, tick, 5)

            pe.wait_ge(n_ones, 1)

            def update1(i):
                for s in range(2):
                    after2(pe, n_c, s, i)
                    after2(pe, n_Tc, s, i, 2, incs=2)
                    after2(pe, n_in, s, i)
                    turn(pe, "pe")
                    for u in range(2):
                        tr(bank[s][0:HID + 1, u * P:(u + 1) * P], G_c[:, s, u, :], ident[:, :])
                        last = tr(bank[s][0:HID, (2 + u) * P:(3 + u) * P], G_in[:, s, 2 + u, :], ident[:, :])
                    last.then_inc(n_T, 1)
                for s in range(2):
                    after2(pe, n_Tc, s, i, incs=2)
                    after2(pe, n_msc, s, i, 2, incs=2)
                    for u in range(2):
                        mm(bank[4 + s][:, u * HID:(u + 1) * HID], G_T[:, s, u, :], wlinT[:, :], start=True, stop=True)
                        last = mm(bank[4 + s][0:HID, (2 + u) * P:(3 + u) * P], wlinT[:, :], G_T[:, s, u, :], start=True, stop=True)
                    last.then_inc(n_ms, 1)
                for s in range(2):
                    after2(pe, n_msc, s, i, incs=2)
                    after2(pe, n_x, s, i, 2)
                    for u in range(2):
                        b = bank[2 + s][:, u * 4 * HID:(u + 1) * 4 * HID]
                        mm(b[:, 0:GATES], G_T[:, s, 2 + u, :], wih1T[:, :], start=True, stop=False)
                        mm(b[:, 0:2 * HID], G_mT[:, s, u, :], whh1T[:, 0:2 * HID], start=False, stop=False)
                        last = mm(b[:, GATES:4 * HID], G_mT[:, s, u, :], whh1T[:, 2 * HID:GATES], start=False, stop=True)
                    last.then_inc(n_mm, 1)
            loop(pe, G_LOOPS, update1)

        @block.vector
        def _(dve):
            v = nc.vector
            ch = Chain(dve, own["dve"])
            lo = P - 32
            for t, val in ((dst_i, PAD_KEY), (src_i, PAD_KEY), (typ_i, 0)):
                v.memset(t[lo:P, LAST_COLS:COLS], val).then_inc(s_padded, 1)
            v.memset(xs[:, N_WIN - 1:NW, :], 0.0).then_inc(s_padded, 1)
            v.memset(before[:, :], 0).then_inc(s_padded, 1)

            dve.wait_ge(s_ids, 96)
            dve.wait_ge(s_padded, 5)
            ch.link(v.tensor_scalar(scan.bitcast(i32), dst_i, 7, None, ALU.arith_shift_right))
            ch.link(v.tensor_copy(win, scan.bitcast(i32)))

            dve.wait_ge(s_before, 16)
            ch.link(v.tensor_tensor(scan[:, 0:1], dst_i[:, 0:1], before[:, :], ALU.is_lt))
            ch.link(v.tensor_tensor(scan[:, 1:COLS], dst_i[:, 1:COLS], dst_i[:, 0:COLS - 1], ALU.is_lt))
            v.tensor_reduce(out_of_order[:, :], scan, AX.X, ALU.add).then_inc(s_flagp, 1)

            def normalise(k):
                flat = NW * HID
                sq = acc[:, :, :].rearrange("p w k -> p (w k)")[:, 0:flat].rearrange("p (w k) -> p w k", k=HID)
                var, std, mean = small[:, 0:NW], small[:, NW:2 * NW], small[:, 2 * NW:3 * NW]

                def bc(t):
                    return t.unsqueeze(2).to_broadcast([P, NW, HID])
                ch.link(v.tensor_reduce(mean, xs[:, :, :], AX.X, ALU.add))
                ch.link(v.tensor_scalar(mean, mean, 1.0 / HID, None, ALU.mult))
                ch.link(v.tensor_tensor(h[:, :, :], xs[:, :, :], bc(mean), ALU.subtract))
                ch.link(v.tensor_tensor(sq, h[:, :, :], h[:, :, :], ALU.mult))
                ch.link(v.tensor_reduce(var, sq, AX.X, ALU.add))
                v.tensor_scalar(var, var, 1.0 / HID, None, ALU.mult).then_inc(s_var, 1)
                dve.wait_ge(s_std, k)
                ch.link(v.reciprocal(std, std))
                ch.link(v.tensor_tensor(h[:, :, :], h[:, :, :], bc(std), ALU.mult))
                v.tensor_scalar(h[:, :, :], h[:, :, :], 0.0, None, ALU.max).then_inc(s_h, 1)

            dve.wait_ge(s_x, 32)
            normalise(1)

            def count(w):
                ch.link(v.tensor_scalar(mask, win, iota[:, ds(w, 1)], None, ALU.is_equal, ALU.add, accum_out=cnt[:, ds(w, 1)]))

            dve.wait_ge(s_const, N_CONST)
            v.memset(wbT[HID:HID + 1, :], 0.0).then_inc(s_constb, 1)
            v.tensor_copy(iota_b[:, :], iota[:, :]).then_inc(s_constb, 1)
            v.tensor_copy(ident_b[:, :], ident[:, :]).then_inc(s_constb, 1)
            v.tensor_scalar(big_b[:, :], ident[:, :], -MASKED, None, ALU.mult).then_inc(s_constb, 1)
            v.tensor_scalar(minus_b[:, :], ident[:, :], -1.0, None, ALU.mult).then_inc(s_constb, 1)
            dve.wait_ge(s_wcopied, len(jobs))
            ch.link(v.tensor_copy(w_parts[:, 0, :], wattr[:, :]))
            ch.link(v.tensor_tensor(w_rest, wattr[:, :], w_parts[:, 0, :], ALU.subtract))
            ch.link(v.tensor_copy(w_parts[:, 1, :], w_rest))
            ch.link(v.tensor_tensor(w_parts[:, 2, :], w_rest, w_parts[:, 1, :], ALU.subtract))
            for c, (_, w) in enumerate(PAIRS):
                m = v.tensor_copy(w_stage[:, c, :], w_parts[:, w, :])
            m.then_inc(w_split, 1)
            pr = PARTS * GV
            ch.link(v.tensor_tensor(sel_a[:, :], ident[0:pr, 0:GV], ident[0:pr, GV:2 * GV], ALU.add))
            ch.link(v.tensor_tensor(sel_a[:, :], sel_a[:, :], ident[0:pr, 2 * GV:3 * GV], ALU.add))
            with dve.Fori(0, N_KEYS // 2) as i:
                ch.body(i, 2)
                count(i * 2)
                count(i * 2 + 1)
                ch.end_body()
            ch.end_loop(N_KEYS // 2)
            dve.sem_inc(s_cnt, 1)

            K = N_KEYS

            def totals(k):
                dve.wait_ge(s_tot, k + 1)
                v.tensor_copy(cc[k][0:K, :], bank[4][0:K, 2 * P:2 * P + 1]).then_inc(s_cc, 1)
                tot, incl = small[:, 3 * P:3 * P + K], small[:, 2 * P:2 * P + K]
                ch.link(v.tensor_copy(tot, bank[4][:, 0:K]))
                ch.link(v.tensor_tensor_scan(incl, tot, tot, 0.0, ALU.add, ALU.max))
                ch.link(v.tensor_tensor(incl, incl, tot, ALU.subtract))
                ch.link(v.tensor_tensor(place0[:, :], incl, bank[4][:, P:P + K], ALU.add))
                if k == 0:
                    v.tensor_copy(unsorted[:, :], bank[4][0:1, 3 * P:3 * P + 1]).then_inc(s_flag, 1)

            def visit_table(k):
                e = [small[0:K, j:j + 1] for j in range(20, 30)]
                start, end, ft, lt, hs, vend, t1 = e[0:7]
                si, ei = e[7].bitcast(i32), e[8].bitcast(i32)
                dve.wait_ge(s_start, k + 1)
                ch.link(v.tensor_copy(start, bank[5][0:K, 0:1]))
                ch.link(v.tensor_tensor(end, start, cc[k][0:K, :], ALU.add))
                ch.link(v.tensor_copy(si, start))
                ch.link(v.tensor_scalar(ei, end, -1.0, None, ALU.add))
                ch.link(v.tensor_scalar(si, si, 7, None, ALU.arith_shift_right))
                ch.link(v.tensor_scalar(ei, ei, 7, None, ALU.arith_shift_right))
                ch.link(v.tensor_copy(ft, si))
                ch.link(v.tensor_copy(lt, ei))
                ch.link(v.scalar_tensor_tensor(t1, lt, 1.0, ft, ALU.add, ALU.subtract))
                ch.link(v.tensor_scalar(hs, cc[k][0:K, :], 0.0, None, ALU.is_gt))
                v.tensor_tensor(nt[0:K, :], t1, hs, ALU.mult).then_inc(s_nt, 1)
                dve.wait_ge(s_vstart, k + 1)
                ch.link(v.tensor_tensor(vend, nt[0:K, :], bank[5][0:K, 1:2], ALU.add))
                v.tensor_tensor(off[0:K, :], ft, bank[5][0:K, 1:2], ALU.subtract).then_inc(s_off, 1)
                dve.wait_ge(s_shift, k + 1)
                ch.link(v.tensor_tensor(t1[0:HW], bank[5][0:HW, 2:3], off[0:HW, :], ALU.subtract))
                ch.link(v.tensor_scalar(dbc[0:HW, :], ones[0:HW, :], t1[0:HW], None, ALU.mult))
                dve.wait_ge(s_iotav, k + 1)
                v.tensor_scalar(vmask[0:HW, :], iota_v[0:HW, :], vend[0:HW], None, ALU.is_ge).then_inc(s_vmask, 1)
                dve.wait_ge(s_vsum, k + 1)
                for q in range(4):
                    c = slice(q * VCHUNK, (q + 1) * VCHUNK)
                    ch.do(v.tensor_scalar(wbase[:, c], bank[q][:, 0:VCHUNK], float(P), None, ALU.mult))
                    ch.do(v.tensor_copy(wwin[0:1, c], bank[q][0:1, 0:VCHUNK]))
                    ch.link(v.tensor_tensor(iota_v[0:1, c], iota_v[0:1, c], bank[4 + q][0:1, 0:VCHUNK], ALU.add))
                    ch.link(v.tensor_scalar(wtile[0:1, c], iota_v[0:1, c], float(TILES - 1), None, ALU.min))
                dve.sem_inc(s_vtab, 1)

            totals(0)
            visit_table(0)

            def place(w, where, ch):
                ch.link(v.tensor_scalar(mask, win, iota[:, ds(w, 1)], None, ALU.is_equal))
                ch.link(v.tensor_tensor_scan(scan, mask, mask, place0[:, ds(w, 1)], ALU.add, ALU.max))
                turn(dve, "dve")
                ch.link(v.copy_predicated(where, mask.bitcast(u16), scan))

            dve.wait_ge(s_flag, 1)
            flag = dve.value_load(unsorted[0:1, 0:1], min_val=0, max_val=N_EDGES)
            with dve.If(flag > 0):
                dch = Chain(dve, d_step)
                dch.link(v.memset(d_place, 0.0))
                with dve.Fori(0, N_KEYS) as w:
                    dch.body(w, 3)
                    place(w, d_place, dch)
                    dch.end_body()
                dch.end_loop(N_KEYS)

                def stage(i):
                    dch.body(i, 3)
                    if not first(i):
                        dve.wait_ge(d_free, i)
                    c = ds(i * SORT_COLS, SORT_COLS)
                    for k, t in enumerate((dst_i, src_i, typ_i)):
                        dch.link(v.tensor_copy(d_rows[:, :, ATTR + k].bitcast(i32), t[:, c]))
                    v.tensor_scalar(d_pos, d_place[:, c], -1.0, None, ALU.add).then_inc(d_ready, 1)
                    dch.end_body()
                dch.link(v.memset(d_rows[:, :, SORT_ROW - 1], 0.0))
                loop(dve, COLS // SORT_COLS, stage)
                dch.end_loop(COLS // SORT_COLS)
                dve.wait_ge(d_ids, 16)
                ids = kB_flat.bitcast(i32).rearrange("p (c k) -> p c k", k=IDS)
                for k, t in enumerate((dst_i, src_i, scan.bitcast(i32))):
                    dch.link(v.tensor_copy(t, ids[:, :, k]))
                dch.link(v.tensor_copy(typ_i, scan.bitcast(i32)))

            v.tensor_copy(dst_f, dst_i).then_inc(s_kA, 1)
            v.scalar_tensor_tensor(row_f, src_i, float(TYPES), typ_i, ALU.mult, ALU.add).then_inc(s_kA, 1)

            dve.wait_ge(r_T, REC0)
            ch.do(v.tensor_copy(src_f, src_i))
            ch.link(v.memset(place_f, 0.0))
            ch.link(v.tensor_scalar(scan.bitcast(i32), src_i, 7, None, ALU.arith_shift_right))
            ch.link(v.tensor_copy(win, scan.bitcast(i32)))
            v.memset(acc[:, :, :], 0.0).then_inc(a_zero, 1)
            dve.wait_ge(a_zero, 1)
            for s in range(2):
                dve.wait_ge(t_st[s], 16 * (NW // 2))

            def add0(i, s):
                r = regs(ENG.DVE, wwin, i * BODY + s * GV, N_WIN - 1)
                after(dve, a_mm, s, i)
                for u in range(GV):
                    if not (first(i) and s == 0 and u == 0):
                        dve.wait_ge(a_acc, i * BODY + s * GV + u)
                    t = acc[:, ds(r[u], 1), 0:HID].rearrange("p a k -> p (a k)")
                    v.tensor_tensor(t, t, bank[s][:, u * HID:(u + 1) * HID], ALU.add).then_inc(a_acc, 1)

            def sums0(i, extra, steps):
                ch.body(i, NS + steps)
                for s in range(NS):
                    after(dve, a_rec, s, i)
                    after(dve, a_mm, s, i, NS)
                    ch.link(v.tensor_tensor(A_kl[:, s, :], A_rec[:, s, :, 0], wbase[:, ds(i * BODY + s * GV, GV)], ALU.subtract))
                    v.tensor_tensor(A_D[:, s, :, :], iota[:, :].unsqueeze(1).to_broadcast([P, GV, P]),
                                    per_group(A_kl[:, s, :], P), ALU.is_equal).then_inc(a_D, 1)
                    if s in (0, 2) and extra:
                        extra(i, s // 2)
                    if s:
                        add0(i, s - 1)
                    elif not first(i):
                        add0(i - 1, NS - 1)
                ch.end_body()

            loop(dve, COUNT_LOOPS, lambda i: sums0(i, lambda i, j: count(i * 2 + j), 2))
            ch.end_loop(COUNT_LOOPS)
            ch.per = 0
            dve.sem_inc(s_cnt, 1)
            totals(1)
            ch.base += ch.k
            ch.k = 0
            ch.base -= COUNT_LOOPS * (NS + 6)
            with dve.Fori(COUNT_LOOPS, COUNT_LOOPS + PLACE_LOOPS) as i:
                sums0(i, lambda i, j: place((i - COUNT_LOOPS) * 2 + j, place_f, ch), 6)
            ch.base += (COUNT_LOOPS + PLACE_LOOPS) * (NS + 6)
            ch.base -= (COUNT_LOOPS + PLACE_LOOPS) * NS
            with dve.Fori(COUNT_LOOPS + PLACE_LOOPS, LOOPS) as i:
                sums0(i, None, 0)
            ch.base += LOOPS * NS
            ch.i = ch.per = ch.k = 0
            add0(LOOPS - 1, NS - 1)
            v.tensor_scalar(place_f, place_f, -1.0, None, ALU.add).then_inc(s_kB, 1)

            dve.wait_ge(a_acc, LOOPS * BODY)
            for stored in at_st:
                dve.wait_ge(stored, 16 * AT_LOOPS)
            dve.sem_inc(a_done, 1)
            v.memset(G_T[HID:HID + 1, :, :, :], 1.0).then_inc(g_ones, 1)

            def gru(i, s, sT, sV, sN, hid):
                b = two(bank[2 + s], 4 * HID)
                after2(dve, sT, s, i)
                ch.link(v.scalar_tensor_tensor(G_u[:, s, :, :], G_t[:, s, :, 0:HID], 1.0, b[:, :, GATES:4 * HID], ALU.add, ALU.mult))
                v.scalar_tensor_tensor(G_v[:, s, :, :], G_u[:, s, :, :], 0.5, b[:, :, 2 * HID:GATES], ALU.mult, ALU.add).then_inc(sV, 1)
                after2(dve, sN, s, i)
                ch.link(v.tensor_tensor(G_d[:, s, :, :], hid, G_n[:, s, :, :], ALU.subtract))
                ch.link(v.scalar_tensor_tensor(G_e[:, s, :, :], G_t[:, s, :, HID:2 * HID], 1.0, G_d[:, s, :, :], ALU.add, ALU.mult))
                ch.link(v.scalar_tensor_tensor(G_d[:, s, :, :], G_e[:, s, :, :], 0.5, G_n[:, s, :, :], ALU.mult, ALU.add))

            def update0(i):
                ch.body(i, 8)
                for s in range(2):
                    w = ds(i * 4 + s * 2, 2)
                    gru(i, s, g_t, g_v, g_n, h[:, w, :])
                    v.tensor_tensor(xs[:, w, :], xs[:, w, :], G_d[:, s, :, :], ALU.add).then_inc(g_x, 1)
                ch.end_body()
            loop(dve, G_LOOPS, update0)
            ch.end_loop(G_LOOPS)
            dve.wait_ge(g_x, 2 * G_LOOPS)
            normalise(2)
            dve.wait_ge(s_h, 2)

            v.memset(P_hT[HID:HID + 1, :, :, :], 1.0).then_inc(p_ones, 1)

            v.memset(B_row[:, :, :, ROW_ONE:ROW], 1.0).then_inc(b_pad, 1)
            v.memset(padrows, 0.0).then_inc(b_pad, 1)
            dve.wait_ge(b_pad, 2)
            v.memset(padrows[:, :, ROW_SRC], float(PAD_KEY)).then_inc(b_pad, 1)

            def tables1(i):
                for s in range(2):
                    after2(dve, p_mm, s, i)
                    if not first(i):
                        dve.wait_ge(p_st[s], 16 * i)
                    v.tensor_copy(P_out[:, s, :, :], two(bank[2 + s], H1)).then_inc(p_p, 1)
            loop(dve, G_LOOPS, tables1)
            dve.wait_ge(s_constb, N_CONSTB)

            def rows(i):
                ch.body(i, (3 + GV) * NS)
                for s in range(NS):
                    r = regs(ENG.DVE, wtile, i * BODY + s * GV, TILES - 1)
                    turn(dve, "dve")
                    for u in range(GV):
                        m = v.tensor_copy(B_rec[:, s, u, :], recs1[:, ds(r[u], 1), :].rearrange("p a k -> p (a k)"))
                        (ch.link if u == GV - 1 else ch.do)(m)
                    v.tensor_tensor(B_kl[:, s, :], B_rec[:, s, :, 0], wbase[:, ds(i * BODY + s * GV, GV)], ALU.subtract).then_inc(b_kl, 1)
                    after(dve, b_kl, s, i)
                    after(dve, b_DT, s, i, NS)
                    v.tensor_tensor(B_D[:, s, :, :], iota[:, :].unsqueeze(1).to_broadcast([P, GV, P]),
                                    per_group(B_kl[:, s, :], P), ALU.is_equal).then_inc(b_D, 1)
                    ch.link(v.tensor_scalar(B_ge[:, s, :], B_kl[:, s, :], 0.0, None, ALU.is_ge))
                    ch.link(v.scalar_tensor_tensor(B_in[:, s, :], B_kl[:, s, :], float(P), B_ge[:, s, :], ALU.is_lt, ALU.mult))
                    ch.link(v.scalar_tensor_tensor(B_sh[:, s, :], B_rec[:, s, :, 2], -BIG, B_in[:, s, :], ALU.add, ALU.mult))
                    if not first(i):
                        dve.wait_ge(b_sc[s], 16 * GV * i)
                    v.tensor_copy(B_row[:, s, :, ROW_SRC], B_rec[:, s, :, 1]).then_inc(b_pos, 1)
                    v.tensor_scalar(B_pos[:, s, :], B_sh[:, s, :], BIG, None, ALU.add).then_inc(b_pos, 1)
                ch.end_body()
            dve.wait_ge(b_pad, 3)
            dve.wait_ge(r_c, REC0 + REC1)
            loop(dve, LOOPS, rows)
            ch.end_loop(LOOPS)

            dve.wait_ge(b_sent, 1)
            visit_table(1)
            for s in range(2):
                dve.wait_ge(p_st[s], 16 * G_LOOPS)
            v.memset(acc[:, :, :], 0.0).then_inc(c_init, 1)
            v.tensor_copy(sel.rearrange("p (u n) -> p u n", u=GV),
                          sel_a[:, :].unsqueeze(2).to_broadcast([PARTS * GV, GV, P])).then_inc(c_init, 1)
            v.memset(wbase_all[:, 0:1], -float(P)).then_inc(c_init, 1)
            v.memset(C_mn[:, 0:1], 0.0).then_inc(c_init, 1)
            v.memset(C_zero, 0.0).then_inc(c_init, 1)
            v.memset(C_step, MASKED / P).then_inc(c_init, 1)
            dve.wait_ge(c_init, N_CINIT)

            def tick(i, s, stages):
                def add_sums(u):
                    k = acc[:, ds(r[u], 1), :].rearrange("p a k -> p (a k)")
                    return v.scalar_tensor_tensor(k, k, C_cr[:, t4, u:u + 1], bank[6 + t4 % 2][:, u * (HID + 1):(u + 1) * (HID + 1)],
                                                  ALU.mult, ALU.add)

                def score(u):
                    return ch.do(v.scalar_tensor_tensor(C_V[:, t1, u, 0:H1], C_V[:, t1, u, 0:H1], 0.0, w2bc[:, :], ALU.max, ALU.mult,
                                                        accum_out=C_raw[:, t1, u:u + 1]))

                def add_parts(half):
                    c = slice(2 * half, 2 * half + 2)
                    v.tensor_tensor(C_V[:, t1, c, 0:H1], two(bank[2 + half], H1), C_V[:, t1, c, 0:H1], ALU.add).then_inc(c_add, 1)

                if 3 in stages:
                    t3, j3 = stages[3]
                    after(dve, c_mg, t3, j3)
                    ch.link(v.tensor_reduce(C_mg[:, t3, :], bank[5][:, 0:GV * PARTS].rearrange("p (u k) -> p u k", k=PARTS), AX.X, ALU.add))
                    ch.link(v.tensor_tensor(C_z[:, t3, :], C_s[:, t3, :], C_mg[:, t3, :], ALU.subtract))
                    v.tensor_scalar(C_d[:, t3, :], C_z[:, t3, :], 0.0, None, ALU.min).then_inc(c_d, 1)
                if 0 in stages:
                    after(dve, c_kl, s, i)
                    after(dve, c_MKt, s, i, NS)
                    after(dve, c_S, s, i, NS)
                    v.tensor_tensor(C_N[:, s, :, :], iota_b[:, :].unsqueeze(1).to_broadcast([P, GV, P]),
                                    per_group(C_kl[:, s, :], P), ALU.not_equal).then_inc(c_N, 1)
                if 4 in stages:
                    t4, j4 = stages[4]
                    r = regs(ENG.DVE, wwin, j4 * BODY + t4 * GV, N_WIN - 1)
                    after(dve, c_ag, t4, j4)
                    after(dve, c_cr, t4, j4)
                    after(dve, c_acc, t4, j4, 1)
                    m_acc = ch.do(add_sums(0))
                if 2 in stages:
                    t2, j2 = stages[2]
                    after(dve, c_MKt, t2, j2)
                    m_tm = ch.do(v.tensor_reduce(C_tm[:, t2, :], four(bank[4], P), AX.X, ALU.max))
                if 4 in stages:
                    ch.need(m_acc)
                    m_acc = ch.do(add_sums(1))
                if 2 in stages:
                    k = t2 * GV
                    ch.need(m_tm)
                    after(dve, c_pen, t2, j2)
                    after(dve, c_new, t2, j2, 1)
                    after(dve, c_mn, t2, j2, NS)
                    v.tensor_tensor_scan(C_mn[:, 1 + k:1 + k + GV], C_pen[:, t2, :], C_tm[:, t2, :], C_mn[:, k:k + 1],
                                         ALU.add, ALU.max).then_inc(c_new, 1)
                if 1 in stages:
                    t1, j1 = stages[1]
                    sp_ = [C_parts[:, t1, k * GV:(k + 1) * GV] for k in range(PARTS)]
                    after(dve, c_pre, t1, j1)
                    add_parts(0)
                    add_parts(1)
                    dve.wait_ge(c_add, j1 * 2 * NS + 2 * t1 + 1)
                    score(0)
                    score(1)
                    after(dve, c_add, t1, j1, incs=2)
                    score(2)
                    m_raw = score(3)
                if 2 in stages and t2 == NS - 1:
                    after(dve, c_new, t2, j2)
                    after(dve, c_df, t2, j2, 1)
                    ch.do(v.tensor_copy(C_mn[:, 0:1], C_mn[:, NS * GV:1 + NS * GV]))
                if 4 in stages:
                    ch.need(m_acc)
                    m_acc = ch.do(add_sums(2))
                if 1 in stages:
                    ch.need(m_raw)
                    ch.do(v.tensor_scalar(sp_[0], C_raw[:, t1, :], b2bc[:, :], None, ALU.add))
                    m_s = ch.do(v.tensor_scalar(C_s[:, t1, :], C_raw[:, t1, :], b2bc[:, :], None, ALU.add))
                if 4 in stages:
                    ch.need(m_acc)
                    add_sums(3).then_inc(c_acc, 1)
                if 1 in stages:
                    ch.need(m_s)
                    ch.link(v.tensor_tensor(C_r[:, t1, :], C_s[:, t1, :], sp_[0], ALU.subtract))
                    ch.link(v.tensor_copy(sp_[1], C_r[:, t1, :]))
                    v.tensor_tensor(sp_[2], C_r[:, t1, :], sp_[1], ALU.subtract).then_inc(c_sp, 1)
            run_ticks(dve, tick, 5, ch, NS * (2 + 3 + 1 + 8) + 1)

            dve.wait_ge(c_acc, NS * LOOPS)
            v.memset(G_T[HID:HID + 1, :, 2:4, :], 1.0).then_inc(n_ones, 1)
            ch.link(v.memset(G_mT[HID:HID + 1, :, :, :], 1.0))
            ch.link(v.tensor_scalar(has, acc[:, :, HID], 0.0, None, ALU.is_gt))
            ch.link(v.tensor_scalar(tmp_w, has, -1.0, 1.0, ALU.mult, ALU.add))
            ch.link(v.tensor_tensor(tmp_w, tmp_w, acc[:, :, HID], ALU.add))
            ch.link(v.reciprocal(rden, tmp_w))

            def update1(i):
                ch.body(i, 8 + 6)
                for s in range(2):
                    w = ds(i * 4 + s * 2, 2)
                    after2(dve, n_T, s, i, 2)
                    v.tensor_tensor(G_c[:, s, :, :], acc[:, w, :], rden[:, w].unsqueeze(2).to_broadcast([P, 2, HID + 1]),
                                    ALU.mult).then_inc(n_c, 1)
                for s in range(2):
                    w = ds(i * 4 + s * 2, 2)
                    after2(dve, n_msc, s, i, incs=2)
                    gru(i, s, n_t, n_v, n_n, G_m[:, s, :, :])
                    ch.link(v.tensor_tensor(G_e[:, s, :, :], G_d[:, s, :, :], h[:, w, :], ALU.subtract))
                    ch.link(v.tensor_tensor(G_d[:, s, :, :], G_e[:, s, :, :], has[:, w].unsqueeze(2).to_broadcast([P, 2, HID]), ALU.mult))
                    ch.link(v.tensor_tensor(G_e[:, s, :, :], G_d[:, s, :, :], h[:, w, :], ALU.add))
                    v.tensor_tensor(xs[:, w, :], xs[:, w, :], G_e[:, s, :, :], ALU.add).then_inc(n_x, 1)
                ch.end_body()
            loop(dve, G_LOOPS, update1)


_INS = ['x', 'src', 'dst', 'edge_attr_16', 'edge_type_8', 'L0_gnn_edge_matrix', 'L0_gnn_w_ih', 'L0_gnn_w_hh',
        'L0_gnn_b_ih', 'L0_gnn_b_hh', 'L1_gnn_W_att1', 'L1_gnn_b_att1', 'L1_gnn_W_att2', 'L1_gnn_b_att2',
        'L1_gnn_W_lin', 'L1_gnn_b_lin', 'L1_gnn_W_ih', 'L1_gnn_b_ih', 'L1_gnn_W_hh', 'L1_gnn_b_hh']
_OUTS = [((12500, 64), 'float32')]


def kernel(**inputs):
    import numpy as _np
    import concourse.bacc as _bacc
    from concourse import mybir as _mybir
    from concourse.bass_utils import run_bass_kernel_spmd as _run

    nc = _bacc.Bacc("TRN2", target_bir_lowering=False, num_devices=1)
    arrays, args = {}, []
    for name in _INS:
        a = _np.ascontiguousarray(inputs[name])
        arrays[f"in_{name}_dram"] = a
        args.append(nc.dram_tensor(f"in_{name}_dram", a.shape, _mybir.dt.from_np(a.dtype), kind="ExternalInput").ap())
    for i, (shape, dtype) in enumerate(_OUTS):
        dt = _mybir.dt.from_np(_np.dtype(dtype))
        args.append(nc.dram_tensor(f"out_{i}_dram", shape, dt, kind="ExternalOutput").ap())
    build(nc, *args)
    r = _run(nc, [arrays], core_ids=[0])
    return r.results[0]["out_0_dram"]
```
